# Optimizing a Trainium2 kernel written in Bass

```python
import numpy as np
import jax
import jax.numpy as jnp

def _softmax(x, axis=-1):
    return jax.nn.softmax(x, axis=axis)

def _gelu(x):
    return jax.nn.gelu(x, approximate=True)

def _silu(x):
    return jax.nn.silu(x)

def _sigmoid(x):
    return jax.nn.sigmoid(x)

def _layernorm(x, axis=-1, eps=1e-05):
    m = jnp.mean(x, axis=axis, keepdims=True)
    v = jnp.var(x, axis=axis, keepdims=True)
    return (x - m) / jnp.sqrt(v + eps)

def _scatter_add(tgt, idx, src, axis=0):
    return tgt.at[idx].add(src)

def _segment_sum(src, seg, n):
    return jax.ops.segment_sum(src, seg, n)
kernel_name = 'mk_lm_tower_d1_tok_ids1024_r4_81d992'

def setup_inputs(seed: int=0):
    np.random.seed(seed)
    _w = jnp.asarray

    def _rec_inputs():
        import jax
        import jax.numpy as jnp
        _rk = jax.random.key(seed)
        x = jax.random.randint(jax.random.fold_in(_rk, 1), (64, 128), 0, 12564, jnp.int32)
        return x
    x = _rec_inputs()

    def _L0_tok_setup():
        import jax, jax.numpy as jnp
        import numpy as np
        BVS = 262144
        BD = 64
        MD = 256
        B, T = (4, 2048)
        SRC_VOCAB = 50257
        key = jax.random.key(seed)
        k_ids, k_emb, k_proj = jax.random.split(key, 3)
        ids = jax.random.randint(k_ids, (B, T), 0, SRC_VOCAB, dtype=jnp.int64 if jax.config.jax_enable_x64 else jnp.int32).astype(jnp.int32)
        emb_weight = jax.random.normal(k_emb, (BVS, BD), dtype=jnp.float32) * 0.02
        proj_weight = jax.random.normal(k_proj, (MD, BD), dtype=jnp.float32) * 0.02
        scale = jnp.float32(0.05)
        return {'ids': ids, 'emb_weight': emb_weight, 'proj_weight': proj_weight, 'scale': scale}
    _L0_tok_all = _L0_tok_setup()
    _L0_tok_in = {k: v for k, v in _L0_tok_all.items() if k in ('emb_weight', 'proj_weight', 'scale')}
    del _L0_tok_all

    def _L0_attn_setup():
        import jax, jax.numpy as jnp
        import numpy as np
        DIM = 256
        HEADS = 8
        DIM_QK = 64
        MAX_POS = 10
        SCALE = DIM_QK ** (-0.5)
        key = jax.random.key(seed)
        ks = jax.random.split(key, 6)
        b, n = (4, 512)
        x = jax.random.normal(ks[0], (b, n, DIM), dtype=jnp.float32)
        mask = jnp.ones((b, n), dtype=bool)
        s = DIM ** (-0.5)
        W_qk = jax.random.normal(ks[1], (DIM, DIM_QK * HEADS * 2), dtype=jnp.float32) * s
        W_v = jax.random.normal(ks[2], (DIM, DIM), dtype=jnp.float32) * s
        W_out = jax.random.normal(ks[3], (DIM, DIM), dtype=jnp.float32) * s
        b_out = jnp.zeros((DIM,), dtype=jnp.float32)
        conv = jax.random.normal(ks[4], (HEADS, 2 * MAX_POS + 1), dtype=jnp.float32) * 0.02
        return {'x': x, 'mask': mask, 'W_qk': W_qk, 'W_v': W_v, 'W_out': W_out, 'b_out': b_out, 'conv': conv}
    _L0_attn_all = _L0_attn_setup()
    _L0_attn_in = {k: v for k, v in _L0_attn_all.items() if k in ('mask', 'W_qk', 'W_v', 'W_out', 'b_out', 'conv')}
    del _L0_attn_all

    def _L0_ffn_setup():
        import jax, jax.numpy as jnp
        import numpy as np
        BLOCK = 32
        W_BITS = 4
        ACT_BITS = 16

        def act_qdq(x):
            qmax = 2.0 ** (ACT_BITS - 1) - 1.0
            scale = jnp.maximum(jnp.max(jnp.abs(x)) / qmax, 1e-12)
            return jnp.clip(jnp.round(x / scale), -qmax - 1.0, qmax) * scale

        def fixed_qdq_u16(x):
            scale = 1.0 / 65536.0
            return jnp.clip(jnp.round(x / scale), 0.0, 65535.0) * scale

        def lpbq_dequant(w):
            O, I = w.shape
            qmax = 2.0 ** (W_BITS - 1) - 1.0
            wb = w.reshape(O, I // BLOCK, BLOCK)
            s = jnp.maximum(jnp.max(jnp.abs(wb), axis=-1, keepdims=True) / qmax, 1e-12)
            wq = jnp.clip(jnp.round(wb / s), -qmax - 1.0, qmax) * s
            return wq.reshape(O, I)
        key = jax.random.key(seed)
        k1, k2, k3, k4 = jax.random.split(key, 4)
        B, S, H, I = (2, 1024, 256, 768)
        x = jax.random.normal(k1, (B, S, H), jnp.float32)
        w_gate = jax.random.normal(k2, (I, H), jnp.float32) * 0.02
        w_up = jax.random.normal(k3, (I, H), jnp.float32) * 0.02
        w_down = jax.random.normal(k4, (H, I), jnp.float32) * 0.02
        return {'x': x, 'w_gate': w_gate, 'w_up': w_up, 'w_down': w_down}
    _L0_ffn_all = _L0_ffn_setup()
    _L0_ffn_in = {k: v for k, v in _L0_ffn_all.items() if k in ('w_gate', 'w_up', 'w_down')}
    del _L0_ffn_all
    return {'x': x, 'L0_tok_emb_weight': _L0_tok_in['emb_weight'], 'L0_tok_proj_weight': _L0_tok_in['proj_weight'], 'L0_tok_scale': _L0_tok_in['scale'], 'L0_attn_mask': _L0_attn_in['mask'], 'L0_attn_W_qk': _L0_attn_in['W_qk'], 'L0_attn_W_v': _L0_attn_in['W_v'], 'L0_attn_W_out': _L0_attn_in['W_out'], 'L0_attn_b_out': _L0_attn_in['b_out'], 'L0_attn_conv': _L0_attn_in['conv'], 'L0_ffn_w_gate': _L0_ffn_in['w_gate'], 'L0_ffn_w_up': _L0_ffn_in['w_up'], 'L0_ffn_w_down': _L0_ffn_in['w_down']}

def reference(x, L0_tok_emb_weight, L0_tok_proj_weight, L0_tok_scale, L0_attn_mask, L0_attn_W_qk, L0_attn_W_v, L0_attn_W_out, L0_attn_b_out, L0_attn_conv, L0_ffn_w_gate, L0_ffn_w_up, L0_ffn_w_down):
    import jax
    import jax.numpy as jnp

    def _L0_tok_ref(ids, emb_weight, proj_weight, scale):
        import jax, jax.numpy as jnp
        import numpy as np
        BVS = 262144
        BD = 64
        MD = 256
        B, T = (4, 2048)
        SRC_VOCAB = 50257
        bvs = emb_weight.shape[0]
        t = ids.astype(jnp.int32)
        mod = jnp.int32(bvs - 1)
        mixed = jnp.int32(36313) * t[..., 1:] ^ jnp.int32(27191) * t[..., :-1]
        o_rest = jnp.mod(mixed, mod)
        o_first = jnp.full(t.shape[:-1] + (1,), mod, dtype=jnp.int32)
        o = jnp.concatenate([o_first, o_rest], axis=-1)
        h = emb_weight[o]
        h = jnp.einsum('btd,md->btm', h, proj_weight)
        return h * scale.astype(h.dtype)

    def _L0_attn_ref(x, mask, W_qk, W_v, W_out, b_out, conv):
        import jax, jax.numpy as jnp
        import numpy as np
        DIM = 256
        HEADS = 8
        DIM_QK = 64
        MAX_POS = 10
        SCALE = DIM_QK ** (-0.5)
        b, n, _ = x.shape
        h, dqk = (HEADS, DIM_QK)
        dv = DIM // h
        qk = x @ W_qk
        q, k = jnp.split(qk, 2, axis=-1)
        v = x @ W_v
        q = q.reshape(b, n, h, dqk).transpose(0, 2, 1, 3)
        k = k.reshape(b, n, h, dqk).transpose(0, 2, 1, 3)
        v = v.reshape(b, n, h, dv).transpose(0, 2, 1, 3)
        dots = jnp.einsum('bhid,bhjd->bhij', q, k) * SCALE
        seq = jnp.arange(n)
        dist = jnp.clip(seq[None, :] - seq[:, None], -MAX_POS, MAX_POS) + MAX_POS
        bias = conv[:, dist]
        attn = jax.nn.softmax(dots + bias[None], axis=-1)
        out = jnp.einsum('bhij,bhjd->bhid', attn, v)
        out = out.transpose(0, 2, 1, 3).reshape(b, n, h * dv)
        return out @ W_out + b_out

    def _L0_ffn_ref(x, w_gate, w_up, w_down):
        import jax, jax.numpy as jnp
        import numpy as np
        BLOCK = 32
        W_BITS = 4
        ACT_BITS = 16

        def act_qdq(x):
            qmax = 2.0 ** (ACT_BITS - 1) - 1.0
            scale = jnp.maximum(jnp.max(jnp.abs(x)) / qmax, 1e-12)
            return jnp.clip(jnp.round(x / scale), -qmax - 1.0, qmax) * scale

        def fixed_qdq_u16(x):
            scale = 1.0 / 65536.0
            return jnp.clip(jnp.round(x / scale), 0.0, 65535.0) * scale

        def lpbq_dequant(w):
            O, I = w.shape
            qmax = 2.0 ** (W_BITS - 1) - 1.0
            wb = w.reshape(O, I // BLOCK, BLOCK)
            s = jnp.maximum(jnp.max(jnp.abs(wb), axis=-1, keepdims=True) / qmax, 1e-12)
            wq = jnp.clip(jnp.round(wb / s), -qmax - 1.0, qmax) * s
            return wq.reshape(O, I)
        x = act_qdq(x)
        up = act_qdq(x @ lpbq_dequant(w_up).T)
        gate = act_qdq(x @ lpbq_dequant(w_gate).T)
        sig = fixed_qdq_u16(jax.nn.sigmoid(gate))
        gate = act_qdq(gate * sig)
        o = act_qdq(gate * up)
        return o @ lpbq_dequant(w_down).T
    h = _L0_tok_ref(x, L0_tok_emb_weight, L0_tok_proj_weight, L0_tok_scale)
    h = h + _L0_attn_ref(_layernorm(h, axis=-1), L0_attn_mask, L0_attn_W_qk, L0_attn_W_v, L0_attn_W_out, L0_attn_b_out, L0_attn_conv)
    h = h + _L0_ffn_ref(_layernorm(h, axis=-1), L0_ffn_w_gate, L0_ffn_w_up, L0_ffn_w_down)
    return h

_drawn_inputs = setup_inputs


def setup_inputs(seed=0):
    import zlib

    import numpy as np

    out = dict(_drawn_inputs(seed))
    spreads = {'L0_attn_b_out': (0.0, 0.1)}
    factors = {'L0_attn_W_qk': 30.26, 'L0_attn_conv': 64.0}
    for name, (base, spread) in spreads.items():
        noise = np.random.default_rng([zlib.crc32(name.encode()), seed]).standard_normal(out[name].shape)
        drawn = base * np.exp(spread * noise) if base else spread * noise
        out[name] = jnp.asarray(drawn.astype(out[name].dtype))
    for name, factor in factors.items():
        out[name] = (out[name] * factor).astype(out[name].dtype)
    return out
```

```python
from contextlib import ExitStack

import concourse.bass as bass
from concourse import mybir

ALU = mybir.AluOpType
ACT = mybir.ActivationFunctionType
F32 = mybir.dt.float32
F16 = mybir.dt.float16
I32 = mybir.dt.int32
U32 = mybir.dt.uint32
I16 = mybir.dt.int16
U16 = mybir.dt.uint16
AX_X = mybir.AxisListType.X
RMAX = bass.bass_isa.ReduceOp.max

P = 128
NSEQ = 64
GS = 4
NG = NSEQ // GS
GT = GS * P
VOC = 262144
ED = 64
DM = 256
DT = DM // P
H = 8
HP = H // 2
DV = DM // H
MAXPOS = 10
FF = 768
FT = FF // P
CT = 3
NCH = FT // CT
CW = CT * GT
WBLK = 32
EPS = 1e-5
QMAX = 32767.0
TINY = 1e-12
HASH_A, HASH_B = 36313, 27191
HASH_BITS = 18

SC_E = 2.0 ** 10
SC_P = 2.0 ** 10
SC_X = 2.0 ** 6
SC_G = 2.0 ** 6
SC_V = 2.0 ** 10
SC_O = 2.0 ** 8
SC_WO = 2.0 ** 8
SC_W = 2.0 ** 10
QK_SCALE = 64.0 ** -0.5


def build(nc, x, emb, proj, scale, w_qk, w_v, w_out, b_out, conv, w_gate, w_up, w_down, out):
    with ExitStack() as keep:
        def sb(name, shape, dt):
            return keep.enter_context(nc.sbuf_tensor(name, shape, dt))

        t = {}
        t["ident32"] = sb("ident32", [P, P], F32)
        t["wup"] = sb("wup_hl", [P, 2, DT, FF], F16)
        t["wgate"] = sb("wgate_hl", [P, 2, DT, FF], F16)
        t["wdown"] = sb("wdown_hl", [P, 2, FT, DM], F16)
        t["big"] = sb("big", [P, NG * NCH * CW], I16)
        t["mean_var"] = sb("mean_var", [P, NSEQ, 2], F32)
        t["dev_max"] = sb("dev_max", [P, NSEQ], F32)
        h2 = t["big"][:, 0:NSEQ * DM * 2].bitcast(F32).rearrange("p (n f) -> p n f", f=DM)
        with ExitStack() as attn:
            def sba(name, shape, dt):
                return attn.enter_context(nc.sbuf_tensor(name, shape, dt))
            a = {}
            a["ident16"] = sba("ident16", [P, P], F16)
            a["emb_rows"] = sba("emb_rows", [P, NSEQ, ED], F32)
            a["pt"] = sba("pt_hl", [P, 2, DM], F16)
            a["g"] = sba("g_hl", [P, 2, HP, P], F16)
            a["mv"] = sba("mv_hl", [P, 2, DM], F16)
            a["wo"] = sba("wo_hl", [P, 2, DT, DM], F16)
            a["bias"] = sba("pos_bias", [P, 2, HP, P], F32)
            a["bout"] = sba("bout_row", [P, DM], F32)
            a["h_scale"] = sba("h_scale", [P, 1], F32)
            a["x_scale"] = sba("x_scale", [P, 1], F32)
            a["minus_half"] = sba("minus_half", [P, GS], F32)
            a["eps"] = sba("eps", [P, GS], F32)
            prepare(nc, t, a, x, emb, proj, scale, w_qk, w_v, w_out, b_out, conv, w_gate, w_up, w_down)
            attention(nc, t, a, h2)
        feed_forward(nc, t, h2, out)


def prepare(nc, t, a, x, emb, proj, scale, w_qk, w_v, w_out, b_out, conv, w_gate, w_up, w_down):
    with ExitStack() as ctx:
        def sb(name, shape, dt):
            return ctx.enter_context(nc.sbuf_tensor(name, shape, dt))

        def sem(name):
            return ctx.enter_context(nc.semaphore(name))

        ids = sb("ids", [NSEQ, P], I32)
        mul_a = sb("mul_a", [NSEQ, P], I32)
        mul_b = sb("mul_b", [NSEQ, P], I32)
        prod_a = sb("prod_a", [NSEQ, P], I32)
        prod_b = sb("prod_b", [NSEQ, P], I32)
        mixed = sb("mixed", [NSEQ, P], I32)
        low_bits = sb("low_bits", [NSEQ, P], I32)
        high_bits = sb("high_bits", [NSEQ, P], I32)
        bucket = sb("bucket", [NSEQ, P], F32)
        wrap = sb("wrap", [NSEQ, P], F32)
        rows = sb("rows", [P, NSEQ], U32)
        p_nat = sb("p_nat", [P, DT, ED], F32)
        p_dup = sb("p_dup", [P, DT, 2, ED], F32)
        pc_dup = sb("pc_dup", [P, DT, 2, ED], F32)
        ones = sb("mean_ones", [P, P], F32)
        wqk_s = sb("wqk_s", [P, DT, 2 * H * ED], F32)
        wv_s = sb("wv_s", [P, DT, DM], F32)
        wo_s = sb("wo_s", [P, DT, DM], F32)
        mq = sb("mq", [P, HP, 2, ED], F32)
        mk = sb("mk", [P, HP, ED], F32)
        conv_s = sb("conv_s", [P, H, 2 * MAXPOS + 1], F32)
        window = sb("window", [P, H, 2 * P], F32)
        scale_s = sb("scale_s", [P, 1], F32)
        raw = [sb(f"ffw{i}", [P, FF * DM // P], F32) for i in range(3)]
        steps = sb("steps", [P, 3, FF * DM // P // WBLK], F32)
        inv_steps = sb("inv_steps", [P, 3, FF * DM // P // WBLK], F32)
        levels = sb("levels", [P, FF * DM // P], I16)
        window_d = nc.dram_tensor("window_scratch", [P, 2 * P * H], F32, kind="Internal").ap()

        ps_a = ctx.enter_context(nc.psum_tensor("ps_a", [P, 512], F32))
        ps_b = ctx.enter_context(nc.psum_tensor("ps_b", [P, 512], F32))
        ps_m = ctx.enter_context(nc.psum_tensor("ps_m", [P, ED], F32))
        ps_ge = ctx.enter_context(nc.psum_tensor("ps_ge", [P, 512], F32))
        ps_go = ctx.enter_context(nc.psum_tensor("ps_go", [P, 512], F32))
        ps_w = ctx.enter_context(nc.psum_tensor("ps_w", [P, 2, 512], F32))

        ids_in = sem("ids_in")
        p_in = sem("p_in")
        attn_in = sem("attn_in")
        small_in = sem("small_in")
        ffw_in = [sem(f"ffw_in{i}") for i in range(3)]
        consts = sem("consts")
        prods = sem("prods")
        hashing = sem("hashing")
        hash_turned = sem("hash_turned")
        rows_ready = sem("rows_ready")
        gathered = sem("gathered")
        windowed = sem("windowed")
        window_out = sem("window_out")
        bias_in = sem("bias_in")
        fold = sem("fold")
        pe_fold = sem("pe_fold")
        act_fold = sem("act_fold")
        quant = sem("quant")
        turned = sem("turned")
        high = sem("high")
        low = sem("low")

        block = ctx.enter_context(nc.Block())
        NB = FF * DM // P // WBLK

        @block.sync
        def _(sp):
            sp.dma_start(ids[:, :], x).then_inc(ids_in, 16)
            sp.dma_start(p_nat[:, :, :], proj.rearrange("(t p) d -> p t d", p=P)).then_inc(p_in, 16)
            sp.dma_start(wqk_s[:, :, :], w_qk.rearrange("(t p) n -> p t n", p=P)).then_inc(attn_in, 16)
            sp.dma_start(wv_s[:, :, :], w_v.rearrange("(t p) n -> p t n", p=P)).then_inc(attn_in, 16)
            sp.dma_start(wo_s[:, :, :], w_out.rearrange("(t p) n -> p t n", p=P)).then_inc(attn_in, 16)
            for i, (w, tiles) in enumerate(((w_up, FT), (w_gate, FT), (w_down, DT))):
                sp.dma_start(raw[i][:, :].rearrange("p (t n) -> p t n", t=tiles),
                             w.rearrange("(t p) n -> p t n", p=P)).then_inc(ffw_in[i], 16)
            sp.wait_ge(windowed, 3)
            sp.dma_start(window_d, window[:, :, :].rearrange("p h m -> p (h m)")).then_inc(window_out, 16)
            sp.wait_ge(window_out, 16)
            pitch = 2 * P * H - 1
            skewed = window_d.rearrange("p m -> (p m)")[P - 1:P - 1 + P * pitch].rearrange("(i m) -> i m", m=pitch)
            for parity in range(2):
                for pair in range(HP):
                    h = 2 * pair + parity
                    sp.dma_start(a["bias"][:, parity, pair, :],
                                 skewed[:, h * 2 * P:h * 2 * P + P]).then_inc(bias_in, 16)
            sp.wait_ge(bias_in, 16 * H)

        @block.gpsimd
        def _(pool):
            pool.memset(a["minus_half"][:, :], -0.5).then_inc(consts, 1)
            pool.memset(a["eps"][:, :], EPS).then_inc(consts, 1)
            pool.iota(mul_a[:, :], pattern=[[0, P]], base=HASH_A, channel_multiplier=0).then_inc(consts, 1)
            pool.iota(mul_b[:, :], pattern=[[0, P]], base=HASH_B, channel_multiplier=0).then_inc(consts, 1)
            pool.memset(t["ident32"][:, :], 0.0).then_inc(consts, 1)
            pool.memset(a["ident16"][:, :], 0.0).then_inc(consts, 1)
            pool.memset(ones[:, :], 1.0 / DM).then_inc(consts, 1)
            pool.wait_ge(ids_in, 16)
            pool.wait_ge(consts, 7)
            pool.tensor_tensor(prod_a[:, :], ids[:, :], mul_a[:, :], ALU.mult).then_inc(prods, 1)
            pool.tensor_tensor(prod_b[:, :], ids[:, :], mul_b[:, :], ALU.mult).then_inc(prods, 1)
            for m in (t["ident32"], a["ident16"]):
                pool.affine_select(out=m[:, :], in_=m[:, :], compare_op=ALU.not_equal, fill=1.0,
                                   base=0, pattern=[[-1, P]], channel_multiplier=1).then_inc(consts, 1)
            pool.wait_ge(rows_ready, 1)
            for n in range(NSEQ):
                pool.indirect_dma_start(a["emb_rows"][:, n, :], None, emb,
                                        bass.IndirectOffsetOnAxis(ap=rows[:, n:n + 1], axis=0)).then_inc(gathered, 16)
            pool.wait_ge(gathered, 16 * NSEQ)

        @block.scalar
        def _(act):
            act.dma_start(scale_s[:, :], scale.to_broadcast([P, 1])).then_inc(small_in, 16)
            act.dma_start(conv_s[:, :, :].rearrange("p h m -> p (h m)"),
                          conv.rearrange("h m -> (h m)").partition_broadcast(P)).then_inc(small_in, 16)
            act.dma_start(a["bout"][:, :], b_out.partition_broadcast(P)).then_inc(small_in, 16)
            act.wait_ge(small_in, 48)
            act.mul(a["h_scale"][:, :], scale_s[:, :], 1.0 / (SC_E * SC_P)).then_inc(act_fold, 1)
            act.mul(a["x_scale"][:, :], scale_s[:, :], SC_X).then_inc(act_fold, 1)
            edge = P - 1 - MAXPOS
            w = 2 * MAXPOS + 1
            act.copy(window[:, :, 0:edge], conv_s[:, :, 0:1].to_broadcast([P, H, edge])).then_inc(windowed, 1)
            act.copy(window[:, :, edge:edge + w], conv_s[:, :, :]).then_inc(windowed, 1)
            act.copy(window[:, :, edge + w:2 * P],
                     conv_s[:, :, w - 1:w].to_broadcast([P, H, 2 * P - edge - w])).then_inc(windowed, 1)
            act.wait_ge(pe_fold, 2)
            mqk = ps_b[:, :].rearrange("p (c d) -> p c d", d=ED)
            act.copy(mq[:, :, :, :], mqk[:, 0:HP, :].unsqueeze(2).to_broadcast([P, HP, 2, ED])).then_inc(act_fold, 1)
            act.copy(mk[:, :, :], mqk[:, HP:2 * HP, :]).then_inc(act_fold, 1)
            for n in range(9):
                act.wait_ge(turned, n + 1)
                i, j = n // 3, n % 3
                act.activation(transposed(t, i, j, 0), ps_w[:, n % 2, :], ACT.Copy, scale=SC_W).then_inc(high, 1)

        @block.vector
        def _(dve):
            dve.wait_ge(prods, 2)
            dve.tensor_tensor(mixed[:, 1:P], prod_a[:, 1:P], prod_b[:, 0:P - 1], ALU.bitwise_xor).then_inc(hashing, 1)
            dve.memset(mixed[:, 0:1], 0).then_inc(hashing, 1)
            dve.wait_ge(hashing, 2)
            dve.tensor_scalar(low_bits[:, :], mixed[:, :], VOC - 1, None, ALU.bitwise_and).then_inc(hashing, 1)
            dve.tensor_scalar(high_bits[:, :], mixed[:, :], HASH_BITS, None, ALU.arith_shift_right).then_inc(hashing, 1)
            dve.wait_ge(hashing, 4)
            dve.tensor_tensor(bucket[:, :], low_bits[:, :], high_bits[:, :], ALU.add).then_inc(hashing, 1)
            dve.wait_ge(hashing, 5)
            dve.tensor_scalar(wrap[:, :], bucket[:, :], float(VOC - 1), float(VOC - 1), ALU.is_ge, ALU.mult).then_inc(hashing, 1)
            dve.wait_ge(hashing, 6)
            dve.tensor_tensor(bucket[:, :], bucket[:, :], wrap[:, :], ALU.subtract).then_inc(hashing, 1)
            dve.wait_ge(hashing, 7)
            dve.tensor_scalar(wrap[:, :], bucket[:, :], 0.0, float(VOC - 1), ALU.is_lt, ALU.mult).then_inc(hashing, 1)
            dve.wait_ge(hashing, 8)
            dve.tensor_tensor(bucket[:, :], bucket[:, :], wrap[:, :], ALU.add).then_inc(hashing, 1)
            dve.wait_ge(hashing, 9)
            dve.memset(bucket[:, 0:1], float(VOC - 1)).then_inc(hashing, 1)
            dve.wait_ge(hash_turned, 1)
            dve.tensor_copy(rows[:, :], ps_a[:, 0:NSEQ]).then_inc(rows_ready, 1)

            dve.wait_ge(p_in, 16)
            dve.tensor_copy(p_dup[:, :, :, :], p_nat[:, :, :].unsqueeze(2).to_broadcast([P, DT, 2, ED])).then_inc(fold, 1)
            dve.wait_ge(pe_fold, 1)
            dve.tensor_tensor(pc_dup[:, :, :, :], p_nat[:, :, :].unsqueeze(2).to_broadcast([P, DT, 2, ED]),
                              ps_m[:, :].unsqueeze(1).unsqueeze(1).to_broadcast([P, DT, 2, ED]),
                              ALU.subtract).then_inc(fold, 1)
            dve.wait_ge(attn_in, 48)
            dve.tensor_scalar(a["wo"][:, 0, :, :], wo_s[:, :, :], SC_WO, None, ALU.mult).then_inc(fold, 1)
            dve.wait_ge(fold, 3)
            dve.scalar_tensor_tensor(a["wo"][:, 1, :, :], wo_s[:, :, :], SC_WO, a["wo"][:, 0, :, :],
                                     ALU.mult, ALU.subtract).then_inc(fold, 1)
            dve.wait_ge(pe_fold, 3)
            for hl, parity in ((0, 0), (0, 1)):
                ps = (ps_ge, ps_go)[parity][:, 0:HP * ED].rearrange("p (c d) -> p c d", d=ED)
                dve.tensor_scalar(a["g"][:, 0, :, parity * ED:(parity + 1) * ED], ps,
                                  SC_G * QK_SCALE, None, ALU.mult).then_inc(fold, 1)
            dve.wait_ge(fold, 6)
            for parity in range(2):
                ps = (ps_ge, ps_go)[parity][:, 0:HP * ED].rearrange("p (c d) -> p c d", d=ED)
                cols = slice(parity * ED, (parity + 1) * ED)
                dve.scalar_tensor_tensor(a["g"][:, 1, :, cols], ps, SC_G * QK_SCALE, a["g"][:, 0, :, cols],
                                         ALU.mult, ALU.subtract).then_inc(fold, 1)
            dve.wait_ge(pe_fold, 4)
            for k, (w, ps, sc) in enumerate(((a["mv"], ps_w[:, 0, 0:DM], SC_V), (a["pt"], ps_w[:, 1, 0:DM], SC_P))):
                dve.tensor_scalar(w[:, 0, :], ps, sc, None, ALU.mult).then_inc(fold, 1)
                dve.wait_ge(fold, 9 + 2 * k)
                dve.scalar_tensor_tensor(w[:, 1, :], ps, sc, w[:, 0, :], ALU.mult, ALU.subtract).then_inc(fold, 1)

            for i in range(3):
                blocks = raw[i][:, :].rearrange("p (b k) -> p b k", k=WBLK)
                lv = levels[:, :].rearrange("p (b k) -> p b k", k=WBLK)
                dve.wait_ge(ffw_in[i], 16)
                dve.tensor_reduce(steps[:, i, :], blocks, AX_X, ALU.max, apply_absolute_value=True).then_inc(quant, 1)
                dve.wait_ge(quant, 5 * i + 1)
                dve.tensor_scalar(steps[:, i, :], steps[:, i, :], 1.0 / 7.0, TINY, ALU.mult, ALU.max).then_inc(quant, 1)
                dve.wait_ge(quant, 5 * i + 2)
                dve.reciprocal(inv_steps[:, i, :], steps[:, i, :]).then_inc(quant, 1)
                dve.wait_ge(quant, 5 * i + 3)
                dve.tensor_tensor(lv, blocks, inv_steps[:, i, :].unsqueeze(2).to_broadcast([P, NB, WBLK]),
                                  ALU.mult).then_inc(quant, 1)
                dve.wait_ge(quant, 5 * i + 4)
                dve.tensor_tensor(blocks, lv, steps[:, i, :].unsqueeze(2).to_broadcast([P, NB, WBLK]),
                                  ALU.mult).then_inc(quant, 1)
            for n in range(9):
                dve.wait_ge(high, n + 1)
                i, j = n // 3, n % 3
                dve.scalar_tensor_tensor(transposed(t, i, j, 1), ps_w[:, n % 2, :], SC_W, transposed(t, i, j, 0),
                                         ALU.mult, ALU.subtract).then_inc(low, 1)

        @block.tensor
        def _(pe):
            pe.wait_ge(consts, 9)
            pe.wait_ge(hashing, 10)
            pe.transpose(ps_a[:, 0:NSEQ], bucket[:, :], t["ident32"][0:NSEQ, 0:NSEQ]).then_inc(hash_turned, 1)
            pe.wait_ge(p_in, 16)
            for k in range(DT):
                last = pe.matmul(ps_m[:, :], ones[:, :], p_nat[:, k, :], start=k == 0, stop=k == DT - 1)
            last.then_inc(pe_fold, 1)
            pe.wait_ge(attn_in, 48)
            pe.wait_ge(fold, 2)
            for c in range(2 * HP):
                for k in range(DT):
                    last = pe.matmul(ps_b[:, c * ED:(c + 1) * ED], wqk_s[:, k, c * P:(c + 1) * P],
                                     pc_dup[:, k, 0, :], start=k == 0, stop=k == DT - 1)
            last.then_inc(pe_fold, 1)
            pe.wait_ge(act_fold, 4)
            for pair in range(HP):
                for parity in range(2):
                    r = slice(parity * ED, (parity + 1) * ED)
                    last = pe.matmul((ps_ge, ps_go)[parity][:, pair * ED:(pair + 1) * ED],
                                     mq[r, pair, :, :].rearrange("c u d -> c (u d)"), mk[r, pair, :],
                                     start=True, stop=True)
            last.then_inc(pe_fold, 1)
            for k in range(DT):
                pe.matmul(ps_w[:, 0, 0:DM], pc_dup[:, k, :, :].rearrange("p u d -> p (u d)"), wv_s[:, k, :],
                          start=k == 0, stop=k == DT - 1)
            for k in range(DT):
                last = pe.transpose(ps_w[:, 1, k * P:(k + 1) * P], p_dup[:, k, :, :].rearrange("p u d -> p (u d)"),
                                    t["ident32"][:, :])
            last.then_inc(pe_fold, 1)
            for n in range(9):
                i, j = n // 3, n % 3
                pe.wait_ge(quant, 5 * i + 5)
                if n < 2:
                    pe.wait_ge(fold, 12)
                if n >= 2:
                    pe.wait_ge(low, n - 1)
                for q in range(4):
                    if i < 2:
                        kt, ot = (4 * j + q) // FT, (4 * j + q) % FT
                        src = raw[i][:, ot * DM + kt * P:ot * DM + (kt + 1) * P]
                    else:
                        kt, ot = (4 * j + q) // DT, (4 * j + q) % DT
                        src = raw[i][:, ot * FF + kt * P:ot * FF + (kt + 1) * P]
                    last = pe.transpose(ps_w[:, n % 2, q * P:(q + 1) * P], src, t["ident32"][:, :])
                last.then_inc(turned, 1)


def transposed(t, i, j, hl):
    w = (t["wup"], t["wgate"], t["wdown"])[i][:, hl, :, :].rearrange("p t n -> p (t n)")
    return w[:, j * 512:(j + 1) * 512]


def is_seq(n):
    return not isinstance(n, int) or 0 <= n < NSEQ


def wait(eng, sem, value):
    if not isinstance(value, int) or value > 0:
        eng.wait_ge(sem, value)


def attention(nc, t, a, h2):
    with ExitStack() as ctx:
        def sb(name, shape, dt):
            return ctx.enter_context(nc.sbuf_tensor(name, shape, dt))

        def sem(name):
            return ctx.enter_context(nc.semaphore(name))

        e_hl = sb("e_hl", [P, GS, 2 * ED], F16)
        eT_hl = sb("eT_hl", [P, GT], F16)
        h_res = sb("h_res", [P, GS, DM], F32)
        bn6 = sb("bn6", [P, GS, 6], F32)
        mv1 = sb("mv1", [P, GS, 2], F32)
        var1 = sb("var1", [P, GS], F32)
        rstd1 = sb("rstd1", [P, GS], F32)
        rs1 = sb("rs1", [P, GS], F32)
        x_dup = sb("x_dup", [P, GS, 2, ED], F32)
        x_hl = sb("x_hl", [P, GS, 2 * ED], F16)
        xT_hl = sb("xT_hl", [P, GT], F16)
        xT = sb("xT", [P, GT], F32)
        qT = sb("qT", [P, HP, GT], F32)
        v_aug = sb("v_aug", [P, GS, H, DV + 1], F32)
        lg = sb("lg", [P, 2, H, P], F32)
        row_max = sb("row_max", [P, 2, H], F32)
        pT = sb("pT", [P, 2, H, P], F32)
        inv_sum = sb("inv_sum", [P, 2, H], F32)
        o_s = sb("o_s", [P, 2, H, DV], F32)
        oT_hl = sb("oT_hl", [P, 2, 2, DT * P], F16)
        bn2 = sb("bn2", [P, GS, 6], F32)
        mv2 = sb("mv2", [P, GS, 2], F32)
        dev = sb("dev", [P, 2, DM], F32)
        dm4 = sb("dm4", [P, GS], F32)

        ps_f = ctx.enter_context(nc.psum_tensor("ps_front", [P, 2, 512], F32))
        ps_s = ctx.enter_context(nc.psum_tensor("ps_scores", [P, 2, 512], F32))
        ps_p = ctx.enter_context(nc.psum_tensor("ps_probs", [P, 2, 512], F32))
        ps_o = ctx.enter_context(nc.psum_tensor("ps_o", [P, 512], F32))
        ps_y = ctx.enter_context(nc.psum_tensor("ps_y", [P, 512], F32))

        ones_set = sem("ones_set")
        e_split = sem("e_split")
        front_done = sem("front_done")
        front_read = sem("front_read")
        stats1 = sem("stats1")
        rstd_step = sem("rstd_step")
        residual = sem("residual")
        x_split = sem("x_split")
        scores = sem("scores")
        biased = sem("biased")
        maxed = sem("maxed")
        shifted = sem("shifted")
        exped = sem("exped")
        p_turned = sem("p_turned")
        p_copied = sem("p_copied")
        mixed = sem("mixed")
        inverted = sem("inverted")
        o_normed = sem("o_normed")
        o_turned = sem("o_turned")
        o_high = sem("o_high")
        o_low = sem("o_low")
        projected = sem("projected")
        h2_done = sem("h2_done")
        stats2 = sem("stats2")
        aggr2 = sem("aggr2")
        dev_done = sem("dev_done")
        dev_maxed = sem("dev_maxed")
        copied2 = sem("copied2")

        block = ctx.enter_context(nc.Block())
        UNITS = 11

        def grouped(eng, front0, slot):
            front0()
            for g in range(2):
                for s in range(GS):
                    slot(g, s)
            with eng.Fori(2, NG - 1) as g:
                for s in range(GS):
                    slot(g, s)
            for g in range(NG - 1, NG + 2):
                for s in range(GS):
                    slot(g, s)

        @block.tensor
        def _(pe):
            def unit_ready(G, k):
                wait(pe, front_read, G * UNITS + k - (1 if k else 0))

            def front_a(G):
                pe.wait_ge(e_split, G * 2 + 2)
                unit_ready(G, 0)
                for s in range(GS):
                    last = pe.transpose(ps_f[:, 0, 0:GT // 2].bitcast(F16)[:, s * P:(s + 1) * P], e_hl[:, s, :], a["ident16"][:, :])
                last.then_inc(front_done, 1)
                pe.wait_ge(front_read, G * UNITS + 1)
                for k in (1, 2):
                    unit_ready(G, k)
                    for s in (2 * k - 2, 2 * k - 1):
                        for hl in range(2):
                            last = pe.matmul(ps_f[:, k % 2, s % 2 * DM:(s % 2 + 1) * DM], eT_hl[:, s * P:(s + 1) * P],
                                             a["pt"][:, hl, :], start=hl == 0, stop=hl == 1)
                    last.then_inc(front_done, 1)

            def front_b(G):
                pe.wait_ge(x_split, G * 3 + 3)
                unit_ready(G, 3)
                for s in range(GS):
                    last = pe.transpose(ps_f[:, 1, 0:GT // 2].bitcast(F16)[:, s * P:(s + 1) * P], x_hl[:, s, :], a["ident16"][:, :])
                last.then_inc(front_done, 1)
                unit_ready(G, 4)
                for s in range(GS):
                    last = pe.transpose(ps_f[:, 0, s * P:(s + 1) * P], x_dup[:, s, :, :].rearrange("p u d -> p (u d)"),
                                        t["ident32"][:, :])
                last.then_inc(front_done, 1)
                for pair in range(HP):
                    k = 5 + pair
                    unit_ready(G, k)
                    for hl in range(2):
                        last = pe.matmul(ps_f[:, k % 2, :], a["g"][:, hl, pair, :], xT_hl[:, :], start=hl == 0, stop=hl == 1)
                    last.then_inc(front_done, 1)

            def values(G):
                for k in (9, 10):
                    unit_ready(G, k)
                    for s in (2 * k - 18, 2 * k - 17):
                        for hl in range(2):
                            last = pe.matmul(ps_f[:, k % 2, s % 2 * DM:(s % 2 + 1) * DM], xT_hl[:, s * P:(s + 1) * P],
                                             a["mv"][:, hl, :], start=hl == 0, stop=hl == 1)
                    last.then_inc(front_done, 1)

            def slot(g, s):
                n = g * GS + s
                if is_seq(n):
                    if s == 0:
                        pe.wait_ge(front_read, g * UNITS + 9)
                    wait(pe, biased, n)
                    for pair in range(HP):
                        for parity in range(2):
                            r = slice(parity * ED, (parity + 1) * ED)
                            last = pe.matmul(ps_s[:, parity, pair * P:(pair + 1) * P], qT[r, pair, s * P:(s + 1) * P],
                                             xT[r, s * P:(s + 1) * P], start=True, stop=True)
                    last.then_inc(scores, 1)
                if is_seq(n + GS):
                    if s == 1:
                        front_a(g + 1)
                if is_seq(n - 1):
                    b = (s + 1) % 2
                    pe.wait_ge(exped, n)
                    wait(pe, p_copied, n - 1)
                    for q in range(H):
                        last = pe.transpose(ps_p[:, q // HP, q % HP * P:(q % HP + 1) * P], lg[:, b, q, :], t["ident32"][:, :])
                    last.then_inc(p_turned, 1)
                if is_seq(n + GS) and s == 3:
                    front_b(g + 1)
                if is_seq(n - 2):
                    pe.wait_ge(o_normed, n - 1)
                    wait(pe, h2_done, n - 2)
                    for k in range(DT):
                        last = pe.transpose(ps_y[:, k * P:(k + 1) * P],
                                            o_s[:, s % 2, :, :].rearrange("p h d -> p (h d)")[:, k * P:(k + 1) * P],
                                            t["ident32"][:, :])
                    last.then_inc(o_turned, 1)
                if is_seq(n - 1):
                    if s == 1:
                        pe.wait_ge(front_read, g * UNITS + UNITS)
                    pe.wait_ge(p_copied, n)
                    wait(pe, o_normed, n - 1)
                    for q in range(H):
                        h = 2 * (q % HP) + q // HP
                        last = pe.matmul(ps_o[:, h * (DV + 1):(h + 1) * (DV + 1)], pT[:, b, q, :],
                                         v_aug[:, (s - 1) % GS, h, :], start=True, stop=True)
                    last.then_inc(mixed, 1)
                if is_seq(n - 2):
                    pe.wait_ge(o_high, n - 1)
                    pe.wait_ge(o_low, n - 1)
                    terms = [(k, xh, wh) for k in range(DT) for xh, wh in ((0, 0), (1, 0), (0, 1))]
                    for i, (k, xh, wh) in enumerate(terms):
                        last = pe.matmul(ps_y[:, DM:2 * DM], oT_hl[:, s % 2, xh, k * P:(k + 1) * P], a["wo"][:, wh, k, :],
                                         start=i == 0, stop=i == len(terms) - 1)
                    last.then_inc(projected, 1)
                if s == 0 and is_seq(n):
                    values(g)

            pe.wait_ge(ones_set, 1)

            def front0():
                front_a(0)
                front_b(0)
            grouped(pe, front0, slot)

        @block.scalar
        def _(act):
            def unit(G, k):
                act.wait_ge(front_done, G * UNITS + k + 1)

            def front_a(G):
                unit(G, 0)
                act.copy(eT_hl[:, :], ps_f[:, 0, 0:GT // 2].bitcast(F16)).then_inc(front_read, 1)
                wait(act, residual, G)
                wait(act, stats1, G * 2)
                for k in (1, 2):
                    unit(G, k)
                    act.mul(h_res[:, 2 * k - 2:2 * k, :], ps_f[:, k % 2, :].rearrange("p (s f) -> p s f", f=DM),
                            a["h_scale"][:, 0:1]).then_inc(front_read, 1)

            def front_b(G):
                unit(G, 3)
                act.copy(xT_hl[:, :], ps_f[:, 1, 0:GT // 2].bitcast(F16)).then_inc(front_read, 1)
                unit(G, 4)
                wait(act, scores, G * GS)
                act.mul(xT[:, :], ps_f[:, 0, :], 1.0 / SC_X).then_inc(front_read, 1)
                for pair in range(HP):
                    unit(G, 5 + pair)
                    act.mul(qT[:, pair, :], ps_f[:, (5 + pair) % 2, :], 1.0 / (SC_X * SC_G)).then_inc(front_read, 1)

            def values(G):
                wait(act, mixed, G * GS)
                for k in (9, 10):
                    unit(G, k)
                    for s in range(2):
                        last = act.mul(v_aug[:, 2 * k - 18 + s, :, 0:DV],
                                       ps_f[:, k % 2, s * DM:(s + 1) * DM].rearrange("p (h d) -> p h d", d=DV),
                                       1.0 / (SC_X * SC_V))
                    last.then_inc(front_read, 1)

            def slot(g, s):
                n = g * GS + s
                if is_seq(n - 1):
                    b = (s + 1) % 2
                    act.wait_ge(shifted, n)
                    act.activation(lg[:, b, :, :], lg[:, b, :, :], ACT.Exp).then_inc(exped, 1)
                if is_seq(n + GS):
                    if s == 1:
                        front_a(g + 1)
                if is_seq(n - 1):
                    act.wait_ge(p_turned, n)
                    wait(act, mixed, n - 2)
                    act.copy(pT[:, b, :, :].rearrange("p (u q) j -> p u (q j)", u=2), ps_p[:, :, :]).then_inc(p_copied, 1)
                if is_seq(n + GS) and s == 3:
                    front_b(g + 1)
                if is_seq(n - 2):
                    act.wait_ge(o_turned, n - 1)
                    wait(act, projected, n - 3)
                    act.mul(oT_hl[:, s % 2, 0, :], ps_y[:, 0:DM], SC_O).then_inc(o_high, 1)
                if is_seq(n - 4):
                    act.wait_ge(aggr2, n - 3)
                    wait(act, dev_maxed, n - 5)
                    act.activation(dev[:, s % 2, :], h2[:, n - 4, :], ACT.Identity, bias=mv2[:, s % GS, 0:1],
                                   scale=-1.0).then_inc(dev_done, 1)
                if s == 0 and is_seq(n):
                    values(g)

            def front0():
                front_a(0)
                front_b(0)
            grouped(act, front0, slot)

        @block.gpsimd
        def _(pool):
            pool.memset(v_aug[:, :, :, DV:DV + 1], 1.0).then_inc(ones_set, 1)

            def front(G):
                pool.wait_ge(stats1, G * 2 + 2)
                pool.tensor_tensor(var1[:, :], mv1[:, :, 1], a["eps"][:, :], ALU.add).then_inc(rstd_step, 1)
                pool.wait_ge(rstd_step, G * 3 + 1)
                pool.tensor_tensor(rstd1[:, :], var1[:, :], a["minus_half"][:, :], ALU.pow).then_inc(rstd_step, 1)
                pool.wait_ge(rstd_step, G * 3 + 2)
                wait(pool, x_split, G * 3)
                pool.tensor_tensor(rs1[:, :], rstd1[:, :], a["x_scale"][:, 0:1].to_broadcast([P, GS]), ALU.mult).then_inc(rstd_step, 1)
                pool.tensor_tensor(h2[:, bass.ts(G, GS), :], h_res[:, :, :],
                                   a["bout"][:, :].unsqueeze(1).to_broadcast([P, GS, DM]), ALU.add).then_inc(residual, 1)

            def slot(g, s):
                n = g * GS + s
                if is_seq(n):
                    pool.wait_ge(maxed, n + 1)
                    pool.tensor_tensor(lg[:, s % 2, :, :], lg[:, s % 2, :, :],
                                       row_max[:, s % 2, :].unsqueeze(2).to_broadcast([P, H, P]),
                                       ALU.subtract).then_inc(shifted, 1)
                if s == 2 and is_seq(n + GS):
                    front(g + 1)

            grouped(pool, lambda: front(0), slot)

        @block.vector
        def _(dve):
            def split_raw(G):
                rows = a["emb_rows"][:, bass.ts(G, GS), :]
                wait(dve, front_done, (G - 1) * UNITS + 1)
                dve.tensor_scalar(e_hl[:, :, 0:ED], rows, SC_E, None, ALU.mult).then_inc(e_split, 1)
                dve.wait_ge(e_split, G * 2 + 1)
                dve.scalar_tensor_tensor(e_hl[:, :, ED:2 * ED], rows, SC_E, e_hl[:, :, 0:ED],
                                         ALU.mult, ALU.subtract).then_inc(e_split, 1)

            def stats_h(G):
                dve.wait_ge(front_read, G * UNITS + 3)
                for s in range(GS):
                    last = dve.bn_stats(bn6[:, s, :], h_res[:, s, :])
                last.then_inc(stats1, 1)

            def wait_stats_h(G):
                dve.wait_ge(stats1, G * 2 + 1)
                wait(dve, rstd_step, G * 3)

            def aggr_h(G):
                for s in range(GS):
                    last = dve.bn_aggr(mv1[:, s, :], bn6[:, s, :])
                last.then_inc(stats1, 1)

            def normalise(G):
                dve.wait_ge(rstd_step, G * 3 + 3)
                wait(dve, front_done, (G - 1) * UNITS + 5)
                dve.tensor_tensor(x_dup[:, :, :, :],
                                  a["emb_rows"][:, bass.ts(G, GS), :].unsqueeze(2).to_broadcast([P, GS, 2, ED]),
                                  rs1[:, :].unsqueeze(2).unsqueeze(3).to_broadcast([P, GS, 2, ED]),
                                  ALU.mult).then_inc(x_split, 1)
                dve.wait_ge(x_split, G * 3 + 1)
                dve.tensor_copy(x_hl[:, :, 0:ED], x_dup[:, :, 0, :]).then_inc(x_split, 1)
                dve.wait_ge(x_split, G * 3 + 2)
                dve.tensor_tensor(x_hl[:, :, ED:2 * ED], x_dup[:, :, 0, :], x_hl[:, :, 0:ED],
                                  ALU.subtract).then_inc(x_split, 1)

            def slot(g, s):
                n = g * GS + s
                b = s % 2
                if is_seq(n - 3):
                    m = (s + 1) % GS
                    dve.wait_ge(projected, n - 2)
                    if s == 3:
                        dve.wait_ge(residual, g + 1)
                    dve.scalar_tensor_tensor(h2[:, n - 3, :], ps_y[:, DM:2 * DM], 1.0 / (SC_O * SC_WO), h2[:, n - 3, :],
                                             ALU.mult, ALU.add).then_inc(h2_done, 1)
                if is_seq(n - 2):
                    dve.wait_ge(mixed, n - 1)
                    o_ps = ps_o[:, 0:H * (DV + 1)].rearrange("p (h d) -> p h d", d=DV + 1)
                    dve.reciprocal(inv_sum[:, b, :], o_ps[:, :, DV]).then_inc(inverted, 1)
                    dve.wait_ge(inverted, n - 1)
                    wait(dve, o_turned, n - 3)
                    dve.tensor_tensor(o_s[:, b, :, :], o_ps[:, :, 0:DV],
                                      inv_sum[:, b, :].unsqueeze(2).to_broadcast([P, H, DV]), ALU.mult).then_inc(o_normed, 1)
                if is_seq(n + GS) and s == 3:
                    normalise(g + 1)
                if is_seq(n):
                    dve.wait_ge(scores, n + 1)
                    wait(dve, p_turned, n - 1)
                    dve.tensor_tensor(lg[:, b, :, :].rearrange("p (u q) j -> p u (q j)", u=2), ps_s[:, :, :],
                                      a["bias"][:, :, :, :].rearrange("p u q j -> p u (q j)"), ALU.add).then_inc(biased, 1)
                    dve.wait_ge(biased, n + 1)
                    dve.tensor_reduce(row_max[:, b, :], lg[:, b, :, :], AX_X, ALU.max).then_inc(maxed, 1)
                if is_seq(n + GS):
                    if s == 0:
                        split_raw(g + 1)
                    if s == 2:
                        stats_h(g + 1)
                if is_seq(n + GS) and s == 2:
                    wait_stats_h(g + 1)
                if is_seq(n - 3):
                    dve.wait_ge(h2_done, n - 2)
                if is_seq(n - 2):
                    dve.wait_ge(o_high, n - 1)
                    dve.scalar_tensor_tensor(oT_hl[:, b, 1, :], ps_y[:, 0:DM], SC_O, oT_hl[:, b, 0, :],
                                             ALU.mult, ALU.subtract).then_inc(o_low, 1)
                if is_seq(n + GS) and s == 2:
                    aggr_h(g + 1)
                if is_seq(n - 3):
                    dve.bn_stats(bn2[:, m, :], h2[:, n - 3, :]).then_inc(stats2, 1)
                    dve.wait_ge(stats2, n - 2)
                if is_seq(n - 5):
                    dve.wait_ge(dev_done, n - 4)
                    dve.tensor_reduce(dm4[:, (s + 3) % GS:(s + 3) % GS + 1], dev[:, (s + 1) % 2, :], AX_X, ALU.max,
                                      apply_absolute_value=True).then_inc(dev_maxed, 1)
                if is_seq(n - 3):
                    dve.bn_aggr(mv2[:, m, :], bn2[:, m, :]).then_inc(aggr2, 1)
                if is_seq(n - 5) and s == 0:
                    dve.wait_ge(dev_maxed, n - 4)
                    dve.tensor_copy(t["dev_max"][:, bass.ts(g - 2, GS)], dm4[:, :]).then_inc(copied2, 1)
                if is_seq(n - 3) and s == 2:
                    dve.wait_ge(aggr2, n - 2)
                    dve.tensor_copy(t["mean_var"][:, bass.ts(g - 1, GS), :], mv2[:, :, :]).then_inc(copied2, 1)

            def front0():
                split_raw(0)
                stats_h(0)
                wait_stats_h(0)
                aggr_h(0)
                normalise(0)
            grouped(dve, front0, slot)


def feed_forward(nc, t, h2, out):
    with ExitStack() as ctx:
        c = {}
        for name in ("s_x", "k_x", "s_gate", "s_up", "k_gate", "k_up", "s_p", "k_p", "k_o", "s_y"):
            c[name] = ctx.enter_context(nc.sbuf_tensor(name, [P, 1], F32))[:, :]
        h2_d = nc.dram_tensor("h2_scratch", [P, NSEQ * DM], F32, kind="Internal").ap()
        qu_d = nc.dram_tensor("qu_scratch", [P, NG * NCH * CW], I16, kind="Internal").ap()
        amax = ctx.enter_context(nc.sbuf_tensor("amax", [P, 4], F32))
        acc = ctx.enter_context(nc.sbuf_tensor("acc", [P, 2], F32))
        acc2 = ctx.enter_context(nc.sbuf_tensor("acc2", [P, 2], F32))
        a_tok = ctx.enter_context(nc.sbuf_tensor("a_tok", [P, NSEQ], F32))
        with ExitStack() as inner:
            xq = inner.enter_context(nc.sbuf_tensor("xq_hl", [P, 2, DT, NSEQ * P], F16))
            input_scale(nc, t, c, a_tok)
            pass_max(nc, t, c, h2, a_tok, xq, amax, h2_d)
            gate_up_scales(nc, c, amax)
            pass_gate(nc, t, c, xq, acc)
            product_scale(nc, c, acc, "s_gate", None, 1.0 / 65536.0, "s_p", "k_p")
            pass_up(nc, t, c, xq, acc2, qu_d)
            product_scale(nc, c, acc2, "s_p", "s_up", 1.0, "s_y", "k_o", SC_W)
        pass_down(nc, t, c, h2_d, qu_d, out)


def input_scale(nc, t, c, a_tok):
    with ExitStack() as ctx:
        def sb(name, shape):
            return ctx.enter_context(nc.sbuf_tensor(name, shape, F32))
        eps, minus_half, var, rstd, tok = (sb(k, [P, NSEQ]) for k in ("x_eps", "x_minus_half", "x_var", "x_rstd", "x_tok"))
        mx, gx = sb("x_mx", [P, 1]), sb("x_gx", [P, 1])
        filled = ctx.enter_context(nc.semaphore("x_filled"))
        powed = ctx.enter_context(nc.semaphore("x_powed"))
        step = ctx.enter_context(nc.semaphore("x_step"))
        reduced = ctx.enter_context(nc.semaphore("x_reduced"))
        block = ctx.enter_context(nc.Block())

        @block.gpsimd
        def _(pool):
            pool.memset(eps[:, :], EPS).then_inc(filled, 1)
            pool.memset(minus_half[:, :], -0.5).then_inc(filled, 1)
            pool.wait_ge(filled, 2)
            pool.tensor_tensor(var[:, :], t["mean_var"][:, :, 1], eps[:, :], ALU.add).then_inc(powed, 1)
            pool.wait_ge(powed, 1)
            pool.tensor_tensor(rstd[:, :], var[:, :], minus_half[:, :], ALU.pow).then_inc(powed, 1)
            pool.wait_ge(step, 2)
            pool.partition_all_reduce(gx[:, :], mx[:, :], P, RMAX).then_inc(reduced, 1)

        @block.vector
        def _(dve):
            dve.wait_ge(powed, 2)
            dve.tensor_tensor(tok[:, :], t["dev_max"][:, :], rstd[:, :], ALU.mult).then_inc(step, 1)
            dve.wait_ge(step, 1)
            dve.tensor_reduce(mx[:, :], tok[:, :], AX_X, ALU.max).then_inc(step, 1)
            dve.wait_ge(reduced, 1)
            dve.tensor_scalar(c["s_x"], gx[:, :], 1.0 / QMAX, TINY, ALU.mult, ALU.max).then_inc(step, 1)
            dve.wait_ge(step, 3)
            dve.reciprocal(c["k_x"], c["s_x"]).then_inc(step, 1)
            dve.wait_ge(step, 4)
            dve.tensor_scalar(a_tok[:, :], rstd[:, :], c["k_x"], None, ALU.mult).then_inc(step, 1)


def gate_up_scales(nc, c, amax):
    with ExitStack() as ctx:
        mx = ctx.enter_context(nc.sbuf_tensor("ug_mx", [P, 2], F32))
        gx = ctx.enter_context(nc.sbuf_tensor("ug_gx", [P, 2], F32))
        sx = ctx.enter_context(nc.sbuf_tensor("ug_sx", [P, 1], F32))
        inv = ctx.enter_context(nc.sbuf_tensor("ug_inv", [P, 2], F32))
        step = ctx.enter_context(nc.semaphore("ug_step"))
        reduced = ctx.enter_context(nc.semaphore("ug_reduced"))
        block = ctx.enter_context(nc.Block())

        @block.gpsimd
        def _(pool):
            pool.wait_ge(step, 2)
            pool.partition_all_reduce(gx[:, :], mx[:, :], P, RMAX).then_inc(reduced, 1)

        @block.vector
        def _(dve):
            dve.tensor_scalar(sx[:, :], c["s_x"], 1.0 / SC_W, None, ALU.mult).then_inc(step, 1)
            dve.tensor_reduce(mx[:, :], amax[:, :].rearrange("p (w c) -> p w c", w=2), AX_X, ALU.max).then_inc(step, 1)
            dve.wait_ge(reduced, 1)
            dve.wait_ge(step, 2)
            for i, s in enumerate(("s_up", "s_gate")):
                dve.tensor_scalar(c[s], gx[:, i:i + 1], sx[:, :], 1.0 / QMAX, ALU.mult, ALU.mult).then_inc(step, 1)
            dve.wait_ge(step, 4)
            for i, s in enumerate(("s_up", "s_gate")):
                dve.tensor_scalar(c[s], c[s], TINY, None, ALU.max).then_inc(step, 1)
            dve.wait_ge(step, 6)
            for i, s in enumerate(("s_up", "s_gate")):
                dve.reciprocal(inv[:, i:i + 1], c[s]).then_inc(step, 1)
            dve.wait_ge(step, 8)
            for i, k in enumerate(("k_up", "k_gate")):
                dve.tensor_scalar(c[k], inv[:, i:i + 1], sx[:, :], None, ALU.mult).then_inc(step, 1)


def product_scale(nc, c, acc, sa, sb_, factor, s_out, k_out, divide=1.0):
    with ExitStack() as ctx:
        names = ("gx", "unit", "sc", "inv")
        gx, unit, sc, inv = (ctx.enter_context(nc.sbuf_tensor(f"{s_out}_{n}", [P, 1], F32))[:, :] for n in names)
        step = ctx.enter_context(nc.semaphore(f"{s_out}_step"))
        reduced = ctx.enter_context(nc.semaphore(f"{s_out}_reduced"))
        block = ctx.enter_context(nc.Block())

        @block.gpsimd
        def _(pool):
            pool.partition_all_reduce(gx, acc[:, 1:2], P, RMAX).then_inc(reduced, 1)

        @block.vector
        def _(dve):
            if sb_ is None:
                dve.tensor_scalar(unit, c[sa], factor, None, ALU.mult).then_inc(step, 1)
            else:
                dve.tensor_scalar(unit, c[sa], c[sb_], None, ALU.mult).then_inc(step, 1)
            dve.wait_ge(step, 1)
            dve.wait_ge(reduced, 1)
            dve.tensor_scalar(sc, gx, unit, 1.0 / QMAX, ALU.mult, ALU.mult).then_inc(step, 1)
            dve.wait_ge(step, 2)
            dve.tensor_scalar(sc, sc, TINY, None, ALU.max).then_inc(step, 1)
            dve.wait_ge(step, 3)
            dve.reciprocal(inv, sc).then_inc(step, 1)
            dve.tensor_scalar(c[s_out], sc, 1.0 / divide, None, ALU.mult).then_inc(step, 1)
            dve.wait_ge(step, 5)
            dve.tensor_scalar(c[k_out], inv, unit, None, ALU.mult).then_inc(step, 1)


def chunk_products(pe, ps, w, ch, xq, tok):
    for f in range(CT):
        cols = slice((ch * CT + f) * P, (ch * CT + f + 1) * P)
        terms = [(k, wh, xh) for k in range(DT) for wh, xh in ((0, 0), (0, 1), (1, 0))]
        for i, (k, wh, xh) in enumerate(terms):
            last = pe.matmul(ps[:, f, :], w[:, wh, k, cols], xq[:, xh, k, tok], start=i == 0, stop=i == len(terms) - 1)
    return last


def pass_max(nc, t, c, h2, a_tok, xq, amax, h2_d):
    with ExitStack() as ctx:
        def sb(name, shape, dt):
            return ctx.enter_context(nc.sbuf_tensor(name, shape, dt))

        def sem(name):
            return ctx.enter_context(nc.semaphore(name))
        y = sb("y_norm", [P, GS, DM], F32)
        xi = sb("x_int", [P, DT, GT], I16)
        amax_g = sb("amax_g", [P, 4], F32)
        ps_x = ctx.enter_context(nc.psum_tensor("ps_x", [P, DT, 512], F32))
        ps_c = [ctx.enter_context(nc.psum_tensor(f"ps_c{i}", [P, CT, 512], F32)) for i in range(2)]
        scaled = sem("scaled")
        x_turned = sem("x_turned")
        rounded = sem("rounded")
        x_split = sem("xq_split")
        products = sem("products")
        chunk_max = sem("chunk_max")
        running = sem("running")
        saved = sem("h2_saved")
        block = ctx.enter_context(nc.Block())

        def groups(eng, group):
            group(0, True)
            with eng.Fori(1, NG - 1) as g:
                group(g, True)
            group(NG - 1, False)

        @block.sync
        def _(sp):
            flat = h2.rearrange("p n f -> p (n f)")
            for q in range(4):
                part = slice(q * NSEQ * DM // 4, (q + 1) * NSEQ * DM // 4)
                sp.dma_start(h2_d[:, part], flat[:, part]).then_inc(saved, 16)
            sp.wait_ge(saved, 64)

        @block.tensor
        def _(pe):
            def turn(g):
                pe.wait_ge(scaled, g + 1)
                wait(pe, rounded, g)
                for s in range(GS):
                    for k in range(DT):
                        last = pe.transpose(ps_x[:, k, s * P:(s + 1) * P], y[:, s, k * P:(k + 1) * P], t["ident32"][:, :])
                last.then_inc(x_turned, 1)

            def group(g, more):
                pe.wait_ge(x_split, g * 2 + 2)
                for m in range(4):
                    if m == 2 and more:
                        turn(g + 1)
                    wait(pe, chunk_max, g * 4 + m - 1)
                    w = (t["wup"], t["wgate"])[m // 2]
                    chunk_products(pe, ps_c[m % 2], w, m % 2, xq, bass.ts(g, GT)).then_inc(products, 1)
            turn(0)
            groups(pe, group)

        @block.scalar
        def _(act):
            def round_(g):
                act.wait_ge(x_turned, g + 1)
                wait(act, x_split, g * 2)
                act.copy(xi[:, :, :], ps_x[:, :, :]).then_inc(rounded, 1)
            round_(0)
            groups(act, lambda g, more: more and round_(g + 1))

        @block.vector
        def _(dve):
            def scale(g):
                wait(dve, x_turned, g)
                for s in range(GS):
                    n = g * GS + s
                    last = dve.tensor_scalar(y[:, s, :], h2[:, n, :], t["mean_var"][:, n, 0:1], a_tok[:, bass.ts(n, 1)],
                                             ALU.subtract, ALU.mult)
                last.then_inc(scaled, 1)

            def split(g):
                tok = bass.ts(g, GT)
                dve.wait_ge(rounded, g + 1)
                dve.tensor_copy(xq[:, 0, :, tok], xi[:, :, :]).then_inc(x_split, 1)
                dve.wait_ge(x_split, g * 2 + 1)
                dve.tensor_tensor(xq[:, 1, :, tok], xi[:, :, :], xq[:, 0, :, tok], ALU.subtract).then_inc(x_split, 1)

            def group(g, more):
                if more:
                    scale(g + 1)
                for m in range(4):
                    if m == 0:
                        dve.wait_ge(running, g + 1)
                    dve.wait_ge(products, g * 4 + m + 1)
                    dve.tensor_reduce(amax_g[:, m:m + 1], ps_c[m % 2][:, :, :].rearrange("p f n -> p (f n)"), AX_X, ALU.max,
                                      apply_absolute_value=True).then_inc(chunk_max, 1)
                    if m == 1 and more:
                        split(g + 1)
                dve.wait_ge(chunk_max, g * 4 + 4)
                dve.tensor_tensor(amax[:, :], amax[:, :], amax_g[:, :], ALU.max).then_inc(running, 1)

            dve.memset(amax[:, :], 0.0).then_inc(running, 1)
            dve.wait_ge(running, 1)
            scale(0)
            split(0)
            groups(dve, group)


def pass_gate(nc, t, c, xq, acc):
    with ExitStack() as ctx:
        def sb(name, shape, dt):
            return ctx.enter_context(nc.sbuf_tensor(name, shape, dt))

        def sem(name):
            return ctx.enter_context(nc.semaphore(name))
        sig = sb("sig", [P, 2, CW], F32)
        qs = sb("qs", [P, 2, CW], U16)
        neg = sb("neg", [P, CW], I16)
        mag = sb("mag", [P, 2, CW], I16)
        ps_c = [ctx.enter_context(nc.psum_tensor(f"ps_g{i}", [P, CT, 512], F32)) for i in range(2)]
        products = sem("g_products")
        quantised = sem("g_quantised")
        sigged = sem("g_sigged")
        sig_q = sem("g_sig_q")
        negated = sem("g_negated")
        waited = sem("g_waited")
        magged = sem("g_magged")
        maxed = sem("g_maxed")
        block = ctx.enter_context(nc.Block())
        big = t["big"]

        def groups(eng, group):
            group(0)
            with eng.Fori(1, NG) as g:
                group(g)

        @block.tensor
        def _(pe):
            def group(g):
                for ch in range(NCH):
                    wait(pe, quantised, g * NCH + ch - 1)
                    chunk_products(pe, ps_c[ch], t["wgate"], ch, xq, bass.ts(g, GT)).then_inc(products, 1)
            groups(pe, group)

        @block.scalar
        def _(act):
            def quantise(m, ch):
                act.wait_ge(products, m + 1)
                act.mul(big[:, bass.ts(m, CW)], ps_c[ch][:, :, :].rearrange("p f n -> p (f n)"),
                        c["k_gate"]).then_inc(quantised, 1)

            def group(g, last=False):
                for ch in range(NCH):
                    m = g * NCH + ch
                    wait(act, sig_q, m - 1)
                    act.wait_ge(quantised, m + 1)
                    if not (last and ch == NCH - 1):
                        quantise(m + 1, 1 - ch)
                    act.activation(sig[:, ch, :], big[:, bass.ts(m, CW)], ACT.Sigmoid, scale=c["s_gate"]).then_inc(sigged, 1)
            quantise(0, 0)
            group(0)
            with act.Fori(1, NG - 1) as g:
                group(g)
            group(NG - 1, True)

        @block.gpsimd
        def _(pool):
            def group(g):
                for ch in range(NCH):
                    m = g * NCH + ch
                    pool.wait_ge(sigged, m + 1)
                    wait(pool, maxed, m - 1)
                    sigmoid_levels(pool, qs[:, ch, :], sig[:, ch, :], waited).then_inc(sig_q, 1)
            groups(pool, group)

        @block.vector
        def _(dve):
            def magnitude(m, ch):
                chunk = big[:, bass.ts(m, CW)]
                dve.wait_ge(quantised, m + 1)
                wait(dve, magged, m)
                dve.tensor_scalar(neg[:, :], chunk, -1.0, None, ALU.mult).then_inc(negated, 1)
                dve.wait_ge(negated, m + 1)
                if not (isinstance(m, int) and m == 0):
                    dve.wait_ge(sig_q, m)
                dve.tensor_tensor(mag[:, ch, :], chunk, neg[:, :], ALU.max).then_inc(magged, 1)

            def reduce(m, ch):
                dve.tensor_tensor_reduce(mag[:, ch, :], mag[:, ch, :], qs[:, ch, :], 1.0,
                                         0.0 if isinstance(m, int) and m == 0 else acc[:, 1 - ch:2 - ch],
                                         ALU.mult, ALU.max, acc[:, ch:ch + 1]).then_inc(maxed, 1)

            def group(g):
                for ch in range(NCH):
                    m = g * NCH + ch
                    magnitude(m, ch)
                    if not (isinstance(m, int) and m == 0):
                        reduce(m - 1, 1 - ch)
            groups(dve, group)
            dve.wait_ge(sig_q, NG * NCH)
            dve.wait_ge(magged, NG * NCH)
            dve.wait_ge(maxed, NG * NCH - 1)
            reduce(NG * NCH - 1, 1)


def sigmoid_levels(pool, out, sig, waited):
    pool.sem_inc(waited, 1)
    return pool.tensor_scalar(out, sig, 65536.0, 1.0, ALU.mult, ALU.mult)


def pass_up(nc, t, c, xq, acc, qu_d):
    with ExitStack() as ctx:
        def sb(name, shape, dt):
            return ctx.enter_context(nc.sbuf_tensor(name, shape, dt))

        def sem(name):
            return ctx.enter_context(nc.semaphore(name))
        sig = sb("u_sig", [P, CW], F32)
        qs = sb("u_qs", [P, 2, CW], U16)
        qu = sb("u_qu", [P, 2, CW], I16)
        mag_g = sb("u_mag_g", [P, CW], I16)
        mag_u = sb("u_mag_u", [P, 2, CW], I16)
        ps_c = [ctx.enter_context(nc.psum_tensor(f"ps_u{i}", [P, CT, 512], F32)) for i in range(2)]
        products = sem("u_products")
        quantised = sem("u_quantised")
        sigged = sem("u_sigged")
        sig_q = sem("u_sig_q")
        mag_up = sem("u_mag_up")
        negated = sem("u_negated")
        waited = sem("u_waited")
        gated = sem("u_gated")
        magged = sem("u_magged")
        maxed = sem("u_maxed")
        saved = [sem(f"u_saved{i}") for i in range(2)]
        block = ctx.enter_context(nc.Block())
        big = t["big"]

        def groups(eng, group):
            group(0)
            with eng.Fori(1, NG) as g:
                group(g)

        @block.sync
        def _(sp):
            def group(g):
                for ch in range(NCH):
                    m = g * NCH + ch
                    sp.wait_ge(quantised, m + 1)
                    sp.dma_start(qu_d[:, bass.ts(m, CW)], qu[:, ch, :]).then_inc(saved[ch], 16)
            groups(sp, group)
            for s in saved:
                sp.wait_ge(s, 16 * NG)

        @block.tensor
        def _(pe):
            def group(g):
                for ch in range(NCH):
                    wait(pe, quantised, g * NCH + ch - 1)
                    chunk_products(pe, ps_c[ch], t["wup"], ch, xq, bass.ts(g, GT)).then_inc(products, 1)
            groups(pe, group)

        @block.scalar
        def _(act):
            def sigmoid(m):
                wait(act, sig_q, m)
                act.activation(sig[:, :], big[:, bass.ts(m, CW)], ACT.Sigmoid, scale=c["s_gate"]).then_inc(sigged, 1)

            def group(g):
                for ch in range(NCH):
                    m = g * NCH + ch
                    ps = ps_c[ch][:, :, :].rearrange("p f n -> p (f n)")
                    sigmoid(m)
                    act.wait_ge(products, m + 1)
                    wait(act, maxed, m - 1)
                    act.activation(mag_u[:, ch, :], ps, ACT.Abs, scale=c["k_up"]).then_inc(mag_up, 1)
                    wait(act, saved[ch], g * 16)
                    act.mul(qu[:, ch, :], ps, c["k_up"]).then_inc(quantised, 1)
            groups(act, group)

        @block.gpsimd
        def _(pool):
            def group(g):
                for ch in range(NCH):
                    m = g * NCH + ch
                    pool.wait_ge(sigged, m + 1)
                    wait(pool, gated, m - 1)
                    sigmoid_levels(pool, qs[:, ch, :], sig[:, :], waited).then_inc(sig_q, 1)
            groups(pool, group)

        @block.vector
        def _(dve):
            def reduce(m, ch):
                dve.tensor_tensor_reduce(mag_u[:, ch, :], mag_g[:, :], mag_u[:, ch, :], 1.0,
                                         0.0 if isinstance(m, int) and m == 0 else acc[:, 1 - ch:2 - ch],
                                         ALU.mult, ALU.max, acc[:, ch:ch + 1]).then_inc(maxed, 1)

            def group(g):
                for ch in range(NCH):
                    m = g * NCH + ch
                    chunk = big[:, bass.ts(m, CW)]
                    wait(dve, magged, m)
                    wait(dve, mag_up, m)
                    dve.wait_ge(sig_q, m + 1)
                    dve.scalar_tensor_tensor(chunk, chunk, c["k_p"], qs[:, ch, :], ALU.mult, ALU.mult).then_inc(gated, 1)
                    if not (isinstance(m, int) and m == 0):
                        reduce(m - 1, 1 - ch)
                    dve.wait_ge(gated, m + 1)
                    wait(dve, maxed, m)
                    dve.tensor_scalar(mag_g[:, :], chunk, -1.0, None, ALU.mult).then_inc(negated, 1)
                    dve.wait_ge(negated, m + 1)
                    dve.tensor_tensor(mag_g[:, :], chunk, mag_g[:, :], ALU.max).then_inc(magged, 1)
            groups(dve, group)
            dve.wait_ge(magged, NG * NCH)
            dve.wait_ge(mag_up, NG * NCH)
            dve.wait_ge(maxed, NG * NCH - 1)
            reduce(NG * NCH - 1, 1)


def pass_down(nc, t, c, h2_d, qu_d, out):
    with ExitStack() as ctx:
        def sb(name, shape, dt):
            return ctx.enter_context(nc.sbuf_tensor(name, shape, dt))

        def sem(name):
            return ctx.enter_context(nc.semaphore(name))
        NB = 4
        qu = sb("d_qu", [P, NB, NCH * CW], I16)
        res = sb("d_res", [P, NB, GS * DM], F32)
        qo = sb("d_qo", [P, 2, CW], I16)
        o_hl = sb("d_o_hl", [P, 2, 2, CW * NCH], F16)
        y = sb("d_y", [P, NB, GS * DM], F32)
        ps_d = [ctx.enter_context(nc.psum_tensor(f"ps_d{i}", [P, 2, 512], F32)) for i in range(2)]
        loaded = [sem(f"d_loaded{i}") for i in range(NB)]
        levels = sem("d_levels")
        o_high = sem("d_high")
        o_low = sem("d_low")
        products = sem("d_products")
        added = sem("d_added")
        stored = [sem(f"d_stored{i}") for i in range(NB)]
        block = ctx.enter_context(nc.Block())
        big = t["big"]
        out_v = out.rearrange("n p f -> p n f")

        def rounds(eng, group):
            for g in range(NB):
                group(g, g, 0)
            with eng.Fori(1, NG // NB) as r:
                for b in range(NB):
                    group(r * NB + b, b, r)

        @block.sync
        def _(sp):
            def load(g, b):
                sp.dma_start(qu[:, b, :], qu_d[:, bass.ts(g, NCH * CW)]).then_inc(loaded[b], 16)
                sp.dma_start(res[:, b, :], h2_d[:, bass.ts(g, GS * DM)]).then_inc(loaded[b], 16)

            def store(g, b):
                sp.wait_ge(added, g + 1)
                sp.dma_start(out_v[:, bass.ts(g, GS), :], y[:, b, :].rearrange("p (s f) -> p s f", f=DM)).then_inc(stored[b], 16)
            for b in range(NB):
                load(b, b)
            with sp.Fori(0, NG // NB - 1) as r:
                for b in range(NB):
                    store(r * NB + b, b)
                    load(r * NB + NB + b, b)
            for b in range(NB):
                store(NG - NB + b, b)
            for s in stored:
                sp.wait_ge(s, 16 * NG // NB)

        @block.vector
        def _(dve):
            def finish(g, b, r):
                dve.wait_ge(products, g + 1)
                wait(dve, stored[b], r * 16)
                dve.scalar_tensor_tensor(y[:, b, :], ps_d[b % 2][:, :, :].rearrange("p b n -> p (b n)"), c["s_y"],
                                         res[:, b, :], ALU.mult, ALU.add).then_inc(added, 1)

            def quantise(g, b, r):
                dve.wait_ge(loaded[b], r * 32 + 32)
                wait(dve, o_low, g * NCH)
                for ch in range(NCH):
                    dve.scalar_tensor_tensor(qo[:, ch, :], big[:, bass.ts(g * NCH + ch, CW)], c["k_o"],
                                             qu[:, b, ch * CW:(ch + 1) * CW], ALU.mult, ALU.mult).then_inc(levels, 1)

            def split(g, b):
                for ch in range(NCH):
                    cols = slice(ch * CW, (ch + 1) * CW)
                    dve.wait_ge(o_high, g * NCH + ch + 1)
                    dve.tensor_tensor(o_hl[:, b % 2, 1, cols], qo[:, ch, :], o_hl[:, b % 2, 0, cols], ALU.subtract).then_inc(o_low, 1)

            def group(g, b, r):
                quantise(g, b, r)
                split(g, b)
                if not (isinstance(g, int) and g == 0):
                    finish(g - 1, (b - 1) % NB, r if b else r - 1)

            for g in range(NB + 1):
                group(g, g % NB, g // NB)
            with dve.Fori(1, NG // NB - 1) as r:
                for b in range(1, NB + 1):
                    group(r * NB + b, b % NB, r if b < NB else r + 1)
            for g in range(NG - NB + 1, NG):
                group(g, g % NB, g // NB)
            finish(NG - 1, NB - 1, NG // NB - 1)

        @block.scalar
        def _(act):
            def group(g, b, r):
                wait(act, products, g - 1)
                for ch in range(NCH):
                    act.wait_ge(levels, g * NCH + ch + 1)
                    act.copy(o_hl[:, b % 2, 0, ch * CW:(ch + 1) * CW], qo[:, ch, :]).then_inc(o_high, 1)
            rounds(act, group)

        @block.tensor
        def _(pe):
            def group(g, b, r):
                pe.wait_ge(o_low, g * NCH + NCH)
                wait(pe, added, g - 1)
                terms = [(k, xh, wh) for k in range(FT) for xh, wh in ((0, 0), (1, 0), (0, 1))]
                for s in range(GS):
                    for i, (k, xh, wh) in enumerate(terms):
                        last = pe.matmul(ps_d[b % 2][:, s // 2, s % 2 * DM:(s % 2 + 1) * DM],
                                         o_hl[:, b % 2, xh, k * GT + s * P:k * GT + (s + 1) * P], t["wdown"][:, wh, k, :],
                                         start=i == 0, stop=i == len(terms) - 1)
                last.then_inc(products, 1)
            rounds(pe, group)


_INS = ["x", "L0_tok_emb_weight", "L0_tok_proj_weight", "L0_tok_scale", "L0_attn_W_qk", "L0_attn_W_v",
        "L0_attn_W_out", "L0_attn_b_out", "L0_attn_conv", "L0_ffn_w_gate", "L0_ffn_w_up", "L0_ffn_w_down"]


def kernel(**inputs):
    import numpy as _np
    import concourse.bacc as _bacc
    from concourse import mybir as _mybir
    from concourse.bass_utils import run_bass_kernel_spmd as _run

    nc = _bacc.Bacc("TRN2", target_bir_lowering=False, num_devices=1)
    arrays, args = {}, []
    for name in _INS:
        v = _np.ascontiguousarray(inputs[name])
        if v.ndim == 0:
            v = v.reshape(1)
        arrays[f"in_{name}"] = v
        args.append(nc.dram_tensor(f"in_{name}", v.shape, _mybir.dt.from_np(v.dtype), kind="ExternalInput").ap())
    out = nc.dram_tensor("out_h", (NSEQ, P, DM), F32, kind="ExternalOutput").ap()
    build(nc, *args, out)
    r = _run(nc, [arrays], core_ids=[0])
    return r.results[0]["out_h"]
```

```python
from contextlib import ExitStack

import concourse.bass as bass
from concourse import mybir

ALU = mybir.AluOpType
ACT = mybir.ActivationFunctionType
F32 = mybir.dt.float32
F16 = mybir.dt.float16
I32 = mybir.dt.int32
U32 = mybir.dt.uint32
I16 = mybir.dt.int16
U16 = mybir.dt.uint16
AX_X = mybir.AxisListType.X
RMAX = bass.bass_isa.ReduceOp.max

P = 128
NSEQ = 64
GS = 4
NG = NSEQ // GS
GT = GS * P
VOC = 262144
ED = 64
DM = 256
DT = DM // P
H = 8
HP = H // 2
DV = DM // H
MAXPOS = 10
FF = 768
FT = FF // P
CT = 3
NCH = FT // CT
CW = CT * GT
WBLK = 32
EPS = 1e-5
QMAX = 32767.0
TINY = 1e-12
HASH_A, HASH_B = 36313, 27191
HASH_BITS = 18

SC_E = 2.0 ** 10
SC_P = 2.0 ** 10
SC_X = 2.0 ** 6
SC_G = 2.0 ** 6
SC_V = 2.0 ** 10
SC_O = 2.0 ** 8
SC_WO = 2.0 ** 8
SC_W = 2.0 ** 10
QK_SCALE = 64.0 ** -0.5


def build(nc, x, emb, proj, scale, w_qk, w_v, w_out, b_out, conv, w_gate, w_up, w_down, out):
    with ExitStack() as keep:
        def sb(name, shape, dt):
            return keep.enter_context(nc.sbuf_tensor(name, shape, dt))

        t = {}
        t["ident32"] = sb("ident32", [P, P], F32)
        t["wup"] = sb("wup_hl", [P, 2, DT, FF], F16)
        t["wgate"] = sb("wgate_hl", [P, 2, DT, FF], F16)
        t["wdown"] = sb("wdown_hl", [P, 2, FT, DM], F16)
        t["big"] = sb("big", [P, NG * NCH * CW], I16)
        t["mean_var"] = sb("mean_var", [P, NSEQ, 2], F32)
        t["rstd"] = sb("rstd2", [P, NSEQ], F32)
        t["dev_max"] = sb("dev_max", [P, NSEQ], F32)
        h2 = t["big"][:, 0:NSEQ * DM * 2].bitcast(F32).rearrange("p (n f) -> p n f", f=DM)
        with ExitStack() as attn:
            def sba(name, shape, dt):
                return attn.enter_context(nc.sbuf_tensor(name, shape, dt))
            a = {}
            a["ident16"] = sba("ident16", [P, P], F16)
            a["emb_rows"] = sba("emb_rows", [P, NSEQ, ED], F32)
            a["pt"] = sba("pt_hl", [P, 2, DM], F16)
            a["g"] = sba("g_hl", [P, 2, HP, P], F16)
            a["mv"] = sba("mv_hl", [P, 2, DM], F16)
            a["wo"] = sba("wo_hl", [P, 2, DT, DM], F16)
            a["bias"] = sba("pos_bias", [P, 2, HP, P], F32)
            a["bout"] = sba("bout_row", [P, DM], F32)
            a["h_scale"] = sba("h_scale", [P, 1], F32)
            a["x_scale"] = sba("x_scale", [P, 1], F32)
            a["minus_half"] = sba("minus_half", [P, GS], F32)
            a["eps"] = sba("eps", [P, GS], F32)
            prepare(nc, t, a, x, emb, proj, scale, w_qk, w_v, w_out, b_out, conv, w_gate, w_up, w_down)
            attention(nc, t, a, h2)
        feed_forward(nc, t, h2, out)


def prepare(nc, t, a, x, emb, proj, scale, w_qk, w_v, w_out, b_out, conv, w_gate, w_up, w_down):
    with ExitStack() as ctx:
        def sb(name, shape, dt):
            return ctx.enter_context(nc.sbuf_tensor(name, shape, dt))

        def sem(name):
            return ctx.enter_context(nc.semaphore(name))

        ids = sb("ids", [NSEQ, P], I32)
        mul_a = sb("mul_a", [NSEQ, P], I32)
        mul_b = sb("mul_b", [NSEQ, P], I32)
        prod_a = sb("prod_a", [NSEQ, P], I32)
        prod_b = sb("prod_b", [NSEQ, P], I32)
        mixed = sb("mixed", [NSEQ, P], I32)
        low_bits = sb("low_bits", [NSEQ, P], I32)
        high_bits = sb("high_bits", [NSEQ, P], I32)
        bucket = sb("bucket", [NSEQ, P], F32)
        wrap = sb("wrap", [NSEQ, P], F32)
        rows = sb("rows", [P, NSEQ], U32)
        p_nat = sb("p_nat", [P, DT, ED], F32)
        p_dup = sb("p_dup", [P, DT, 2, ED], F32)
        pc_dup = sb("pc_dup", [P, DT, 2, ED], F32)
        ones = sb("mean_ones", [P, P], F32)
        wqk_s = sb("wqk_s", [P, DT, 2 * H * ED], F32)
        wv_s = sb("wv_s", [P, DT, DM], F32)
        wo_s = sb("wo_s", [P, DT, DM], F32)
        mq = sb("mq", [P, HP, 2, ED], F32)
        mk = sb("mk", [P, HP, ED], F32)
        conv_s = sb("conv_s", [P, H, 2 * MAXPOS + 1], F32)
        window = sb("window", [P, H, 2 * P], F32)
        scale_s = sb("scale_s", [P, 1], F32)
        raw = [sb(f"ffw{i}", [P, FF * DM // P], F32) for i in range(3)]
        steps = sb("steps", [P, 3, FF * DM // P // WBLK], F32)
        inv_steps = sb("inv_steps", [P, 3, FF * DM // P // WBLK], F32)
        levels = sb("levels", [P, FF * DM // P], I16)
        window_d = nc.dram_tensor("window_scratch", [P, 2 * P * H], F32, kind="Internal").ap()

        ps_a = ctx.enter_context(nc.psum_tensor("ps_a", [P, 512], F32))
        ps_b = ctx.enter_context(nc.psum_tensor("ps_b", [P, 512], F32))
        ps_m = ctx.enter_context(nc.psum_tensor("ps_m", [P, ED], F32))
        ps_ge = ctx.enter_context(nc.psum_tensor("ps_ge", [P, 512], F32))
        ps_go = ctx.enter_context(nc.psum_tensor("ps_go", [P, 512], F32))
        ps_w = ctx.enter_context(nc.psum_tensor("ps_w", [P, 2, 512], F32))

        ids_in = sem("ids_in")
        p_in = sem("p_in")
        attn_in = sem("attn_in")
        small_in = sem("small_in")
        ffw_in = [sem(f"ffw_in{i}") for i in range(3)]
        consts = sem("consts")
        prods = sem("prods")
        hashing = sem("hashing")
        hash_turned = sem("hash_turned")
        rows_ready = sem("rows_ready")
        gathered = sem("gathered")
        windowed = sem("windowed")
        window_out = sem("window_out")
        bias_in = sem("bias_in")
        fold = sem("fold")
        pe_fold = sem("pe_fold")
        act_fold = sem("act_fold")
        quant = sem("quant")
        turned = sem("turned")
        high = sem("high")
        low = sem("low")

        block = ctx.enter_context(nc.Block())
        NB = FF * DM // P // WBLK

        @block.sync
        def _(sp):
            sp.dma_start(ids[:, :], x).then_inc(ids_in, 16)
            sp.dma_start(p_nat[:, :, :], proj.rearrange("(t p) d -> p t d", p=P)).then_inc(p_in, 16)
            sp.dma_start(wqk_s[:, :, :], w_qk.rearrange("(t p) n -> p t n", p=P)).then_inc(attn_in, 16)
            sp.dma_start(wv_s[:, :, :], w_v.rearrange("(t p) n -> p t n", p=P)).then_inc(attn_in, 16)
            sp.dma_start(wo_s[:, :, :], w_out.rearrange("(t p) n -> p t n", p=P)).then_inc(attn_in, 16)
            for i, (w, tiles) in enumerate(((w_up, FT), (w_gate, FT), (w_down, DT))):
                sp.dma_start(raw[i][:, :].rearrange("p (t n) -> p t n", t=tiles),
                             w.rearrange("(t p) n -> p t n", p=P)).then_inc(ffw_in[i], 16)
            sp.wait_ge(windowed, 3)
            sp.dma_start(window_d, window[:, :, :].rearrange("p h m -> p (h m)")).then_inc(window_out, 16)
            sp.wait_ge(window_out, 16)
            pitch = 2 * P * H - 1
            skewed = window_d.rearrange("p m -> (p m)")[P - 1:P - 1 + P * pitch].rearrange("(i m) -> i m", m=pitch)
            for parity in range(2):
                for pair in range(HP):
                    h = 2 * pair + parity
                    sp.dma_start(a["bias"][:, parity, pair, :],
                                 skewed[:, h * 2 * P:h * 2 * P + P]).then_inc(bias_in, 16)
            sp.wait_ge(bias_in, 16 * H)

        @block.gpsimd
        def _(pool):
            pool.memset(a["minus_half"][:, :], -0.5).then_inc(consts, 1)
            pool.memset(a["eps"][:, :], EPS).then_inc(consts, 1)
            pool.iota(mul_a[:, :], pattern=[[0, P]], base=HASH_A, channel_multiplier=0).then_inc(consts, 1)
            pool.iota(mul_b[:, :], pattern=[[0, P]], base=HASH_B, channel_multiplier=0).then_inc(consts, 1)
            pool.memset(t["ident32"][:, :], 0.0).then_inc(consts, 1)
            pool.memset(a["ident16"][:, :], 0.0).then_inc(consts, 1)
            pool.memset(ones[:, :], 1.0 / DM).then_inc(consts, 1)
            pool.wait_ge(ids_in, 16)
            pool.wait_ge(consts, 7)
            pool.tensor_tensor(prod_a[:, :], ids[:, :], mul_a[:, :], ALU.mult).then_inc(prods, 1)
            pool.tensor_tensor(prod_b[:, :], ids[:, :], mul_b[:, :], ALU.mult).then_inc(prods, 1)
            for m in (t["ident32"], a["ident16"]):
                pool.affine_select(out=m[:, :], in_=m[:, :], compare_op=ALU.not_equal, fill=1.0,
                                   base=0, pattern=[[-1, P]], channel_multiplier=1).then_inc(consts, 1)
            pool.wait_ge(rows_ready, 1)
            for n in range(NSEQ):
                pool.indirect_dma_start(a["emb_rows"][:, n, :], None, emb,
                                        bass.IndirectOffsetOnAxis(ap=rows[:, n:n + 1], axis=0)).then_inc(gathered, 16)
            pool.wait_ge(gathered, 16 * NSEQ)

        @block.scalar
        def _(act):
            act.dma_start(scale_s[:, :], scale.to_broadcast([P, 1])).then_inc(small_in, 16)
            act.dma_start(conv_s[:, :, :].rearrange("p h m -> p (h m)"),
                          conv.rearrange("h m -> (h m)").partition_broadcast(P)).then_inc(small_in, 16)
            act.dma_start(a["bout"][:, :], b_out.partition_broadcast(P)).then_inc(small_in, 16)
            act.wait_ge(small_in, 48)
            act.mul(a["h_scale"][:, :], scale_s[:, :], 1.0 / (SC_E * SC_P)).then_inc(act_fold, 1)
            act.mul(a["x_scale"][:, :], scale_s[:, :], SC_X).then_inc(act_fold, 1)
            edge = P - 1 - MAXPOS
            w = 2 * MAXPOS + 1
            act.copy(window[:, :, 0:edge], conv_s[:, :, 0:1].to_broadcast([P, H, edge])).then_inc(windowed, 1)
            act.copy(window[:, :, edge:edge + w], conv_s[:, :, :]).then_inc(windowed, 1)
            act.copy(window[:, :, edge + w:2 * P],
                     conv_s[:, :, w - 1:w].to_broadcast([P, H, 2 * P - edge - w])).then_inc(windowed, 1)
            act.wait_ge(pe_fold, 2)
            mqk = ps_b[:, :].rearrange("p (c d) -> p c d", d=ED)
            act.copy(mq[:, :, :, :], mqk[:, 0:HP, :].unsqueeze(2).to_broadcast([P, HP, 2, ED])).then_inc(act_fold, 1)
            act.copy(mk[:, :, :], mqk[:, HP:2 * HP, :]).then_inc(act_fold, 1)
            for n in range(9):
                act.wait_ge(turned, n + 1)
                i, j = n // 3, n % 3
                act.activation(transposed(t, i, j, 0), ps_w[:, n % 2, :], ACT.Copy, scale=SC_W).then_inc(high, 1)

        @block.vector
        def _(dve):
            dve.wait_ge(prods, 2)
            dve.tensor_tensor(mixed[:, 1:P], prod_a[:, 1:P], prod_b[:, 0:P - 1], ALU.bitwise_xor).then_inc(hashing, 1)
            dve.memset(mixed[:, 0:1], 0).then_inc(hashing, 1)
            dve.wait_ge(hashing, 2)
            dve.tensor_scalar(low_bits[:, :], mixed[:, :], VOC - 1, None, ALU.bitwise_and).then_inc(hashing, 1)
            dve.tensor_scalar(high_bits[:, :], mixed[:, :], HASH_BITS, None, ALU.arith_shift_right).then_inc(hashing, 1)
            dve.wait_ge(hashing, 4)
            dve.tensor_tensor(bucket[:, :], low_bits[:, :], high_bits[:, :], ALU.add).then_inc(hashing, 1)
            dve.wait_ge(hashing, 5)
            dve.tensor_scalar(wrap[:, :], bucket[:, :], float(VOC - 1), float(VOC - 1), ALU.is_ge, ALU.mult).then_inc(hashing, 1)
            dve.wait_ge(hashing, 6)
            dve.tensor_tensor(bucket[:, :], bucket[:, :], wrap[:, :], ALU.subtract).then_inc(hashing, 1)
            dve.wait_ge(hashing, 7)
            dve.tensor_scalar(wrap[:, :], bucket[:, :], 0.0, float(VOC - 1), ALU.is_lt, ALU.mult).then_inc(hashing, 1)
            dve.wait_ge(hashing, 8)
            dve.tensor_tensor(bucket[:, :], bucket[:, :], wrap[:, :], ALU.add).then_inc(hashing, 1)
            dve.wait_ge(hashing, 9)
            dve.memset(bucket[:, 0:1], float(VOC - 1)).then_inc(hashing, 1)
            dve.wait_ge(hash_turned, 1)
            dve.tensor_copy(rows[:, :], ps_a[:, 0:NSEQ]).then_inc(rows_ready, 1)

            dve.wait_ge(p_in, 16)
            dve.tensor_copy(p_dup[:, :, :, :], p_nat[:, :, :].unsqueeze(2).to_broadcast([P, DT, 2, ED])).then_inc(fold, 1)
            dve.wait_ge(pe_fold, 1)
            dve.tensor_tensor(pc_dup[:, :, :, :], p_nat[:, :, :].unsqueeze(2).to_broadcast([P, DT, 2, ED]),
                              ps_m[:, :].unsqueeze(1).unsqueeze(1).to_broadcast([P, DT, 2, ED]),
                              ALU.subtract).then_inc(fold, 1)
            dve.wait_ge(attn_in, 48)
            dve.tensor_scalar(a["wo"][:, 0, :, :], wo_s[:, :, :], SC_WO, None, ALU.mult).then_inc(fold, 1)
            dve.wait_ge(fold, 3)
            dve.scalar_tensor_tensor(a["wo"][:, 1, :, :], wo_s[:, :, :], SC_WO, a["wo"][:, 0, :, :],
                                     ALU.mult, ALU.subtract).then_inc(fold, 1)
            dve.wait_ge(pe_fold, 3)
            for hl, parity in ((0, 0), (0, 1)):
                ps = (ps_ge, ps_go)[parity][:, 0:HP * ED].rearrange("p (c d) -> p c d", d=ED)
                dve.tensor_scalar(a["g"][:, 0, :, parity * ED:(parity + 1) * ED], ps,
                                  SC_G * QK_SCALE, None, ALU.mult).then_inc(fold, 1)
            dve.wait_ge(fold, 6)
            for parity in range(2):
                ps = (ps_ge, ps_go)[parity][:, 0:HP * ED].rearrange("p (c d) -> p c d", d=ED)
                cols = slice(parity * ED, (parity + 1) * ED)
                dve.scalar_tensor_tensor(a["g"][:, 1, :, cols], ps, SC_G * QK_SCALE, a["g"][:, 0, :, cols],
                                         ALU.mult, ALU.subtract).then_inc(fold, 1)
            dve.wait_ge(pe_fold, 4)
            for k, (w, ps, sc) in enumerate(((a["mv"], ps_w[:, 0, 0:DM], SC_V), (a["pt"], ps_w[:, 1, 0:DM], SC_P))):
                dve.tensor_scalar(w[:, 0, :], ps, sc, None, ALU.mult).then_inc(fold, 1)
                dve.wait_ge(fold, 9 + 2 * k)
                dve.scalar_tensor_tensor(w[:, 1, :], ps, sc, w[:, 0, :], ALU.mult, ALU.subtract).then_inc(fold, 1)

            for i in range(3):
                blocks = raw[i][:, :].rearrange("p (b k) -> p b k", k=WBLK)
                lv = levels[:, :].rearrange("p (b k) -> p b k", k=WBLK)
                dve.wait_ge(ffw_in[i], 16)
                dve.tensor_reduce(steps[:, i, :], blocks, AX_X, ALU.max, apply_absolute_value=True).then_inc(quant, 1)
                dve.wait_ge(quant, 5 * i + 1)
                dve.tensor_scalar(steps[:, i, :], steps[:, i, :], 1.0 / 7.0, TINY, ALU.mult, ALU.max).then_inc(quant, 1)
                dve.wait_ge(quant, 5 * i + 2)
                dve.reciprocal(inv_steps[:, i, :], steps[:, i, :]).then_inc(quant, 1)
                dve.wait_ge(quant, 5 * i + 3)
                dve.tensor_tensor(lv, blocks, inv_steps[:, i, :].unsqueeze(2).to_broadcast([P, NB, WBLK]),
                                  ALU.mult).then_inc(quant, 1)
                dve.wait_ge(quant, 5 * i + 4)
                dve.tensor_tensor(blocks, lv, steps[:, i, :].unsqueeze(2).to_broadcast([P, NB, WBLK]),
                                  ALU.mult).then_inc(quant, 1)
            for n in range(9):
                dve.wait_ge(high, n + 1)
                i, j = n // 3, n % 3
                dve.scalar_tensor_tensor(transposed(t, i, j, 1), ps_w[:, n % 2, :], SC_W, transposed(t, i, j, 0),
                                         ALU.mult, ALU.subtract).then_inc(low, 1)

        @block.tensor
        def _(pe):
            pe.wait_ge(consts, 9)
            pe.wait_ge(hashing, 10)
            pe.transpose(ps_a[:, 0:NSEQ], bucket[:, :], t["ident32"][0:NSEQ, 0:NSEQ]).then_inc(hash_turned, 1)
            pe.wait_ge(p_in, 16)
            for k in range(DT):
                last = pe.matmul(ps_m[:, :], ones[:, :], p_nat[:, k, :], start=k == 0, stop=k == DT - 1)
            last.then_inc(pe_fold, 1)
            pe.wait_ge(attn_in, 48)
            pe.wait_ge(fold, 2)
            for c in range(2 * HP):
                for k in range(DT):
                    last = pe.matmul(ps_b[:, c * ED:(c + 1) * ED], wqk_s[:, k, c * P:(c + 1) * P],
                                     pc_dup[:, k, 0, :], start=k == 0, stop=k == DT - 1)
            last.then_inc(pe_fold, 1)
            pe.wait_ge(act_fold, 4)
            for pair in range(HP):
                for parity in range(2):
                    r = slice(parity * ED, (parity + 1) * ED)
                    last = pe.matmul((ps_ge, ps_go)[parity][:, pair * ED:(pair + 1) * ED],
                                     mq[r, pair, :, :].rearrange("c u d -> c (u d)"), mk[r, pair, :],
                                     start=True, stop=True)
            last.then_inc(pe_fold, 1)
            for k in range(DT):
                pe.matmul(ps_w[:, 0, 0:DM], pc_dup[:, k, :, :].rearrange("p u d -> p (u d)"), wv_s[:, k, :],
                          start=k == 0, stop=k == DT - 1)
            for k in range(DT):
                last = pe.transpose(ps_w[:, 1, k * P:(k + 1) * P], p_dup[:, k, :, :].rearrange("p u d -> p (u d)"),
                                    t["ident32"][:, :])
            last.then_inc(pe_fold, 1)
            for n in range(9):
                i, j = n // 3, n % 3
                pe.wait_ge(quant, 5 * i + 5)
                if n < 2:
                    pe.wait_ge(fold, 12)
                if n >= 2:
                    pe.wait_ge(low, n - 1)
                for q in range(4):
                    if i < 2:
                        kt, ot = (4 * j + q) // FT, (4 * j + q) % FT
                        src = raw[i][:, ot * DM + kt * P:ot * DM + (kt + 1) * P]
                    else:
                        kt, ot = (4 * j + q) // DT, (4 * j + q) % DT
                        src = raw[i][:, ot * FF + kt * P:ot * FF + (kt + 1) * P]
                    last = pe.transpose(ps_w[:, n % 2, q * P:(q + 1) * P], src, t["ident32"][:, :])
                last.then_inc(turned, 1)


def transposed(t, i, j, hl):
    w = (t["wup"], t["wgate"], t["wdown"])[i][:, hl, :, :].rearrange("p t n -> p (t n)")
    return w[:, j * 512:(j + 1) * 512]


def is_seq(n):
    return not isinstance(n, int) or 0 <= n < NSEQ


def wait(eng, sem, value):
    if not isinstance(value, int) or value > 0:
        eng.wait_ge(sem, value)


def attention(nc, t, a, h2):
    with ExitStack() as ctx:
        def sb(name, shape, dt):
            return ctx.enter_context(nc.sbuf_tensor(name, shape, dt))

        def sem(name):
            return ctx.enter_context(nc.semaphore(name))

        e_hl = sb("e_hl", [P, GS, 2 * ED], F16)
        eT_hl = sb("eT_hl", [P, GT], F16)
        h_res = sb("h_res", [P, GS, DM], F32)
        bn6 = sb("bn6", [P, GS, 6], F32)
        mv1 = sb("mv1", [P, GS, 2], F32)
        var1 = sb("var1", [P, GS], F32)
        rstd1 = sb("rstd1", [P, GS], F32)
        rs1 = sb("rs1", [P, GS], F32)
        x_dup = sb("x_dup", [P, GS, 2, ED], F32)
        x_hl = sb("x_hl", [P, GS, 2 * ED], F16)
        xT_hl = sb("xT_hl", [P, GT], F16)
        xT = sb("xT", [P, 2, GT], F32)
        qT = sb("qT", [P, 2, HP, GT], F32)
        v_aug = sb("v_aug", [P, 2, GS, H, DV + 1], F32)
        lg = sb("lg", [P, 2, H, P], F32)
        row_max = sb("row_max", [P, 2, H], F32)
        pT = sb("pT", [P, 2, H, P], F32)
        inv_sum = sb("inv_sum", [P, 2, H], F32)
        o_s = sb("o_s", [P, 2, H, DV], F32)
        oT_hl = sb("oT_hl", [P, 2, 2, DT * P], F16)
        bn2 = sb("bn2", [P, GS, 6], F32)
        mv2 = sb("mv2", [P, GS, 2], F32)
        dev = sb("dev", [P, 2, DM], F32)
        dm4 = sb("dm4", [P, GS], F32)
        var2 = sb("var2", [P, GS], F32)

        ps_f = ctx.enter_context(nc.psum_tensor("ps_front", [P, 2, 512], F32))
        ps_s = ctx.enter_context(nc.psum_tensor("ps_scores", [P, 2, 512], F32))
        ps_p = ctx.enter_context(nc.psum_tensor("ps_probs", [P, 2, 512], F32))
        ps_o = ctx.enter_context(nc.psum_tensor("ps_o", [P, 512], F32))
        ps_y = ctx.enter_context(nc.psum_tensor("ps_y", [P, 512], F32))

        ones_set = sem("ones_set")
        e_split = sem("e_split")
        front_done = sem("front_done")
        front_read = sem("front_read")
        stats1 = sem("stats1")
        rstd_step = sem("rstd_step")
        residual = sem("residual")
        x_split = sem("x_split")
        scores = sem("scores")
        biased = sem("biased")
        maxed = sem("maxed")
        shifted = sem("shifted")
        exped = sem("exped")
        p_turned = sem("p_turned")
        p_copied = sem("p_copied")
        mixed = sem("mixed")
        inverted = sem("inverted")
        o_normed = sem("o_normed")
        o_turned = sem("o_turned")
        o_high = sem("o_high")
        o_low = sem("o_low")
        projected = sem("projected")
        h2_done = sem("h2_done")
        stats2 = sem("stats2")
        aggr2 = sem("aggr2")
        dev_done = sem("dev_done")
        dev_maxed = sem("dev_maxed")
        mv_moved = sem("mv_moved")
        dev_moved = sem("dev_moved")
        rstd2_step = sem("rstd2_step")

        block = ctx.enter_context(nc.Block())
        V0, V1, NORMAL_SPLIT, NORMAL_WHOLE, RAW, H0, H1, Q0, Q1, Q2, Q3 = units = list(range(11))
        UNITS = len(units)

        def units_of(g):
            if g == -2:
                return [RAW, H0, H1]
            if g == -1:
                return units[NORMAL_SPLIT:]
            if g == NG - 2:
                return [k for k in units if k not in (RAW, H0, H1)]
            return [V0, V1] if g == NG - 1 else units

        def before(g, k):
            if not isinstance(g, int):
                return g * UNITS + (len(units_of(-2)) + len(units_of(-1)) + k)
            return sum(len(units_of(e)) for e in range(-2, g)) + units_of(g).index(k)

        def grouped(eng, front0, slot):
            front0()
            for g in range(2):
                for s in range(GS):
                    slot(g, s, g % 2)
            with eng.Fori(1, NG // 2 - 1) as pair:
                for b in range(2):
                    for s in range(GS):
                        slot(pair * 2 + b, s, b)
            for g in range(NG - 2, NG + 2):
                for s in range(GS):
                    slot(g, s, g % 2)

        @block.tensor
        def _(pe):
            def unit_ready(g, k):
                mine = units_of(g) if isinstance(g, int) else units
                other_bank = k != mine[0] and (mine[mine.index(k) - 1] - k) % 2
                wait(pe, front_read, before(g, k) - (1 if other_bank else 0))

            def turn_raw(G):
                pe.wait_ge(e_split, G * 2 + 2)
                unit_ready(G - 2, RAW)
                for s in range(GS):
                    last = pe.transpose(ps_f[:, RAW % 2, 0:GT // 2].bitcast(F16)[:, s * P:(s + 1) * P], e_hl[:, s, :],
                                        a["ident16"][:, :])
                last.then_inc(front_done, 1)

            def project_raw(G, k):
                if k == H0:
                    pe.wait_ge(front_read, before(G - 2, RAW) + 1)
                unit_ready(G - 2, k)
                for s in (2 * (k - H0), 2 * (k - H0) + 1):
                    for hl in range(2):
                        last = pe.matmul(ps_f[:, k % 2, s % 2 * DM:(s % 2 + 1) * DM], eT_hl[:, s * P:(s + 1) * P],
                                         a["pt"][:, hl, :], start=hl == 0, stop=hl == 1)
                last.then_inc(front_done, 1)

            def turn_normal_split(G):
                pe.wait_ge(x_split, G * 3 + 3)
                unit_ready(G - 1, NORMAL_SPLIT)
                for s in range(GS):
                    last = pe.transpose(ps_f[:, NORMAL_SPLIT % 2, 0:GT // 2].bitcast(F16)[:, s * P:(s + 1) * P],
                                        x_hl[:, s, :], a["ident16"][:, :])
                last.then_inc(front_done, 1)

            def turn_normal_whole(G):
                unit_ready(G - 1, NORMAL_WHOLE)
                for s in range(GS):
                    last = pe.transpose(ps_f[:, NORMAL_WHOLE % 2, s * P:(s + 1) * P],
                                        x_dup[:, s, :, :].rearrange("p u d -> p (u d)"), t["ident32"][:, :])
                last.then_inc(front_done, 1)

            def queries(G, pair):
                k = Q0 + pair
                unit_ready(G - 1, k)
                if pair == 0:
                    pe.wait_ge(front_read, before(G - 1, NORMAL_SPLIT) + 1)
                for hl in range(2):
                    last = pe.matmul(ps_f[:, k % 2, :], a["g"][:, hl, pair, :], xT_hl[:, :], start=hl == 0, stop=hl == 1)
                last.then_inc(front_done, 1)

            def values(G, k):
                unit_ready(G, k)
                for s in (2 * k, 2 * k + 1):
                    for hl in range(2):
                        last = pe.matmul(ps_f[:, k % 2, s % 2 * DM:(s % 2 + 1) * DM], xT_hl[:, s * P:(s + 1) * P],
                                         a["mv"][:, hl, :], start=hl == 0, stop=hl == 1)
                last.then_inc(front_done, 1)

            def front_units(g, s):
                nxt, raw = is_seq((g + 1) * GS), is_seq((g + 2) * GS)
                if s == 0 and is_seq(g * GS):
                    return [lambda: values(g, V0), lambda: values(g, V1)]
                if s == 1 and nxt:
                    return [lambda: turn_normal_split(g + 1), lambda: turn_normal_whole(g + 1)] + (
                        [lambda: turn_raw(g + 2)] if raw else [])
                if s == 2 and nxt:
                    return ([lambda: project_raw(g + 2, H0), lambda: project_raw(g + 2, H1)] if raw else []) + [
                        lambda: queries(g + 1, 0)]
                if s == 3 and nxt:
                    return [lambda: queries(g + 1, 1), lambda: queries(g + 1, 2), lambda: queries(g + 1, 3)]
                return []

            def slot(g, s, par):
                n = g * GS + s
                front = front_units(g, s)
                if is_seq(n):
                    if s == 0:
                        pe.wait_ge(front_read, before(g - 1, Q3) + 1)
                    wait(pe, biased, n)
                    for pair in range(HP):
                        for parity in range(2):
                            r = slice(parity * ED, (parity + 1) * ED)
                            last = pe.matmul(ps_s[:, parity, pair * P:(pair + 1) * P], qT[r, par, pair, s * P:(s + 1) * P],
                                             xT[r, par, s * P:(s + 1) * P], start=True, stop=True)
                    last.then_inc(scores, 1)
                if is_seq(n - 2):
                    pe.wait_ge(o_normed, n - 1)
                    wait(pe, h2_done, n - 2)
                    for k in range(DT):
                        last = pe.transpose(ps_y[:, k * P:(k + 1) * P],
                                            o_s[:, s % 2, :, :].rearrange("p h d -> p (h d)")[:, k * P:(k + 1) * P],
                                            t["ident32"][:, :])
                    last.then_inc(o_turned, 1)
                if front:
                    front[0]()
                if is_seq(n - 1):
                    b = (s + 1) % 2
                    pe.wait_ge(exped, n)
                    wait(pe, p_copied, n - 1)
                    for q in range(H):
                        last = pe.transpose(ps_p[:, q // HP, q % HP * P:(q % HP + 1) * P], lg[:, b, q, :], t["ident32"][:, :])
                    last.then_inc(p_turned, 1)
                if len(front) > 1:
                    front[1]()
                if is_seq(n - 2):
                    pe.wait_ge(o_high, n - 1)
                    pe.wait_ge(o_low, n - 1)
                    terms = [(k, xh, wh) for k in range(DT) for xh, wh in ((0, 0), (1, 0), (0, 1))]
                    for i, (k, xh, wh) in enumerate(terms):
                        last = pe.matmul(ps_y[:, DM:2 * DM], oT_hl[:, s % 2, xh, k * P:(k + 1) * P], a["wo"][:, wh, k, :],
                                         start=i == 0, stop=i == len(terms) - 1)
                    last.then_inc(projected, 1)
                if len(front) > 2:
                    front[2]()
                if is_seq(n - 1):
                    if s == 1:
                        pe.wait_ge(front_read, before(g, V1) + 1)
                    pe.wait_ge(p_copied, n)
                    wait(pe, o_normed, n - 1)
                    for q in range(H):
                        h = 2 * (q % HP) + q // HP
                        last = pe.matmul(ps_o[:, h * (DV + 1):(h + 1) * (DV + 1)], pT[:, b, q, :],
                                         v_aug[:, par if s else 1 - par, (s - 1) % GS, h, :], start=True, stop=True)
                    last.then_inc(mixed, 1)

            pe.wait_ge(ones_set, 1)

            def front0():
                turn_raw(0)
                project_raw(0, H0)
                project_raw(0, H1)
                turn_normal_split(0)
                turn_normal_whole(0)
                turn_raw(1)
                project_raw(1, H0)
                project_raw(1, H1)
                for pair in range(HP):
                    queries(0, pair)
            grouped(pe, front0, slot)

        @block.scalar
        def _(act):
            def unit(g, k):
                act.wait_ge(front_done, before(g, k) + 1)

            def copy_raw(G):
                unit(G - 2, RAW)
                act.copy(eT_hl[:, :], ps_f[:, RAW % 2, 0:GT // 2].bitcast(F16)).then_inc(front_read, 1)

            def copy_h(G, k):
                if k == H0:
                    wait(act, residual, G)
                    wait(act, stats1, G * 2)
                unit(G - 2, k)
                act.mul(h_res[:, 2 * (k - H0):2 * (k - H0) + 2, :], ps_f[:, k % 2, :].rearrange("p (s f) -> p s f", f=DM),
                        a["h_scale"][:, 0:1]).then_inc(front_read, 1)

            def copy_normal_split(G):
                unit(G - 1, NORMAL_SPLIT)
                act.copy(xT_hl[:, :], ps_f[:, NORMAL_SPLIT % 2, 0:GT // 2].bitcast(F16)).then_inc(front_read, 1)

            def copy_normal_whole(G, par):
                unit(G - 1, NORMAL_WHOLE)
                wait(act, scores, (G - 1) * GS)
                act.mul(xT[:, par, :], ps_f[:, NORMAL_WHOLE % 2, :], 1.0 / SC_X).then_inc(front_read, 1)

            def copy_queries(G, par, pair):
                k = Q0 + pair
                unit(G - 1, k)
                act.mul(qT[:, par, pair, :], ps_f[:, k % 2, :], 1.0 / (SC_X * SC_G)).then_inc(front_read, 1)

            def copy_values(G, par, k):
                if k == V0:
                    wait(act, mixed, (G - 1) * GS)
                unit(G, k)
                act.mul(v_aug[:, par, 2 * k:2 * k + 2, :, 0:DV].rearrange("p s h d -> p (s h) d"),
                        ps_f[:, k % 2, :].rearrange("p (h d) -> p h d", d=DV),
                        1.0 / (SC_X * SC_V)).then_inc(front_read, 1)

            def front_units(g, s, par):
                nxt, raw = is_seq((g + 1) * GS), is_seq((g + 2) * GS)
                if s == 0 and is_seq(g * GS):
                    return [lambda: copy_values(g, par, V0), lambda: copy_values(g, par, V1)]
                if s == 1 and nxt:
                    return [lambda: copy_normal_split(g + 1), lambda: copy_normal_whole(g + 1, 1 - par)] + (
                        [lambda: copy_raw(g + 2)] if raw else [])
                if s == 2 and nxt:
                    return ([lambda: copy_h(g + 2, H0), lambda: copy_h(g + 2, H1)] if raw else []) + [
                        lambda: copy_queries(g + 1, 1 - par, 0)]
                if s == 3 and nxt:
                    return [lambda: copy_queries(g + 1, 1 - par, 1), lambda: copy_queries(g + 1, 1 - par, 2),
                            lambda: copy_queries(g + 1, 1 - par, 3)]
                return []

            def slot(g, s, par):
                n = g * GS + s
                front = front_units(g, s, par)
                if is_seq(n - 1):
                    b = (s + 1) % 2
                    act.wait_ge(shifted, n)
                    act.activation(lg[:, b, :, :], lg[:, b, :, :], ACT.Exp).then_inc(exped, 1)
                if is_seq(n - 2):
                    act.wait_ge(o_turned, n - 1)
                    wait(act, projected, n - 3)
                    act.mul(oT_hl[:, s % 2, 0, :], ps_y[:, 0:DM], SC_O).then_inc(o_high, 1)
                if front:
                    front[0]()
                if is_seq(n - 1):
                    act.wait_ge(p_turned, n)
                    wait(act, mixed, n - 2)
                    act.copy(pT[:, b, :, :].rearrange("p (u q) j -> p u (q j)", u=2), ps_p[:, :, :]).then_inc(p_copied, 1)
                for unit_read in front[1:]:
                    unit_read()
                if is_seq(n - 4):
                    act.wait_ge(aggr2, n - 3)
                    wait(act, dev_maxed, n - 5)
                    act.activation(dev[:, s % 2, :], h2[:, n - 4, :], ACT.Identity, bias=mv2[:, s % GS, 0:1],
                                   scale=-1.0).then_inc(dev_done, 1)

            def front0():
                copy_raw(0)
                copy_h(0, H0)
                copy_h(0, H1)
                copy_normal_split(0)
                copy_normal_whole(0, 0)
                copy_raw(1)
                copy_h(1, H0)
                copy_h(1, H1)
                for pair in range(HP):
                    copy_queries(0, 0, pair)
            grouped(act, front0, slot)

        @block.gpsimd
        def _(pool):
            pool.memset(v_aug[:, :, :, :, DV:DV + 1].rearrange("p b s h u -> p (b s h u)"), 1.0).then_inc(ones_set, 1)

            def rstd_of_h(G):
                pool.wait_ge(stats1, G * 2 + 2)
                pool.tensor_tensor(var1[:, :], mv1[:, :, 1], a["eps"][:, :], ALU.add).then_inc(rstd_step, 1)
                pool.wait_ge(rstd_step, G * 3 + 1)
                pool.tensor_tensor(rstd1[:, :], var1[:, :], a["minus_half"][:, :], ALU.pow).then_inc(rstd_step, 1)
                pool.wait_ge(rstd_step, G * 3 + 2)
                wait(pool, x_split, G * 3)
                pool.tensor_tensor(rs1[:, :], rstd1[:, :], a["x_scale"][:, 0:1].to_broadcast([P, GS]), ALU.mult).then_inc(rstd_step, 1)

            def add_bias(G):
                pool.wait_ge(front_read, before(G - 2, H1) + 1)
                pool.tensor_tensor(h2[:, bass.ts(G, GS), :], h_res[:, :, :],
                                   a["bout"][:, :].unsqueeze(1).to_broadcast([P, GS, DM]), ALU.add).then_inc(residual, 1)

            def rstd_of_h2(G):
                pool.wait_ge(mv_moved, G + 1)
                wait(pool, rstd2_step, G * 2)
                pool.tensor_tensor(var2[:, :], t["mean_var"][:, bass.ts(G, GS), 1], a["eps"][:, :], ALU.add).then_inc(rstd2_step, 1)
                pool.wait_ge(rstd2_step, G * 2 + 1)
                pool.tensor_tensor(t["rstd"][:, bass.ts(G, GS)], var2[:, :], a["minus_half"][:, :], ALU.pow).then_inc(rstd2_step, 1)

            def slot(g, s, par):
                n = g * GS + s
                if s == 0 and is_seq(n + GS):
                    rstd_of_h(g + 1)
                if is_seq(n):
                    pool.wait_ge(maxed, n + 1)
                    pool.tensor_tensor(lg[:, s % 2, :, :], lg[:, s % 2, :, :],
                                       row_max[:, s % 2, :].unsqueeze(2).to_broadcast([P, H, P]),
                                       ALU.subtract).then_inc(shifted, 1)
                if s == 0 and is_seq(n + GS):
                    add_bias(g + 1)
                if s == 3 and is_seq(n - 4):
                    rstd_of_h2(g - 1)

            def front0():
                rstd_of_h(0)
                add_bias(0)
            grouped(pool, front0, slot)

        @block.vector
        def _(dve):
            def split_raw(G):
                rows = a["emb_rows"][:, bass.ts(G, GS), :]
                if not (isinstance(G, int) and G == 0):
                    dve.wait_ge(front_done, before(G - 3, RAW) + 1)
                dve.tensor_scalar(e_hl[:, :, 0:ED], rows, SC_E, None, ALU.mult).then_inc(e_split, 1)
                dve.wait_ge(e_split, G * 2 + 1)
                dve.scalar_tensor_tensor(e_hl[:, :, ED:2 * ED], rows, SC_E, e_hl[:, :, 0:ED],
                                         ALU.mult, ALU.subtract).then_inc(e_split, 1)

            def stats_h(G):
                dve.wait_ge(front_read, before(G - 2, H1) + 1)
                for s in range(GS):
                    last = dve.bn_stats(bn6[:, s, :], h_res[:, s, :])
                last.then_inc(stats1, 1)

            def wait_stats_h(G):
                dve.wait_ge(stats1, G * 2 + 1)
                wait(dve, rstd_step, G * 3)

            def aggr_h(G):
                for s in range(GS):
                    last = dve.bn_aggr(mv1[:, s, :], bn6[:, s, :])
                last.then_inc(stats1, 1)

            def normalise(G):
                dve.wait_ge(rstd_step, G * 3 + 3)
                if not (isinstance(G, int) and G == 0):
                    dve.wait_ge(front_done, before(G - 2, NORMAL_WHOLE) + 1)
                dve.tensor_tensor(x_dup[:, :, :, :],
                                  a["emb_rows"][:, bass.ts(G, GS), :].unsqueeze(2).to_broadcast([P, GS, 2, ED]),
                                  rs1[:, :].unsqueeze(2).unsqueeze(3).to_broadcast([P, GS, 2, ED]),
                                  ALU.mult).then_inc(x_split, 1)
                dve.wait_ge(x_split, G * 3 + 1)
                dve.tensor_copy(x_hl[:, :, 0:ED], x_dup[:, :, 0, :]).then_inc(x_split, 1)
                dve.wait_ge(x_split, G * 3 + 2)
                dve.tensor_tensor(x_hl[:, :, ED:2 * ED], x_dup[:, :, 0, :], x_hl[:, :, 0:ED],
                                  ALU.subtract).then_inc(x_split, 1)

            def slot(g, s, par):
                n = g * GS + s
                b = s % 2
                m = (s + 1) % GS
                if is_seq(n - 3):
                    dve.wait_ge(projected, n - 2)
                    if s == 3:
                        dve.wait_ge(residual, g + 1)
                    dve.scalar_tensor_tensor(h2[:, n - 3, :], ps_y[:, DM:2 * DM], 1.0 / (SC_O * SC_WO), h2[:, n - 3, :],
                                             ALU.mult, ALU.add).then_inc(h2_done, 1)
                if is_seq(n - 2):
                    dve.wait_ge(mixed, n - 1)
                    o_ps = ps_o[:, 0:H * (DV + 1)].rearrange("p (h d) -> p h d", d=DV + 1)
                    dve.reciprocal(inv_sum[:, b, :], o_ps[:, :, DV]).then_inc(inverted, 1)
                if is_seq(n - 3):
                    dve.wait_ge(h2_done, n - 2)
                if is_seq(n - 2):
                    dve.wait_ge(inverted, n - 1)
                    wait(dve, o_turned, n - 3)
                    dve.tensor_tensor(o_s[:, b, :, :], o_ps[:, :, 0:DV],
                                      inv_sum[:, b, :].unsqueeze(2).to_broadcast([P, H, DV]), ALU.mult).then_inc(o_normed, 1)
                if is_seq(n - 3):
                    dve.bn_stats(bn2[:, m, :], h2[:, n - 3, :]).then_inc(stats2, 1)
                if is_seq(n):
                    dve.wait_ge(scores, n + 1)
                    wait(dve, p_turned, n - 1)
                    dve.tensor_tensor(lg[:, b, :, :].rearrange("p (u q) j -> p u (q j)", u=2), ps_s[:, :, :],
                                      a["bias"][:, :, :, :].rearrange("p u q j -> p u (q j)"), ALU.add).then_inc(biased, 1)
                if is_seq(n - 2):
                    dve.wait_ge(o_high, n - 1)
                    dve.scalar_tensor_tensor(oT_hl[:, b, 1, :], ps_y[:, 0:DM], SC_O, oT_hl[:, b, 0, :],
                                             ALU.mult, ALU.subtract).then_inc(o_low, 1)
                if is_seq(n):
                    dve.wait_ge(biased, n + 1)
                    dve.tensor_reduce(row_max[:, b, :], lg[:, b, :, :], AX_X, ALU.max).then_inc(maxed, 1)
                if s == 0 and is_seq(n + GS):
                    normalise(g + 1)
                    if is_seq(n + 2 * GS):
                        split_raw(g + 2)
                if s == 3 and is_seq(n + 2 * GS):
                    stats_h(g + 2)
                    wait_stats_h(g + 2)
                if is_seq(n - 3):
                    dve.wait_ge(stats2, n - 2)
                if is_seq(n - 5):
                    dve.wait_ge(dev_done, n - 4)
                    dve.tensor_reduce(dm4[:, (s + 3) % GS:(s + 3) % GS + 1], dev[:, (s + 1) % 2, :], AX_X, ALU.max,
                                      apply_absolute_value=True).then_inc(dev_maxed, 1)
                if s == 3 and is_seq(n + 2 * GS):
                    aggr_h(g + 2)
                if is_seq(n - 3):
                    dve.bn_aggr(mv2[:, m, :], bn2[:, m, :]).then_inc(aggr2, 1)
                if is_seq(n - 5) and s == 0:
                    dve.wait_ge(dev_maxed, n - 4)
                    dve.tensor_copy(t["dev_max"][:, bass.ts(g - 2, GS)], dm4[:, :]).then_inc(dev_moved, 1)
                if is_seq(n - 3) and s == 2:
                    dve.wait_ge(aggr2, n - 2)
                    dve.tensor_copy(t["mean_var"][:, bass.ts(g - 1, GS), :], mv2[:, :, :]).then_inc(mv_moved, 1)

            def front0():
                for G in (0, 1):
                    split_raw(G)
                    stats_h(G)
                    wait_stats_h(G)
                    aggr_h(G)
                    if G == 0:
                        normalise(0)
            grouped(dve, front0, slot)


def feed_forward(nc, t, h2, out):
    with ExitStack() as ctx:
        c = {}
        for name in ("s_x", "k_x", "s_gate", "s_up", "k_gate", "k_up", "s_p", "k_p", "k_o", "s_y"):
            c[name] = ctx.enter_context(nc.sbuf_tensor(name, [P, 1], F32))[:, :]
        h2_d = nc.dram_tensor("h2_scratch", [P, NSEQ * DM], F32, kind="Internal").ap()
        qu_d = nc.dram_tensor("qu_scratch", [P, NG * NCH * CW], I16, kind="Internal").ap()
        amax = ctx.enter_context(nc.sbuf_tensor("amax", [P, 4], F32))
        acc = ctx.enter_context(nc.sbuf_tensor("acc", [P, 2], F32))
        acc2 = ctx.enter_context(nc.sbuf_tensor("acc2", [P, 2], F32))
        a_tok = ctx.enter_context(nc.sbuf_tensor("a_tok", [P, NSEQ], F32))
        with ExitStack() as inner:
            xq = inner.enter_context(nc.sbuf_tensor("xq_hl", [P, 2, DT, NSEQ * P], F16))
            input_scale(nc, t, c, a_tok)
            pass_max(nc, t, c, h2, a_tok, xq, amax, h2_d)
            gate_up_scales(nc, c, amax)
            pass_gate(nc, t, c, xq, acc)
            product_scale(nc, c, acc, "s_gate", None, 1.0 / 65536.0, "s_p", "k_p")
            pass_up(nc, t, c, xq, acc2, qu_d)
            product_scale(nc, c, acc2, "s_p", "s_up", 1.0, "s_y", "k_o", SC_W)
        pass_down(nc, t, c, h2_d, qu_d, out)


def input_scale(nc, t, c, a_tok):
    with ExitStack() as ctx:
        def sb(name, shape):
            return ctx.enter_context(nc.sbuf_tensor(name, shape, F32))
        tok = sb("x_tok", [P, NSEQ])
        rstd = t["rstd"]
        mx, gx = sb("x_mx", [P, 1]), sb("x_gx", [P, 1])
        step = ctx.enter_context(nc.semaphore("x_step"))
        reduced = ctx.enter_context(nc.semaphore("x_reduced"))
        block = ctx.enter_context(nc.Block())

        @block.gpsimd
        def _(pool):
            pool.wait_ge(step, 2)
            pool.partition_all_reduce(gx[:, :], mx[:, :], P, RMAX).then_inc(reduced, 1)

        @block.vector
        def _(dve):
            dve.tensor_tensor(tok[:, :], t["dev_max"][:, :], rstd[:, :], ALU.mult).then_inc(step, 1)
            dve.wait_ge(step, 1)
            dve.tensor_reduce(mx[:, :], tok[:, :], AX_X, ALU.max).then_inc(step, 1)
            dve.wait_ge(reduced, 1)
            dve.tensor_scalar(c["s_x"], gx[:, :], 1.0 / QMAX, TINY, ALU.mult, ALU.max).then_inc(step, 1)
            dve.wait_ge(step, 3)
            dve.reciprocal(c["k_x"], c["s_x"]).then_inc(step, 1)
            dve.wait_ge(step, 4)
            dve.tensor_scalar(a_tok[:, :], rstd[:, :], c["k_x"], None, ALU.mult).then_inc(step, 1)


def gate_up_scales(nc, c, amax):
    with ExitStack() as ctx:
        mx = ctx.enter_context(nc.sbuf_tensor("ug_mx", [P, 2], F32))
        gx = ctx.enter_context(nc.sbuf_tensor("ug_gx", [P, 2], F32))
        sx = ctx.enter_context(nc.sbuf_tensor("ug_sx", [P, 1], F32))
        inv = ctx.enter_context(nc.sbuf_tensor("ug_inv", [P, 2], F32))
        step = ctx.enter_context(nc.semaphore("ug_step"))
        reduced = ctx.enter_context(nc.semaphore("ug_reduced"))
        block = ctx.enter_context(nc.Block())

        @block.gpsimd
        def _(pool):
            pool.wait_ge(step, 2)
            pool.partition_all_reduce(gx[:, :], mx[:, :], P, RMAX).then_inc(reduced, 1)

        @block.vector
        def _(dve):
            dve.tensor_scalar(sx[:, :], c["s_x"], 1.0 / SC_W, None, ALU.mult).then_inc(step, 1)
            dve.tensor_reduce(mx[:, :], amax[:, :].rearrange("p (w c) -> p w c", w=2), AX_X, ALU.max).then_inc(step, 1)
            dve.wait_ge(reduced, 1)
            dve.wait_ge(step, 2)
            for i, s in enumerate(("s_up", "s_gate")):
                dve.tensor_scalar(c[s], gx[:, i:i + 1], sx[:, :], 1.0 / QMAX, ALU.mult, ALU.mult).then_inc(step, 1)
            dve.wait_ge(step, 4)
            for i, s in enumerate(("s_up", "s_gate")):
                dve.tensor_scalar(c[s], c[s], TINY, None, ALU.max).then_inc(step, 1)
            dve.wait_ge(step, 6)
            for i, s in enumerate(("s_up", "s_gate")):
                dve.reciprocal(inv[:, i:i + 1], c[s]).then_inc(step, 1)
            dve.wait_ge(step, 8)
            for i, k in enumerate(("k_up", "k_gate")):
                dve.tensor_scalar(c[k], inv[:, i:i + 1], sx[:, :], None, ALU.mult).then_inc(step, 1)


def product_scale(nc, c, acc, sa, sb_, factor, s_out, k_out, divide=1.0):
    with ExitStack() as ctx:
        names = ("gx", "unit", "sc", "inv")
        gx, unit, sc, inv = (ctx.enter_context(nc.sbuf_tensor(f"{s_out}_{n}", [P, 1], F32))[:, :] for n in names)
        step = ctx.enter_context(nc.semaphore(f"{s_out}_step"))
        reduced = ctx.enter_context(nc.semaphore(f"{s_out}_reduced"))
        block = ctx.enter_context(nc.Block())

        @block.gpsimd
        def _(pool):
            pool.partition_all_reduce(gx, acc[:, 1:2], P, RMAX).then_inc(reduced, 1)

        @block.vector
        def _(dve):
            if sb_ is None:
                dve.tensor_scalar(unit, c[sa], factor, None, ALU.mult).then_inc(step, 1)
            else:
                dve.tensor_scalar(unit, c[sa], c[sb_], None, ALU.mult).then_inc(step, 1)
            dve.wait_ge(step, 1)
            dve.wait_ge(reduced, 1)
            dve.tensor_scalar(sc, gx, unit, 1.0 / QMAX, ALU.mult, ALU.mult).then_inc(step, 1)
            dve.wait_ge(step, 2)
            dve.tensor_scalar(sc, sc, TINY, None, ALU.max).then_inc(step, 1)
            dve.wait_ge(step, 3)
            dve.reciprocal(inv, sc).then_inc(step, 1)
            dve.tensor_scalar(c[s_out], sc, 1.0 / divide, None, ALU.mult).then_inc(step, 1)
            dve.wait_ge(step, 5)
            dve.tensor_scalar(c[k_out], inv, unit, None, ALU.mult).then_inc(step, 1)


def chunk_products(pe, ps, w, ch, xq, tok):
    for f in range(CT):
        cols = slice((ch * CT + f) * P, (ch * CT + f + 1) * P)
        terms = [(k, wh, xh) for k in range(DT) for wh, xh in ((0, 0), (0, 1), (1, 0))]
        for i, (k, wh, xh) in enumerate(terms):
            last = pe.matmul(ps[:, f, :], w[:, wh, k, cols], xq[:, xh, k, tok], start=i == 0, stop=i == len(terms) - 1)
    return last


def pass_max(nc, t, c, h2, a_tok, xq, amax, h2_d):
    with ExitStack() as ctx:
        def sb(name, shape, dt):
            return ctx.enter_context(nc.sbuf_tensor(name, shape, dt))

        def sem(name):
            return ctx.enter_context(nc.semaphore(name))
        y = sb("y_norm", [P, GS, DM], F32)
        xi = sb("x_int", [P, DT, GT], I16)
        amax_g = sb("amax_g", [P, 4], F32)
        ps_x = ctx.enter_context(nc.psum_tensor("ps_x", [P, DT, 512], F32))
        ps_c = [ctx.enter_context(nc.psum_tensor(f"ps_c{i}", [P, CT, 512], F32)) for i in range(2)]
        scaled = sem("scaled")
        x_turned = sem("x_turned")
        rounded = sem("rounded")
        x_split = sem("xq_split")
        products = sem("products")
        chunk_max = sem("chunk_max")
        running = sem("running")
        saved = sem("h2_saved")
        block = ctx.enter_context(nc.Block())

        def groups(eng, group):
            group(0, True)
            with eng.Fori(1, NG - 1) as g:
                group(g, True)
            group(NG - 1, False)

        @block.sync
        def _(sp):
            flat = h2.rearrange("p n f -> p (n f)")
            for q in range(4):
                part = slice(q * NSEQ * DM // 4, (q + 1) * NSEQ * DM // 4)
                sp.dma_start(h2_d[:, part], flat[:, part]).then_inc(saved, 16)
            sp.wait_ge(saved, 64)

        @block.tensor
        def _(pe):
            def turn(g):
                pe.wait_ge(scaled, g + 1)
                wait(pe, rounded, g)
                for s in range(GS):
                    for k in range(DT):
                        last = pe.transpose(ps_x[:, k, s * P:(s + 1) * P], y[:, s, k * P:(k + 1) * P], t["ident32"][:, :])
                last.then_inc(x_turned, 1)

            def group(g, more):
                pe.wait_ge(x_split, g * 2 + 2)
                for m in range(4):
                    if m == 2 and more:
                        turn(g + 1)
                    wait(pe, chunk_max, g * 4 + m - 1)
                    w = (t["wup"], t["wgate"])[m // 2]
                    chunk_products(pe, ps_c[m % 2], w, m % 2, xq, bass.ts(g, GT)).then_inc(products, 1)
            turn(0)
            groups(pe, group)

        @block.scalar
        def _(act):
            def round_(g):
                act.wait_ge(x_turned, g + 1)
                wait(act, x_split, g * 2)
                act.copy(xi[:, :, :], ps_x[:, :, :]).then_inc(rounded, 1)
            round_(0)
            groups(act, lambda g, more: more and round_(g + 1))

        @block.vector
        def _(dve):
            def scale(g):
                wait(dve, x_turned, g)
                for s in range(GS):
                    n = g * GS + s
                    last = dve.tensor_scalar(y[:, s, :], h2[:, n, :], t["mean_var"][:, n, 0:1], a_tok[:, bass.ts(n, 1)],
                                             ALU.subtract, ALU.mult)
                last.then_inc(scaled, 1)

            def split(g):
                tok = bass.ts(g, GT)
                dve.wait_ge(rounded, g + 1)
                dve.tensor_copy(xq[:, 0, :, tok], xi[:, :, :]).then_inc(x_split, 1)
                dve.wait_ge(x_split, g * 2 + 1)
                dve.tensor_tensor(xq[:, 1, :, tok], xi[:, :, :], xq[:, 0, :, tok], ALU.subtract).then_inc(x_split, 1)

            def group(g, more):
                if more:
                    scale(g + 1)
                for m in range(4):
                    if m == 0:
                        dve.wait_ge(running, g + 1)
                    dve.wait_ge(products, g * 4 + m + 1)
                    dve.tensor_reduce(amax_g[:, m:m + 1], ps_c[m % 2][:, :, :].rearrange("p f n -> p (f n)"), AX_X, ALU.max,
                                      apply_absolute_value=True).then_inc(chunk_max, 1)
                    if m == 1 and more:
                        split(g + 1)
                dve.wait_ge(chunk_max, g * 4 + 4)
                dve.tensor_tensor(amax[:, :], amax[:, :], amax_g[:, :], ALU.max).then_inc(running, 1)

            dve.memset(amax[:, :], 0.0).then_inc(running, 1)
            dve.wait_ge(running, 1)
            scale(0)
            split(0)
            groups(dve, group)


def pass_gate(nc, t, c, xq, acc):
    with ExitStack() as ctx:
        def sb(name, shape, dt):
            return ctx.enter_context(nc.sbuf_tensor(name, shape, dt))

        def sem(name):
            return ctx.enter_context(nc.semaphore(name))
        sig = sb("sig", [P, 2, CW], F32)
        qs = sb("qs", [P, 2, CW], U16)
        neg = sb("neg", [P, CW], I16)
        mag = sb("mag", [P, 2, CW], I16)
        ps_c = [ctx.enter_context(nc.psum_tensor(f"ps_g{i}", [P, CT, 512], F32)) for i in range(2)]
        products = sem("g_products")
        quantised = sem("g_quantised")
        sigged = sem("g_sigged")
        sig_q = sem("g_sig_q")
        negated = sem("g_negated")
        waited = sem("g_waited")
        magged = sem("g_magged")
        maxed = sem("g_maxed")
        block = ctx.enter_context(nc.Block())
        big = t["big"]

        def groups(eng, group):
            group(0)
            with eng.Fori(1, NG) as g:
                group(g)

        @block.tensor
        def _(pe):
            def group(g):
                for ch in range(NCH):
                    wait(pe, quantised, g * NCH + ch - 1)
                    chunk_products(pe, ps_c[ch], t["wgate"], ch, xq, bass.ts(g, GT)).then_inc(products, 1)
            groups(pe, group)

        @block.scalar
        def _(act):
            def quantise(m, ch):
                act.wait_ge(products, m + 1)
                act.mul(big[:, bass.ts(m, CW)], ps_c[ch][:, :, :].rearrange("p f n -> p (f n)"),
                        c["k_gate"]).then_inc(quantised, 1)

            def group(g, last=False):
                for ch in range(NCH):
                    m = g * NCH + ch
                    wait(act, sig_q, m - 1)
                    act.wait_ge(quantised, m + 1)
                    if not (last and ch == NCH - 1):
                        quantise(m + 1, 1 - ch)
                    act.activation(sig[:, ch, :], big[:, bass.ts(m, CW)], ACT.Sigmoid, scale=c["s_gate"]).then_inc(sigged, 1)
            quantise(0, 0)
            group(0)
            with act.Fori(1, NG - 1) as g:
                group(g)
            group(NG - 1, True)

        @block.gpsimd
        def _(pool):
            def group(g):
                for ch in range(NCH):
                    m = g * NCH + ch
                    pool.wait_ge(sigged, m + 1)
                    wait(pool, maxed, m - 1)
                    sigmoid_levels(pool, qs[:, ch, :], sig[:, ch, :], waited).then_inc(sig_q, 1)
            groups(pool, group)

        @block.vector
        def _(dve):
            def magnitude(m, ch):
                chunk = big[:, bass.ts(m, CW)]
                dve.wait_ge(quantised, m + 1)
                wait(dve, magged, m)
                dve.tensor_scalar(neg[:, :], chunk, -1.0, None, ALU.mult).then_inc(negated, 1)
                dve.wait_ge(negated, m + 1)
                if not (isinstance(m, int) and m == 0):
                    dve.wait_ge(sig_q, m)
                dve.tensor_tensor(mag[:, ch, :], chunk, neg[:, :], ALU.max).then_inc(magged, 1)

            def reduce(m, ch):
                dve.tensor_tensor_reduce(mag[:, ch, :], mag[:, ch, :], qs[:, ch, :], 1.0,
                                         0.0 if isinstance(m, int) and m == 0 else acc[:, 1 - ch:2 - ch],
                                         ALU.mult, ALU.max, acc[:, ch:ch + 1]).then_inc(maxed, 1)

            def group(g):
                for ch in range(NCH):
                    m = g * NCH + ch
                    magnitude(m, ch)
                    if not (isinstance(m, int) and m == 0):
                        reduce(m - 1, 1 - ch)
            groups(dve, group)
            dve.wait_ge(sig_q, NG * NCH)
            dve.wait_ge(magged, NG * NCH)
            dve.wait_ge(maxed, NG * NCH - 1)
            reduce(NG * NCH - 1, 1)


def sigmoid_levels(pool, out, sig, waited):
    pool.sem_inc(waited, 1)
    return pool.tensor_scalar(out, sig, 65536.0, 1.0, ALU.mult, ALU.mult)


def pass_up(nc, t, c, xq, acc, qu_d):
    with ExitStack() as ctx:
        def sb(name, shape, dt):
            return ctx.enter_context(nc.sbuf_tensor(name, shape, dt))

        def sem(name):
            return ctx.enter_context(nc.semaphore(name))
        sig = sb("u_sig", [P, CW], F32)
        qs = sb("u_qs", [P, 2, CW], U16)
        qu = sb("u_qu", [P, 2, CW], I16)
        mag_g = sb("u_mag_g", [P, CW], I16)
        mag_u = sb("u_mag_u", [P, 2, CW], I16)
        ps_c = [ctx.enter_context(nc.psum_tensor(f"ps_u{i}", [P, CT, 512], F32)) for i in range(2)]
        products = sem("u_products")
        quantised = sem("u_quantised")
        sigged = sem("u_sigged")
        sig_q = sem("u_sig_q")
        mag_up = sem("u_mag_up")
        negated = sem("u_negated")
        waited = sem("u_waited")
        gated = sem("u_gated")
        magged = sem("u_magged")
        maxed = sem("u_maxed")
        saved = [sem(f"u_saved{i}") for i in range(2)]
        block = ctx.enter_context(nc.Block())
        big = t["big"]

        def groups(eng, group):
            group(0)
            with eng.Fori(1, NG) as g:
                group(g)

        @block.sync
        def _(sp):
            def group(g):
                for ch in range(NCH):
                    m = g * NCH + ch
                    sp.wait_ge(quantised, m + 1)
                    sp.dma_start(qu_d[:, bass.ts(m, CW)], qu[:, ch, :]).then_inc(saved[ch], 16)
            groups(sp, group)
            for s in saved:
                sp.wait_ge(s, 16 * NG)

        @block.tensor
        def _(pe):
            def group(g):
                for ch in range(NCH):
                    wait(pe, quantised, g * NCH + ch - 1)
                    chunk_products(pe, ps_c[ch], t["wup"], ch, xq, bass.ts(g, GT)).then_inc(products, 1)
            groups(pe, group)

        @block.scalar
        def _(act):
            def sigmoid(m):
                wait(act, sig_q, m)
                act.activation(sig[:, :], big[:, bass.ts(m, CW)], ACT.Sigmoid, scale=c["s_gate"]).then_inc(sigged, 1)

            def group(g):
                for ch in range(NCH):
                    m = g * NCH + ch
                    ps = ps_c[ch][:, :, :].rearrange("p f n -> p (f n)")
                    sigmoid(m)
                    act.wait_ge(products, m + 1)
                    wait(act, maxed, m - 1)
                    act.activation(mag_u[:, ch, :], ps, ACT.Abs, scale=c["k_up"]).then_inc(mag_up, 1)
                    wait(act, saved[ch], g * 16)
                    act.mul(qu[:, ch, :], ps, c["k_up"]).then_inc(quantised, 1)
            groups(act, group)

        @block.gpsimd
        def _(pool):
            def group(g):
                for ch in range(NCH):
                    m = g * NCH + ch
                    pool.wait_ge(sigged, m + 1)
                    wait(pool, gated, m - 1)
                    sigmoid_levels(pool, qs[:, ch, :], sig[:, :], waited).then_inc(sig_q, 1)
            groups(pool, group)

        @block.vector
        def _(dve):
            def reduce(m, ch):
                dve.tensor_tensor_reduce(mag_u[:, ch, :], mag_g[:, :], mag_u[:, ch, :], 1.0,
                                         0.0 if isinstance(m, int) and m == 0 else acc[:, 1 - ch:2 - ch],
                                         ALU.mult, ALU.max, acc[:, ch:ch + 1]).then_inc(maxed, 1)

            def group(g):
                for ch in range(NCH):
                    m = g * NCH + ch
                    chunk = big[:, bass.ts(m, CW)]
                    wait(dve, magged, m)
                    wait(dve, mag_up, m)
                    dve.wait_ge(sig_q, m + 1)
                    dve.scalar_tensor_tensor(chunk, chunk, c["k_p"], qs[:, ch, :], ALU.mult, ALU.mult).then_inc(gated, 1)
                    if not (isinstance(m, int) and m == 0):
                        reduce(m - 1, 1 - ch)
                    dve.wait_ge(gated, m + 1)
                    wait(dve, maxed, m)
                    dve.tensor_scalar(mag_g[:, :], chunk, -1.0, None, ALU.mult).then_inc(negated, 1)
                    dve.wait_ge(negated, m + 1)
                    dve.tensor_tensor(mag_g[:, :], chunk, mag_g[:, :], ALU.max).then_inc(magged, 1)
            groups(dve, group)
            dve.wait_ge(magged, NG * NCH)
            dve.wait_ge(mag_up, NG * NCH)
            dve.wait_ge(maxed, NG * NCH - 1)
            reduce(NG * NCH - 1, 1)


def pass_down(nc, t, c, h2_d, qu_d, out):
    with ExitStack() as ctx:
        def sb(name, shape, dt):
            return ctx.enter_context(nc.sbuf_tensor(name, shape, dt))

        def sem(name):
            return ctx.enter_context(nc.semaphore(name))
        NB = 4
        qu = sb("d_qu", [P, NB, NCH * CW], I16)
        res = sb("d_res", [P, NB, GS * DM], F32)
        qo = sb("d_qo", [P, 2, CW], I16)
        o_hl = sb("d_o_hl", [P, 2, 2, CW * NCH], F16)
        y = sb("d_y", [P, NB, GS * DM], F32)
        ps_d = [ctx.enter_context(nc.psum_tensor(f"ps_d{i}", [P, 2, 512], F32)) for i in range(2)]
        loaded = [sem(f"d_loaded{i}") for i in range(NB)]
        levels = sem("d_levels")
        o_high = sem("d_high")
        o_low = sem("d_low")
        products = sem("d_products")
        added = sem("d_added")
        stored = [sem(f"d_stored{i}") for i in range(NB)]
        block = ctx.enter_context(nc.Block())
        big = t["big"]
        out_v = out.rearrange("n p f -> p n f")

        def rounds(eng, group):
            for g in range(NB):
                group(g, g, 0)
            with eng.Fori(1, NG // NB) as r:
                for b in range(NB):
                    group(r * NB + b, b, r)

        @block.sync
        def _(sp):
            def load(g, b):
                sp.dma_start(qu[:, b, :], qu_d[:, bass.ts(g, NCH * CW)]).then_inc(loaded[b], 16)
                sp.dma_start(res[:, b, :], h2_d[:, bass.ts(g, GS * DM)]).then_inc(loaded[b], 16)

            def store(g, b):
                sp.wait_ge(added, g + 1)
                sp.dma_start(out_v[:, bass.ts(g, GS), :], y[:, b, :].rearrange("p (s f) -> p s f", f=DM)).then_inc(stored[b], 16)
            for b in range(NB):
                load(b, b)
            with sp.Fori(0, NG // NB - 1) as r:
                for b in range(NB):
                    store(r * NB + b, b)
                    load(r * NB + NB + b, b)
            for b in range(NB):
                store(NG - NB + b, b)
            for s in stored:
                sp.wait_ge(s, 16 * NG // NB)

        @block.vector
        def _(dve):
            def finish(g, b, r):
                dve.wait_ge(products, g + 1)
                wait(dve, stored[b], r * 16)
                dve.scalar_tensor_tensor(y[:, b, :], ps_d[b % 2][:, :, :].rearrange("p b n -> p (b n)"), c["s_y"],
                                         res[:, b, :], ALU.mult, ALU.add).then_inc(added, 1)

            def quantise(g, b, r):
                dve.wait_ge(loaded[b], r * 32 + 32)
                wait(dve, o_low, g * NCH)
                for ch in range(NCH):
                    dve.scalar_tensor_tensor(qo[:, ch, :], big[:, bass.ts(g * NCH + ch, CW)], c["k_o"],
                                             qu[:, b, ch * CW:(ch + 1) * CW], ALU.mult, ALU.mult).then_inc(levels, 1)

            def split(g, b):
                for ch in range(NCH):
                    cols = slice(ch * CW, (ch + 1) * CW)
                    dve.wait_ge(o_high, g * NCH + ch + 1)
                    dve.tensor_tensor(o_hl[:, b % 2, 1, cols], qo[:, ch, :], o_hl[:, b % 2, 0, cols], ALU.subtract).then_inc(o_low, 1)

            def group(g, b, r):
                quantise(g, b, r)
                split(g, b)
                if not (isinstance(g, int) and g == 0):
                    finish(g - 1, (b - 1) % NB, r if b else r - 1)

            for g in range(NB + 1):
                group(g, g % NB, g // NB)
            with dve.Fori(1, NG // NB - 1) as r:
                for b in range(1, NB + 1):
                    group(r * NB + b, b % NB, r if b < NB else r + 1)
            for g in range(NG - NB + 1, NG):
                group(g, g % NB, g // NB)
            finish(NG - 1, NB - 1, NG // NB - 1)

        @block.scalar
        def _(act):
            def group(g, b, r):
                wait(act, products, g - 1)
                for ch in range(NCH):
                    act.wait_ge(levels, g * NCH + ch + 1)
                    act.copy(o_hl[:, b % 2, 0, ch * CW:(ch + 1) * CW], qo[:, ch, :]).then_inc(o_high, 1)
            rounds(act, group)

        @block.tensor
        def _(pe):
            def group(g, b, r):
                pe.wait_ge(o_low, g * NCH + NCH)
                wait(pe, added, g - 1)
                terms = [(k, xh, wh) for k in range(FT) for xh, wh in ((0, 0), (1, 0), (0, 1))]
                for s in range(GS):
                    for i, (k, xh, wh) in enumerate(terms):
                        last = pe.matmul(ps_d[b % 2][:, s // 2, s % 2 * DM:(s % 2 + 1) * DM],
                                         o_hl[:, b % 2, xh, k * GT + s * P:k * GT + (s + 1) * P], t["wdown"][:, wh, k, :],
                                         start=i == 0, stop=i == len(terms) - 1)
                last.then_inc(products, 1)
            rounds(pe, group)


_INS = ["x", "L0_tok_emb_weight", "L0_tok_proj_weight", "L0_tok_scale", "L0_attn_W_qk", "L0_attn_W_v",
        "L0_attn_W_out", "L0_attn_b_out", "L0_attn_conv", "L0_ffn_w_gate", "L0_ffn_w_up", "L0_ffn_w_down"]


def kernel(**inputs):
    import numpy as _np
    import concourse.bacc as _bacc
    from concourse import mybir as _mybir
    from concourse.bass_utils import run_bass_kernel_spmd as _run

    nc = _bacc.Bacc("TRN2", target_bir_lowering=False, num_devices=1)
    arrays, args = {}, []
    for name in _INS:
        v = _np.ascontiguousarray(inputs[name])
        if v.ndim == 0:
            v = v.reshape(1)
        arrays[f"in_{name}"] = v
        args.append(nc.dram_tensor(f"in_{name}", v.shape, _mybir.dt.from_np(v.dtype), kind="ExternalInput").ap())
    out = nc.dram_tensor("out_h", (NSEQ, P, DM), F32, kind="ExternalOutput").ap()
    build(nc, *args, out)
    r = _run(nc, [arrays], core_ids=[0])
    return r.results[0]["out_h"]
```

```python
from contextlib import ExitStack

import concourse.bass as bass
from concourse import mybir

ALU = mybir.AluOpType
ACT = mybir.ActivationFunctionType
F32 = mybir.dt.float32
F16 = mybir.dt.float16
I32 = mybir.dt.int32
U32 = mybir.dt.uint32
I16 = mybir.dt.int16
U16 = mybir.dt.uint16
AX_X = mybir.AxisListType.X
RMAX = bass.bass_isa.ReduceOp.max

P = 128
NSEQ = 64
GS = 4
NG = NSEQ // GS
GT = GS * P
VOC = 262144
ED = 64
DM = 256
DT = DM // P
H = 8
HP = H // 2
DV = DM // H
MAXPOS = 10
FF = 768
FT = FF // P
CT = 3
NCH = FT // CT
NB = 4
CW = CT * GT
WBLK = 32
EPS = 1e-5
QMAX = 32767.0
TINY = 1e-12
HASH_A, HASH_B = 36313, 27191
HASH_BITS = 18

SC_E = 2.0 ** 10
SC_P = 2.0 ** 10
SC_X = 2.0 ** 6
SC_G = 2.0 ** 6
SC_V = 2.0 ** 10
SC_O = 2.0 ** 8
SC_WO = 2.0 ** 8
SC_W = 2.0 ** 10
QK_SCALE = 64.0 ** -0.5


def build(nc, x, emb, proj, scale, w_qk, w_v, w_out, b_out, conv, w_gate, w_up, w_down, out):
    with ExitStack() as keep:
        def sb(name, shape, dt):
            return keep.enter_context(nc.sbuf_tensor(name, shape, dt))

        t = {}
        t["ident32"] = sb("ident32", [P, P], F32)
        t["wup"] = sb("wup_hl", [P, 2, DT, FF], F16)
        t["wgate"] = sb("wgate_hl", [P, 2, DT, FF], F16)
        t["wdown"] = sb("wdown_hl", [P, 2, FT, DM], F16)
        t["big"] = sb("big", [P, NG * NCH * CW], I16)
        t["mean_var"] = sb("mean_var", [P, NSEQ, 2], F32)
        t["rstd"] = sb("rstd2", [P, NSEQ], F32)
        t["dev_max"] = sb("dev_max", [P, NSEQ], F32)
        h2 = t["big"][:, 0:NSEQ * DM * 2].bitcast(F32).rearrange("p (n f) -> p n f", f=DM)
        with ExitStack() as attn:
            def sba(name, shape, dt):
                return attn.enter_context(nc.sbuf_tensor(name, shape, dt))
            a = {}
            a["ident16"] = sba("ident16", [P, P], F16)
            a["rows"] = sba("rows", [P, NSEQ], U32)
            a["emb_rows"] = sba("emb_rows", [P, 2, GS, ED], F32)
            a["pt"] = sba("pt_hl", [P, 2, DM], F16)
            a["g"] = sba("g_hl", [P, 2, HP, P], F16)
            a["mv"] = sba("mv_hl", [P, 2, DM], F16)
            a["wo"] = sba("wo_hl", [P, 2, DT, DM], F16)
            a["bias"] = sba("pos_bias", [P, 2, HP, P], F32)
            a["bout"] = sba("bout_row", [P, DM], F32)
            a["h_scale"] = sba("h_scale", [P, 1], F32)
            a["x_scale"] = sba("x_scale", [P, 1], F32)
            a["minus_half"] = sba("minus_half", [P, GS], F32)
            a["eps"] = sba("eps", [P, GS], F32)
            W = FF * DM // P
            free = t["big"][:, NSEQ * DM * 2:]
            a["raw"] = [free[:, 2 * i * W:2 * (i + 1) * W].bitcast(F32) for i in range(3)]
            a["levels"] = free[:, 6 * W:7 * W]
            a["steps"] = sba("steps", [P, 3, FF * DM // P // WBLK], F32)
            a["inv_steps"] = sba("inv_steps", [P, 3, FF * DM // P // WBLK], F32)
            a["quant"] = attn.enter_context(nc.semaphore("quant"))
            prepare(nc, t, a, x, emb, proj, scale, w_qk, w_v, w_out, b_out, conv, w_gate, w_up, w_down)
            attention(nc, t, a, emb, h2)
        feed_forward(nc, t, h2, out)


def prepare(nc, t, a, x, emb, proj, scale, w_qk, w_v, w_out, b_out, conv, w_gate, w_up, w_down):
    with ExitStack() as ctx:
        def sb(name, shape, dt):
            return ctx.enter_context(nc.sbuf_tensor(name, shape, dt))

        def sem(name):
            return ctx.enter_context(nc.semaphore(name))

        ids = sb("ids", [NSEQ, P], I32)
        mul_a = sb("mul_a", [NSEQ, P], I32)
        mul_b = sb("mul_b", [NSEQ, P], I32)
        prod_a = sb("prod_a", [NSEQ, P], I32)
        prod_b = sb("prod_b", [NSEQ, P], I32)
        mixed = sb("mixed", [NSEQ, P], I32)
        low_bits = sb("low_bits", [NSEQ, P], I32)
        high_bits = sb("high_bits", [NSEQ, P], I32)
        bucket = sb("bucket", [NSEQ, P], F32)
        wrap = sb("wrap", [NSEQ, P], F32)
        rows = a["rows"]
        p_nat = sb("p_nat", [P, DT, ED], F32)
        p_dup = sb("p_dup", [P, DT, 2, ED], F32)
        pc_dup = sb("pc_dup", [P, DT, 2, ED], F32)
        ones = sb("mean_ones", [P, P], F32)
        wqk_s = sb("wqk_s", [P, DT, 2 * H * ED], F32)
        wv_s = sb("wv_s", [P, DT, DM], F32)
        wo_s = sb("wo_s", [P, DT, DM], F32)
        mq = sb("mq", [P, HP, 2, ED], F32)
        mk = sb("mk", [P, HP, ED], F32)
        conv_s = sb("conv_s", [P, H, 2 * MAXPOS + 1], F32)
        window = sb("window", [P, H, 2 * P], F32)
        scale_s = sb("scale_s", [P, 1], F32)
        raw = a["raw"]
        window_d = nc.dram_tensor("window_scratch", [P, 2 * P * H], F32, kind="Internal").ap()

        ps_a = ctx.enter_context(nc.psum_tensor("ps_a", [P, 512], F32))
        ps_b = ctx.enter_context(nc.psum_tensor("ps_b", [P, 512], F32))
        ps_m = ctx.enter_context(nc.psum_tensor("ps_m", [P, ED], F32))
        ps_ge = ctx.enter_context(nc.psum_tensor("ps_ge", [P, 512], F32))
        ps_go = ctx.enter_context(nc.psum_tensor("ps_go", [P, 512], F32))
        ps_w = ctx.enter_context(nc.psum_tensor("ps_w", [P, 2, 512], F32))

        ids_in = sem("ids_in")
        p_in = sem("p_in")
        attn_in = sem("attn_in")
        small_in = sem("small_in")
        ffw_in = [sem(f"ffw_in{i}") for i in range(3)]
        consts = sem("consts")
        prods = sem("prods")
        hashing = sem("hashing")
        hash_turned = sem("hash_turned")
        rows_ready = sem("rows_ready")
        gathered = sem("gathered")
        windowed = sem("windowed")
        window_out = sem("window_out")
        bias_in = sem("bias_in")
        fold = sem("fold")
        pe_fold = sem("pe_fold")
        act_fold = sem("act_fold")

        block = ctx.enter_context(nc.Block())

        @block.sync
        def _(sp):
            sp.dma_start(ids[:, :], x).then_inc(ids_in, 16)
            sp.dma_start(p_nat[:, :, :], proj.rearrange("(t p) d -> p t d", p=P)).then_inc(p_in, 16)
            sp.dma_start(wqk_s[:, :, :], w_qk.rearrange("(t p) n -> p t n", p=P)).then_inc(attn_in, 16)
            sp.dma_start(wv_s[:, :, :], w_v.rearrange("(t p) n -> p t n", p=P)).then_inc(attn_in, 16)
            sp.dma_start(wo_s[:, :, :], w_out.rearrange("(t p) n -> p t n", p=P)).then_inc(attn_in, 16)
            for i, (w, tiles) in enumerate(((w_up, FT), (w_gate, FT), (w_down, DT))):
                sp.dma_start(raw[i][:, :].rearrange("p (t n) -> p t n", t=tiles),
                             w.rearrange("(t p) n -> p t n", p=P)).then_inc(ffw_in[i], 16)
            sp.wait_ge(windowed, 3)
            sp.dma_start(window_d, window[:, :, :].rearrange("p h m -> p (h m)")).then_inc(window_out, 16)
            sp.wait_ge(window_out, 16)
            pitch = 2 * P * H - 1
            skewed = window_d.rearrange("p m -> (p m)")[P - 1:P - 1 + P * pitch].rearrange("(i m) -> i m", m=pitch)
            for parity in range(2):
                for pair in range(HP):
                    h = 2 * pair + parity
                    sp.dma_start(a["bias"][:, parity, pair, :],
                                 skewed[:, h * 2 * P:h * 2 * P + P]).then_inc(bias_in, 16)
            sp.wait_ge(bias_in, 16 * H)
            sp.wait_ge(ffw_in[1], 16)
            sp.wait_ge(ffw_in[2], 16)

        @block.gpsimd
        def _(pool):
            pool.memset(a["minus_half"][:, :], -0.5).then_inc(consts, 1)
            pool.memset(a["eps"][:, :], EPS).then_inc(consts, 1)
            pool.iota(mul_a[:, :], pattern=[[0, P]], base=HASH_A, channel_multiplier=0).then_inc(consts, 1)
            pool.iota(mul_b[:, :], pattern=[[0, P]], base=HASH_B, channel_multiplier=0).then_inc(consts, 1)
            pool.memset(t["ident32"][:, :], 0.0).then_inc(consts, 1)
            pool.memset(a["ident16"][:, :], 0.0).then_inc(consts, 1)
            pool.memset(ones[:, :], 1.0 / DM).then_inc(consts, 1)
            pool.wait_ge(ids_in, 16)
            pool.wait_ge(consts, 7)
            pool.tensor_tensor(prod_a[:, :], ids[:, :], mul_a[:, :], ALU.mult).then_inc(prods, 1)
            pool.tensor_tensor(prod_b[:, :], ids[:, :], mul_b[:, :], ALU.mult).then_inc(prods, 1)
            for m in (t["ident32"], a["ident16"]):
                pool.affine_select(out=m[:, :], in_=m[:, :], compare_op=ALU.not_equal, fill=1.0,
                                   base=0, pattern=[[-1, P]], channel_multiplier=1).then_inc(consts, 1)
            pool.wait_ge(rows_ready, 1)
            for n in range(2 * GS):
                pool.indirect_dma_start(a["emb_rows"][:, n // GS, n % GS, :], None, emb,
                                        bass.IndirectOffsetOnAxis(ap=rows[:, n:n + 1], axis=0)).then_inc(gathered, 16)
            pool.wait_ge(gathered, 16 * 2 * GS)

        @block.scalar
        def _(act):
            act.dma_start(scale_s[:, :], scale.to_broadcast([P, 1])).then_inc(small_in, 16)
            act.dma_start(conv_s[:, :, :].rearrange("p h m -> p (h m)"),
                          conv.rearrange("h m -> (h m)").partition_broadcast(P)).then_inc(small_in, 16)
            act.dma_start(a["bout"][:, :], b_out.partition_broadcast(P)).then_inc(small_in, 16)
            act.wait_ge(small_in, 48)
            act.mul(a["h_scale"][:, :], scale_s[:, :], 1.0 / (SC_E * SC_P)).then_inc(act_fold, 1)
            act.mul(a["x_scale"][:, :], scale_s[:, :], SC_X).then_inc(act_fold, 1)
            edge = P - 1 - MAXPOS
            w = 2 * MAXPOS + 1
            act.copy(window[:, :, 0:edge], conv_s[:, :, 0:1].to_broadcast([P, H, edge])).then_inc(windowed, 1)
            act.copy(window[:, :, edge:edge + w], conv_s[:, :, :]).then_inc(windowed, 1)
            act.copy(window[:, :, edge + w:2 * P],
                     conv_s[:, :, w - 1:w].to_broadcast([P, H, 2 * P - edge - w])).then_inc(windowed, 1)
            act.wait_ge(pe_fold, 2)
            mqk = ps_b[:, :].rearrange("p (c d) -> p c d", d=ED)
            act.copy(mq[:, :, :, :], mqk[:, 0:HP, :].unsqueeze(2).to_broadcast([P, HP, 2, ED])).then_inc(act_fold, 1)
            act.copy(mk[:, :, :], mqk[:, HP:2 * HP, :]).then_inc(act_fold, 1)

        @block.vector
        def _(dve):
            dve.wait_ge(prods, 2)
            dve.tensor_tensor(mixed[:, 1:P], prod_a[:, 1:P], prod_b[:, 0:P - 1], ALU.bitwise_xor).then_inc(hashing, 1)
            dve.memset(mixed[:, 0:1], 0).then_inc(hashing, 1)
            dve.wait_ge(hashing, 2)
            dve.tensor_scalar(low_bits[:, :], mixed[:, :], VOC - 1, None, ALU.bitwise_and).then_inc(hashing, 1)
            dve.tensor_scalar(high_bits[:, :], mixed[:, :], HASH_BITS, None, ALU.arith_shift_right).then_inc(hashing, 1)
            dve.wait_ge(hashing, 4)
            dve.tensor_tensor(bucket[:, :], low_bits[:, :], high_bits[:, :], ALU.add).then_inc(hashing, 1)
            dve.wait_ge(hashing, 5)
            dve.tensor_scalar(wrap[:, :], bucket[:, :], float(VOC - 1), float(VOC - 1), ALU.is_ge, ALU.mult).then_inc(hashing, 1)
            dve.wait_ge(hashing, 6)
            dve.tensor_tensor(bucket[:, :], bucket[:, :], wrap[:, :], ALU.subtract).then_inc(hashing, 1)
            dve.wait_ge(hashing, 7)
            dve.tensor_scalar(wrap[:, :], bucket[:, :], 0.0, float(VOC - 1), ALU.is_lt, ALU.mult).then_inc(hashing, 1)
            dve.wait_ge(hashing, 8)
            dve.tensor_tensor(bucket[:, :], bucket[:, :], wrap[:, :], ALU.add).then_inc(hashing, 1)
            dve.wait_ge(hashing, 9)
            dve.memset(bucket[:, 0:1], float(VOC - 1)).then_inc(hashing, 1)
            dve.wait_ge(hash_turned, 1)
            dve.tensor_copy(rows[:, :], ps_a[:, 0:NSEQ]).then_inc(rows_ready, 1)

            dve.wait_ge(p_in, 16)
            dve.tensor_copy(p_dup[:, :, :, :], p_nat[:, :, :].unsqueeze(2).to_broadcast([P, DT, 2, ED])).then_inc(fold, 1)
            dve.wait_ge(pe_fold, 1)
            dve.tensor_tensor(pc_dup[:, :, :, :], p_nat[:, :, :].unsqueeze(2).to_broadcast([P, DT, 2, ED]),
                              ps_m[:, :].unsqueeze(1).unsqueeze(1).to_broadcast([P, DT, 2, ED]),
                              ALU.subtract).then_inc(fold, 1)
            dve.wait_ge(attn_in, 48)
            dve.tensor_scalar(a["wo"][:, 0, :, :], wo_s[:, :, :], SC_WO, None, ALU.mult).then_inc(fold, 1)
            dve.wait_ge(fold, 3)
            dve.scalar_tensor_tensor(a["wo"][:, 1, :, :], wo_s[:, :, :], SC_WO, a["wo"][:, 0, :, :],
                                     ALU.mult, ALU.subtract).then_inc(fold, 1)
            dve.wait_ge(ffw_in[0], 16)
            for step in quantise(dve, a, 0):
                step()
            dve.wait_ge(pe_fold, 3)
            for hl, parity in ((0, 0), (0, 1)):
                ps = (ps_ge, ps_go)[parity][:, 0:HP * ED].rearrange("p (c d) -> p c d", d=ED)
                dve.tensor_scalar(a["g"][:, 0, :, parity * ED:(parity + 1) * ED], ps,
                                  SC_G * QK_SCALE, None, ALU.mult).then_inc(fold, 1)
            dve.wait_ge(fold, 6)
            for parity in range(2):
                ps = (ps_ge, ps_go)[parity][:, 0:HP * ED].rearrange("p (c d) -> p c d", d=ED)
                cols = slice(parity * ED, (parity + 1) * ED)
                dve.scalar_tensor_tensor(a["g"][:, 1, :, cols], ps, SC_G * QK_SCALE, a["g"][:, 0, :, cols],
                                         ALU.mult, ALU.subtract).then_inc(fold, 1)
            dve.wait_ge(pe_fold, 4)
            for k, (w, ps, sc) in enumerate(((a["mv"], ps_w[:, 0, 0:DM], SC_V), (a["pt"], ps_w[:, 1, 0:DM], SC_P))):
                dve.tensor_scalar(w[:, 0, :], ps, sc, None, ALU.mult).then_inc(fold, 1)
                dve.wait_ge(fold, 9 + 2 * k)
                dve.scalar_tensor_tensor(w[:, 1, :], ps, sc, w[:, 0, :], ALU.mult, ALU.subtract).then_inc(fold, 1)

        @block.tensor
        def _(pe):
            pe.wait_ge(consts, 9)
            pe.wait_ge(hashing, 10)
            pe.transpose(ps_a[:, 0:NSEQ], bucket[:, :], t["ident32"][0:NSEQ, 0:NSEQ]).then_inc(hash_turned, 1)
            pe.wait_ge(p_in, 16)
            for k in range(DT):
                last = pe.matmul(ps_m[:, :], ones[:, :], p_nat[:, k, :], start=k == 0, stop=k == DT - 1)
            last.then_inc(pe_fold, 1)
            pe.wait_ge(attn_in, 48)
            pe.wait_ge(fold, 2)
            for c in range(2 * HP):
                for k in range(DT):
                    last = pe.matmul(ps_b[:, c * ED:(c + 1) * ED], wqk_s[:, k, c * P:(c + 1) * P],
                                     pc_dup[:, k, 0, :], start=k == 0, stop=k == DT - 1)
            last.then_inc(pe_fold, 1)
            pe.wait_ge(act_fold, 4)
            for pair in range(HP):
                for parity in range(2):
                    r = slice(parity * ED, (parity + 1) * ED)
                    last = pe.matmul((ps_ge, ps_go)[parity][:, pair * ED:(pair + 1) * ED],
                                     mq[r, pair, :, :].rearrange("c u d -> c (u d)"), mk[r, pair, :],
                                     start=True, stop=True)
            last.then_inc(pe_fold, 1)
            for k in range(DT):
                pe.matmul(ps_w[:, 0, 0:DM], pc_dup[:, k, :, :].rearrange("p u d -> p (u d)"), wv_s[:, k, :],
                          start=k == 0, stop=k == DT - 1)
            for k in range(DT):
                last = pe.transpose(ps_w[:, 1, k * P:(k + 1) * P], p_dup[:, k, :, :].rearrange("p u d -> p (u d)"),
                                    t["ident32"][:, :])
            last.then_inc(pe_fold, 1)


def quantise(dve, a, i):
    NB = FF * DM // P // WBLK
    quant, steps, inv_steps = a["quant"], a["steps"], a["inv_steps"]
    blocks = a["raw"][i][:, :].rearrange("p (b k) -> p b k", k=WBLK)
    lv = a["levels"][:, :].rearrange("p (b k) -> p b k", k=WBLK)

    def block_steps():
        dve.tensor_reduce(steps[:, i, :], blocks, AX_X, ALU.max, apply_absolute_value=True).then_inc(quant, 1)
        dve.wait_ge(quant, 5 * i + 1)
        dve.tensor_scalar(steps[:, i, :], steps[:, i, :], 1.0 / 7.0, TINY, ALU.mult, ALU.max).then_inc(quant, 1)
        dve.wait_ge(quant, 5 * i + 2)
        dve.reciprocal(inv_steps[:, i, :], steps[:, i, :]).then_inc(quant, 1)

    def to_levels():
        dve.wait_ge(quant, 5 * i + 3)
        dve.tensor_tensor(lv, blocks, inv_steps[:, i, :].unsqueeze(2).to_broadcast([P, NB, WBLK]),
                          ALU.mult).then_inc(quant, 1)

    def to_weights():
        dve.wait_ge(quant, 5 * i + 4)
        dve.tensor_tensor(blocks, lv, steps[:, i, :].unsqueeze(2).to_broadcast([P, NB, WBLK]),
                          ALU.mult).then_inc(quant, 1)
    return block_steps, to_levels, to_weights


def transposed(t, i, j, hl):
    w = (t["wup"], t["wgate"], t["wdown"])[i][:, hl, :, :].rearrange("p t n -> p (t n)")
    return w[:, j * 512:(j + 1) * 512]


def is_seq(n):
    return not isinstance(n, int) or 0 <= n < NSEQ


def wait(eng, sem, value):
    if not isinstance(value, int) or value > 0:
        eng.wait_ge(sem, value)


def attention(nc, t, a, emb, h2):
    with ExitStack() as ctx:
        def sb(name, shape, dt):
            return ctx.enter_context(nc.sbuf_tensor(name, shape, dt))

        def sem(name):
            return ctx.enter_context(nc.semaphore(name))

        e_hl = sb("e_hl", [P, GS, 2 * ED], F16)
        eT_hl = sb("eT_hl", [P, GT], F16)
        h_res = sb("h_res", [P, GS, DM], F32)
        bn6 = sb("bn6", [P, GS, 6], F32)
        mv1 = sb("mv1", [P, GS, 2], F32)
        var1 = sb("var1", [P, GS], F32)
        rstd1 = sb("rstd1", [P, GS], F32)
        rs1 = sb("rs1", [P, GS], F32)
        x_dup = sb("x_dup", [P, GS, 2, ED], F32)
        x_hl = sb("x_hl", [P, GS, 2 * ED], F16)
        xT_hl = sb("xT_hl", [P, GT], F16)
        xT = sb("xT", [P, 2, GT], F32)
        qT = sb("qT", [P, 2, HP, GT], F32)
        v_aug = sb("v_aug", [P, 2, GS, H, DV + 1], F32)
        lg = sb("lg", [P, 2, H, P], F32)
        row_max = sb("row_max", [P, 2, H], F32)
        pT = sb("pT", [P, 2, H, P], F32)
        inv_sum = sb("inv_sum", [P, 2, H], F32)
        o_s = sb("o_s", [P, 2, H, DV], F32)
        oT_hl = sb("oT_hl", [P, 2, 2, DT * P], F16)
        bn2 = sb("bn2", [P, GS, 6], F32)
        mv2 = sb("mv2", [P, GS, 2], F32)
        dev = sb("dev", [P, 2, DM], F32)
        dm4 = sb("dm4", [P, GS], F32)
        var2 = sb("var2", [P, GS], F32)
        row_numbers = sb("row_numbers", [P, 2, GS], U32)

        ps_f = ctx.enter_context(nc.psum_tensor("ps_front", [P, 2, 512], F32))
        ps_s = ctx.enter_context(nc.psum_tensor("ps_scores", [P, 2, 512], F32))
        ps_p = ctx.enter_context(nc.psum_tensor("ps_probs", [P, 2, 512], F32))
        ps_o = ctx.enter_context(nc.psum_tensor("ps_o", [P, 512], F32))
        ps_y = ctx.enter_context(nc.psum_tensor("ps_y", [P, 512], F32))

        ones_set = sem("ones_set")
        e_split = sem("e_split")
        front_done = sem("front_done")
        front_read = sem("front_read")
        stats1 = sem("stats1")
        rstd_step = sem("rstd_step")
        residual = sem("residual")
        x_split = sem("x_split")
        scores = sem("scores")
        biased = sem("biased")
        maxed = sem("maxed")
        shifted = sem("shifted")
        exped = sem("exped")
        p_turned = sem("p_turned")
        p_copied = sem("p_copied")
        mixed = sem("mixed")
        inverted = sem("inverted")
        o_normed = sem("o_normed")
        o_turned = sem("o_turned")
        o_high = sem("o_high")
        o_low = sem("o_low")
        projected = sem("projected")
        h2_done = sem("h2_done")
        stats2 = sem("stats2")
        aggr2 = sem("aggr2")
        dev_done = sem("dev_done")
        dev_maxed = sem("dev_maxed")
        mv_moved = sem("mv_moved")
        dev_moved = sem("dev_moved")
        rstd2_step = sem("rstd2_step")

        ffw_turned = sem("ffw_turned")
        ffw_high = sem("ffw_high")
        ffw_low = sem("ffw_low")
        gathered = [sem(f"gathered{i}") for i in range(2)]
        numbered = sem("numbered")
        carried = sem("carried")

        def gathered_count(G, par):
            return (G - par) * (16 * GS // 2)

        block = ctx.enter_context(nc.Block())
        V0, V1, NORMAL_SPLIT, NORMAL_WHOLE, RAW, H0, H1, Q0, Q1, Q2, Q3 = units = list(range(11))
        UNITS = len(units)

        def units_of(g):
            if g == -2:
                return [RAW, H0, H1]
            if g == -1:
                return [NORMAL_SPLIT, NORMAL_WHOLE, Q0, Q1, Q2, Q3, RAW, H0, H1]
            if g == NG - 2:
                return [k for k in units if k not in (RAW, H0, H1)]
            return [V0, V1] if g == NG - 1 else units

        def before(g, k):
            if not isinstance(g, int):
                return g * UNITS + (len(units_of(-2)) + len(units_of(-1)) + k)
            return sum(len(units_of(e)) for e in range(-2, g)) + units_of(g).index(k)

        def grouped(eng, front0, slot):
            front0()
            for g in range(2):
                for s in range(GS):
                    slot(g, s, g % 2)
            with eng.Fori(1, NG // 2 - 2) as pair:
                for b in range(2):
                    for s in range(GS):
                        slot(pair * 2 + b, s, b)
            for g in range(NG - 4, NG + 2):
                for s in range(GS):
                    slot(g, s, g % 2)

        @block.tensor
        def _(pe):
            def unit_ready(g, k):
                mine = units_of(g) if isinstance(g, int) else units
                other_bank = k != mine[0] and (mine[mine.index(k) - 1] - k) % 2
                wait(pe, front_read, before(g, k) - (1 if other_bank else 0))

            def turn_raw(G):
                pe.wait_ge(e_split, G * 2 + 2)
                unit_ready(G - 2, RAW)
                for s in range(GS):
                    last = pe.transpose(ps_f[:, RAW % 2, 0:GT // 2].bitcast(F16)[:, s * P:(s + 1) * P], e_hl[:, s, :],
                                        a["ident16"][:, :])
                last.then_inc(front_done, 1)

            def project_raw(G, k):
                if k == H0:
                    pe.wait_ge(front_read, before(G - 2, RAW) + 1)
                unit_ready(G - 2, k)
                for s in (2 * (k - H0), 2 * (k - H0) + 1):
                    for hl in range(2):
                        last = pe.matmul(ps_f[:, k % 2, s % 2 * DM:(s % 2 + 1) * DM], eT_hl[:, s * P:(s + 1) * P],
                                         a["pt"][:, hl, :], start=hl == 0, stop=hl == 1)
                last.then_inc(front_done, 1)

            def turn_normal_split(G):
                pe.wait_ge(x_split, G * 3 + 3)
                unit_ready(G - 1, NORMAL_SPLIT)
                for s in range(GS):
                    last = pe.transpose(ps_f[:, NORMAL_SPLIT % 2, 0:GT // 2].bitcast(F16)[:, s * P:(s + 1) * P],
                                        x_hl[:, s, :], a["ident16"][:, :])
                last.then_inc(front_done, 1)

            def turn_normal_whole(G):
                unit_ready(G - 1, NORMAL_WHOLE)
                for s in range(GS):
                    last = pe.transpose(ps_f[:, NORMAL_WHOLE % 2, s * P:(s + 1) * P],
                                        x_dup[:, s, :, :].rearrange("p u d -> p (u d)"), t["ident32"][:, :])
                last.then_inc(front_done, 1)

            def queries(G, pair):
                k = Q0 + pair
                unit_ready(G - 1, k)
                if pair == 0:
                    pe.wait_ge(front_read, before(G - 1, NORMAL_SPLIT) + 1)
                for hl in range(2):
                    last = pe.matmul(ps_f[:, k % 2, :], a["g"][:, hl, pair, :], xT_hl[:, :], start=hl == 0, stop=hl == 1)
                last.then_inc(front_done, 1)

            def values(G, k):
                unit_ready(G, k)
                for s in (2 * k, 2 * k + 1):
                    for hl in range(2):
                        last = pe.matmul(ps_f[:, k % 2, s % 2 * DM:(s % 2 + 1) * DM], xT_hl[:, s * P:(s + 1) * P],
                                         a["mv"][:, hl, :], start=hl == 0, stop=hl == 1)
                last.then_inc(front_done, 1)

            def front_units(g, s):
                nxt, raw = is_seq((g + 1) * GS), is_seq((g + 2) * GS)
                if s == 0 and is_seq(g * GS):
                    return [None, lambda: values(g, V0), lambda: values(g, V1)]
                if s == 1 and nxt:
                    return [lambda: turn_normal_split(g + 1), lambda: turn_normal_whole(g + 1),
                            (lambda: turn_raw(g + 2)) if raw else None]
                if s == 2 and nxt:
                    return [(lambda: project_raw(g + 2, H0)) if raw else None,
                            (lambda: project_raw(g + 2, H1)) if raw else None, lambda: queries(g + 1, 0)]
                if s == 3 and nxt:
                    return [lambda: queries(g + 1, 1), lambda: queries(g + 1, 2), lambda: queries(g + 1, 3)]
                return [None] * 3

            def slot(g, s, par):
                n = g * GS + s
                front = front_units(g, s)
                if is_seq(n):
                    if s == 0:
                        pe.wait_ge(front_read, before(g - 1, Q3) + 1)
                    wait(pe, biased, n)
                    for pair in range(HP):
                        for parity in range(2):
                            r = slice(parity * ED, (parity + 1) * ED)
                            last = pe.matmul(ps_s[:, parity, pair * P:(pair + 1) * P], qT[r, par, pair, s * P:(s + 1) * P],
                                             xT[r, par, s * P:(s + 1) * P], start=True, stop=True)
                    last.then_inc(scores, 1)
                if is_seq(n - 2):
                    pe.wait_ge(o_normed, n - 1)
                    wait(pe, h2_done, n - 2)
                    for k in range(DT):
                        last = pe.transpose(ps_y[:, k * P:(k + 1) * P],
                                            o_s[:, s % 2, :, :].rearrange("p h d -> p (h d)")[:, k * P:(k + 1) * P],
                                            t["ident32"][:, :])
                    last.then_inc(o_turned, 1)
                if front[0]:
                    front[0]()
                if is_seq(n - 1):
                    b = (s + 1) % 2
                    pe.wait_ge(exped, n)
                    wait(pe, p_copied, n - 1)
                    for q in range(H):
                        last = pe.transpose(ps_p[:, q // HP, q % HP * P:(q % HP + 1) * P], lg[:, b, q, :], t["ident32"][:, :])
                    last.then_inc(p_turned, 1)
                if front[1]:
                    front[1]()
                if is_seq(n - 2):
                    pe.wait_ge(o_high, n - 1)
                    pe.wait_ge(o_low, n - 1)
                    terms = [(k, xh, wh) for k in range(DT) for xh, wh in ((0, 0), (1, 0), (0, 1))]
                    for i, (k, xh, wh) in enumerate(terms):
                        last = pe.matmul(ps_y[:, DM:2 * DM], oT_hl[:, s % 2, xh, k * P:(k + 1) * P], a["wo"][:, wh, k, :],
                                         start=i == 0, stop=i == len(terms) - 1)
                    last.then_inc(projected, 1)
                if is_seq(n - 1):
                    if s == 1:
                        pe.wait_ge(front_read, before(g, V1) + 1)
                    pe.wait_ge(p_copied, n)
                    wait(pe, o_normed, n - 1)
                    for q in range(H):
                        if q == H // 2 and front[2]:
                            front[2]()
                        h = 2 * (q % HP) + q // HP
                        last = pe.matmul(ps_o[:, h * (DV + 1):(h + 1) * (DV + 1)], pT[:, b, q, :],
                                         v_aug[:, par if s else 1 - par, (s - 1) % GS, h, :], start=True, stop=True)
                    last.then_inc(mixed, 1)
                elif front[2]:
                    front[2]()

            pe.wait_ge(ones_set, 1)

            def turn_weights(n):
                i, j = n // 3, n % 3
                pe.wait_ge(a["quant"], 5 * i + 5)
                wait(pe, ffw_low, n - 1)
                for q in range(4):
                    if i < 2:
                        kt, ot = (4 * j + q) // FT, (4 * j + q) % FT
                        src = a["raw"][i][:, ot * DM + kt * P:ot * DM + (kt + 1) * P]
                    else:
                        kt, ot = (4 * j + q) // DT, (4 * j + q) % DT
                        src = a["raw"][i][:, ot * FF + kt * P:ot * FF + (kt + 1) * P]
                    last = pe.transpose(ps_p[:, n % 2, q * P:(q + 1) * P], src, t["ident32"][:, :])
                last.then_inc(ffw_turned, 1)

            def front0():
                turn_raw(0)
                turn_weights(0)
                turn_weights(1)
                project_raw(0, H0)
                project_raw(0, H1)
                turn_weights(2)
                turn_normal_split(0)
                turn_normal_whole(0)
                for pair in range(HP):
                    queries(0, pair)
                turn_raw(1)
                for n in range(3, 6):
                    turn_weights(n)
                project_raw(1, H0)
                project_raw(1, H1)
                for n in range(6, 9):
                    turn_weights(n)
                pe.wait_ge(ffw_low, 9)
            grouped(pe, front0, slot)

        @block.scalar
        def _(act):
            def unit(g, k):
                act.wait_ge(front_done, before(g, k) + 1)

            def copy_raw(G):
                unit(G - 2, RAW)
                act.copy(eT_hl[:, :], ps_f[:, RAW % 2, 0:GT // 2].bitcast(F16)).then_inc(front_read, 1)

            def copy_h(G, k):
                if k == H0:
                    wait(act, residual, G)
                    wait(act, stats1, G * 2)
                unit(G - 2, k)
                act.mul(h_res[:, 2 * (k - H0):2 * (k - H0) + 2, :], ps_f[:, k % 2, :].rearrange("p (s f) -> p s f", f=DM),
                        a["h_scale"][:, 0:1]).then_inc(front_read, 1)

            def copy_normal_split(G):
                unit(G - 1, NORMAL_SPLIT)
                act.copy(xT_hl[:, :], ps_f[:, NORMAL_SPLIT % 2, 0:GT // 2].bitcast(F16)).then_inc(front_read, 1)

            def copy_normal_whole(G, par):
                unit(G - 1, NORMAL_WHOLE)
                wait(act, scores, (G - 1) * GS)
                act.mul(xT[:, par, :], ps_f[:, NORMAL_WHOLE % 2, :], 1.0 / SC_X).then_inc(front_read, 1)

            def copy_queries(G, par, pair):
                k = Q0 + pair
                unit(G - 1, k)
                act.mul(qT[:, par, pair, :], ps_f[:, k % 2, :], 1.0 / (SC_X * SC_G)).then_inc(front_read, 1)

            def copy_values(G, par, k):
                if k == V0:
                    wait(act, mixed, (G - 1) * GS)
                unit(G, k)
                act.mul(v_aug[:, par, 2 * k:2 * k + 2, :, 0:DV].rearrange("p s h d -> p (s h) d"),
                        ps_f[:, k % 2, :].rearrange("p (h d) -> p h d", d=DV),
                        1.0 / (SC_X * SC_V)).then_inc(front_read, 1)

            def front_units(g, s, par):
                nxt, raw = is_seq((g + 1) * GS), is_seq((g + 2) * GS)
                if s == 0 and is_seq(g * GS):
                    return [None, lambda: copy_values(g, par, V0), lambda: copy_values(g, par, V1)]
                if s == 1 and nxt:
                    return [lambda: copy_normal_split(g + 1), lambda: copy_normal_whole(g + 1, 1 - par)] + (
                        [lambda: copy_raw(g + 2)] if raw else [])
                if s == 2 and nxt:
                    return ([lambda: copy_h(g + 2, H0), lambda: copy_h(g + 2, H1)] if raw else [None]) + [
                        lambda: copy_queries(g + 1, 1 - par, 0)]
                if s == 3 and nxt:
                    return [lambda: copy_queries(g + 1, 1 - par, 1), lambda: copy_queries(g + 1, 1 - par, 2),
                            lambda: copy_queries(g + 1, 1 - par, 3)]
                return []

            def slot(g, s, par):
                n = g * GS + s
                front = front_units(g, s, par)
                if is_seq(n - 1):
                    b = (s + 1) % 2
                    act.wait_ge(shifted, n)
                    act.activation(lg[:, b, :, :], lg[:, b, :, :], ACT.Exp).then_inc(exped, 1)
                if is_seq(n - 2):
                    act.wait_ge(o_turned, n - 1)
                    wait(act, projected, n - 3)
                    act.mul(oT_hl[:, s % 2, 0, :], ps_y[:, 0:DM], SC_O).then_inc(o_high, 1)
                if front and front[0]:
                    front[0]()
                if is_seq(n - 1):
                    act.wait_ge(p_turned, n)
                    wait(act, mixed, n - 2)
                    act.copy(pT[:, b, :, :].rearrange("p (u q) j -> p u (q j)", u=2), ps_p[:, :, :]).then_inc(p_copied, 1)
                for unit_read in front[1:]:
                    unit_read()
                if is_seq(n - 4):
                    act.wait_ge(aggr2, n - 3)
                    wait(act, dev_maxed, n - 5)
                    act.activation(dev[:, s % 2, :], h2[:, n - 4, :], ACT.Identity, bias=mv2[:, s % GS, 0:1],
                                   scale=-1.0).then_inc(dev_done, 1)

            def front0():
                copy_raw(0)
                high_weights(0)
                high_weights(1)
                copy_h(0, H0)
                copy_h(0, H1)
                high_weights(2)
                copy_normal_split(0)
                copy_normal_whole(0, 0)
                for pair in range(HP):
                    copy_queries(0, 0, pair)
                copy_raw(1)
                for n in range(3, 6):
                    high_weights(n)
                copy_h(1, H0)
                copy_h(1, H1)
                for n in range(6, 9):
                    high_weights(n)

            def high_weights(n):
                act.wait_ge(ffw_turned, n + 1)
                act.activation(transposed(t, n // 3, n % 3, 0), ps_p[:, n % 2, :], ACT.Copy, scale=SC_W).then_inc(ffw_high, 1)

            grouped(act, front0, slot)

        @block.gpsimd
        def _(pool):
            pool.memset(v_aug[:, :, :, :, DV:DV + 1].rearrange("p b s h u -> p (b s h u)"), 1.0).then_inc(ones_set, 1)

            def rstd_of_h(G):
                pool.wait_ge(stats1, G * 2 + 2)
                pool.tensor_tensor(var1[:, :], mv1[:, :, 1], a["eps"][:, :], ALU.add).then_inc(rstd_step, 1)
                pool.wait_ge(rstd_step, G * 3 + 1)
                pool.tensor_tensor(rstd1[:, :], var1[:, :], a["minus_half"][:, :], ALU.pow).then_inc(rstd_step, 1)
                pool.wait_ge(rstd_step, G * 3 + 2)
                wait(pool, x_split, G * 3)
                pool.tensor_tensor(rs1[:, :], rstd1[:, :], a["x_scale"][:, 0:1].to_broadcast([P, GS]), ALU.mult).then_inc(rstd_step, 1)

            def copy_row_numbers(G, par):
                wait(pool, gathered[par], gathered_count(G - 2, par))
                pool.wait_ge(x_split, (G - 2) * 3 + 3)
                pool.sem_inc(carried, 1)
                pool.tensor_copy(row_numbers[:, par, :], a["rows"][:, bass.ts(G, GS)]).then_inc(numbered, 1)
                pool.wait_ge(numbered, G - 1)
                pool.sem_inc(carried, 1)

            def gather(par, s):
                pool.indirect_dma_start(a["emb_rows"][:, par, s, :], None, emb,
                                        bass.IndirectOffsetOnAxis(ap=row_numbers[:, par, s:s + 1], axis=0)).then_inc(gathered[par], 16)

            def add_bias(G):
                pool.wait_ge(front_read, before(G - 2, H1) + 1)
                pool.tensor_tensor(h2[:, bass.ts(G, GS), :], h_res[:, :, :],
                                   a["bout"][:, :].unsqueeze(1).to_broadcast([P, GS, DM]), ALU.add).then_inc(residual, 1)

            def rstd_of_h2(G):
                pool.wait_ge(mv_moved, G + 1)
                wait(pool, rstd2_step, G * 2)
                pool.tensor_tensor(var2[:, :], t["mean_var"][:, bass.ts(G, GS), 1], a["eps"][:, :], ALU.add).then_inc(rstd2_step, 1)
                pool.wait_ge(rstd2_step, G * 2 + 1)
                pool.tensor_tensor(t["rstd"][:, bass.ts(G, GS)], var2[:, :], a["minus_half"][:, :], ALU.pow).then_inc(rstd2_step, 1)

            def slot(g, s, par):
                n = g * GS + s
                if s == 0 and is_seq(n + GS):
                    rstd_of_h(g + 1)
                if is_seq(n):
                    pool.wait_ge(maxed, n + 1)
                    pool.tensor_tensor(lg[:, s % 2, :, :], lg[:, s % 2, :, :],
                                       row_max[:, s % 2, :].unsqueeze(2).to_broadcast([P, H, P]),
                                       ALU.subtract).then_inc(shifted, 1)
                if s == 0 and is_seq(n + GS):
                    add_bias(g + 1)
                if is_seq(n + 3 * GS):
                    if s == 1:
                        copy_row_numbers(g + 3, 1 - par)
                        gather(1 - par, 0)
                        gather(1 - par, 1)
                    if s > 1:
                        gather(1 - par, s)
                if s == 3 and is_seq(n - 4):
                    rstd_of_h2(g - 1)

            def front0():
                rstd_of_h(0)
                add_bias(0)
                copy_row_numbers(2, 0)
                for s in range(GS):
                    gather(0, s)
            grouped(pool, front0, slot)

        @block.vector
        def _(dve):
            def split_raw(G, par):
                wait(dve, gathered[par], gathered_count(G, par))
                rows = a["emb_rows"][:, par, :, :]
                if not (isinstance(G, int) and G == 0):
                    dve.wait_ge(front_done, before(G - 3, RAW) + 1)
                dve.tensor_scalar(e_hl[:, :, 0:ED], rows, SC_E, None, ALU.mult).then_inc(e_split, 1)
                dve.wait_ge(e_split, G * 2 + 1)
                dve.scalar_tensor_tensor(e_hl[:, :, ED:2 * ED], rows, SC_E, e_hl[:, :, 0:ED],
                                         ALU.mult, ALU.subtract).then_inc(e_split, 1)

            def stats_h(G):
                dve.wait_ge(front_read, before(G - 2, H1) + 1)
                for s in range(GS):
                    last = dve.bn_stats(bn6[:, s, :], h_res[:, s, :])
                last.then_inc(stats1, 1)

            def wait_stats_h(G):
                dve.wait_ge(stats1, G * 2 + 1)
                wait(dve, rstd_step, G * 3)

            def aggr_h(G):
                for s in range(GS):
                    last = dve.bn_aggr(mv1[:, s, :], bn6[:, s, :])
                last.then_inc(stats1, 1)

            def normalise(G, par):
                dve.wait_ge(rstd_step, G * 3 + 3)
                if not (isinstance(G, int) and G == 0):
                    dve.wait_ge(front_done, before(G - 2, NORMAL_WHOLE) + 1)
                dve.tensor_tensor(x_dup[:, :, :, :],
                                  a["emb_rows"][:, par, :, :].unsqueeze(2).to_broadcast([P, GS, 2, ED]),
                                  rs1[:, :].unsqueeze(2).unsqueeze(3).to_broadcast([P, GS, 2, ED]),
                                  ALU.mult).then_inc(x_split, 1)
                dve.wait_ge(x_split, G * 3 + 1)
                dve.tensor_copy(x_hl[:, :, 0:ED], x_dup[:, :, 0, :]).then_inc(x_split, 1)
                dve.wait_ge(x_split, G * 3 + 2)
                dve.tensor_tensor(x_hl[:, :, ED:2 * ED], x_dup[:, :, 0, :], x_hl[:, :, 0:ED],
                                  ALU.subtract).then_inc(x_split, 1)

            def slot(g, s, par):
                n = g * GS + s
                b = s % 2
                m = (s + 1) % GS
                if is_seq(n - 3):
                    dve.wait_ge(projected, n - 2)
                    if s == 3:
                        dve.wait_ge(residual, g + 1)
                    dve.scalar_tensor_tensor(h2[:, n - 3, :], ps_y[:, DM:2 * DM], 1.0 / (SC_O * SC_WO), h2[:, n - 3, :],
                                             ALU.mult, ALU.add).then_inc(h2_done, 1)
                if is_seq(n - 2):
                    dve.wait_ge(mixed, n - 1)
                    o_ps = ps_o[:, 0:H * (DV + 1)].rearrange("p (h d) -> p h d", d=DV + 1)
                    dve.reciprocal(inv_sum[:, b, :], o_ps[:, :, DV]).then_inc(inverted, 1)
                if is_seq(n - 3):
                    dve.wait_ge(h2_done, n - 2)
                if is_seq(n - 2):
                    dve.wait_ge(inverted, n - 1)
                    wait(dve, o_turned, n - 3)
                    dve.tensor_tensor(o_s[:, b, :, :], o_ps[:, :, 0:DV],
                                      inv_sum[:, b, :].unsqueeze(2).to_broadcast([P, H, DV]), ALU.mult).then_inc(o_normed, 1)
                if is_seq(n - 3):
                    dve.bn_stats(bn2[:, m, :], h2[:, n - 3, :]).then_inc(stats2, 1)
                if is_seq(n):
                    dve.wait_ge(scores, n + 1)
                    wait(dve, p_turned, n - 1)
                    dve.tensor_tensor(lg[:, b, :, :].rearrange("p (u q) j -> p u (q j)", u=2), ps_s[:, :, :],
                                      a["bias"][:, :, :, :].rearrange("p u q j -> p u (q j)"), ALU.add).then_inc(biased, 1)
                if is_seq(n - 2):
                    dve.wait_ge(o_high, n - 1)
                    dve.scalar_tensor_tensor(oT_hl[:, b, 1, :], ps_y[:, 0:DM], SC_O, oT_hl[:, b, 0, :],
                                             ALU.mult, ALU.subtract).then_inc(o_low, 1)
                if is_seq(n):
                    dve.wait_ge(biased, n + 1)
                    dve.tensor_reduce(row_max[:, b, :], lg[:, b, :, :], AX_X, ALU.max).then_inc(maxed, 1)
                if s == 0 and is_seq(n + GS):
                    normalise(g + 1, 1 - par)
                    if is_seq(n + 2 * GS):
                        split_raw(g + 2, par)
                if s == 3 and is_seq(n + 2 * GS):
                    stats_h(g + 2)
                    wait_stats_h(g + 2)
                if is_seq(n - 3):
                    dve.wait_ge(stats2, n - 2)
                if is_seq(n - 5):
                    dve.wait_ge(dev_done, n - 4)
                    dve.tensor_reduce(dm4[:, (s + 3) % GS:(s + 3) % GS + 1], dev[:, (s + 1) % 2, :], AX_X, ALU.max,
                                      apply_absolute_value=True).then_inc(dev_maxed, 1)
                if s == 3 and is_seq(n + 2 * GS):
                    aggr_h(g + 2)
                if is_seq(n - 3):
                    dve.bn_aggr(mv2[:, m, :], bn2[:, m, :]).then_inc(aggr2, 1)
                if is_seq(n - 5) and s == 0:
                    dve.wait_ge(dev_maxed, n - 4)
                    dve.tensor_copy(t["dev_max"][:, bass.ts(g - 2, GS)], dm4[:, :]).then_inc(dev_moved, 1)
                if is_seq(n - 3) and s == 2:
                    dve.wait_ge(aggr2, n - 2)
                    dve.tensor_copy(t["mean_var"][:, bass.ts(g - 1, GS), :], mv2[:, :, :]).then_inc(mv_moved, 1)

            def front0():
                split_raw(0, 0)
                steps1, levels1, weights1 = quantise(dve, a, 1)
                steps2, levels2, weights2 = quantise(dve, a, 2)
                steps1()
                low_weights(0)
                low_weights(1)
                stats_h(0)
                wait_stats_h(0)
                aggr_h(0)
                levels1()
                normalise(0, 0)
                low_weights(2)
                weights1()
                split_raw(1, 1)
                steps2()
                levels2()
                low_weights(3)
                weights2()
                low_weights(4)
                low_weights(5)
                stats_h(1)
                wait_stats_h(1)
                aggr_h(1)
                for n in range(6, 9):
                    low_weights(n)

            def low_weights(n):
                dve.wait_ge(ffw_high, n + 1)
                dve.scalar_tensor_tensor(transposed(t, n // 3, n % 3, 1), ps_p[:, n % 2, :], SC_W,
                                         transposed(t, n // 3, n % 3, 0), ALU.mult, ALU.subtract).then_inc(ffw_low, 1)

            grouped(dve, front0, slot)


def feed_forward(nc, t, h2, out):
    with ExitStack() as ctx:
        c = {}
        for name in ("s_x", "k_x", "s_gate", "s_up", "k_gate", "k_up", "s_p", "k_p", "k_o", "s_y"):
            c[name] = ctx.enter_context(nc.sbuf_tensor(name, [P, 1], F32))[:, :]
        h2_d = nc.dram_tensor("h2_scratch", [P, NSEQ * DM], F32, kind="Internal").ap()
        qu_d = nc.dram_tensor("qu_scratch", [P, NG * NCH * CW], I16, kind="Internal").ap()
        amax = ctx.enter_context(nc.sbuf_tensor("amax", [P, 4], F32))
        acc = ctx.enter_context(nc.sbuf_tensor("acc", [P, 2], F32))
        acc2 = ctx.enter_context(nc.sbuf_tensor("acc2", [P, 2], F32))
        a_tok = ctx.enter_context(nc.sbuf_tensor("a_tok", [P, NSEQ], F32))
        xq = ctx.enter_context(nc.sbuf_tensor("xq_hl", [P, 2, DT, NSEQ * P], F16))
        flat = xq[:, :, :, :].rearrange("p l k n -> p (l k n)")
        cuts = [0]
        for size in (NB * NCH * CW, NB * GS * DM * 2, NB * GS * DM * 2, NCH * CW):
            cuts.append(cuts[-1] + size)
        parts = [flat[:, i:j] for i, j in zip(cuts, cuts[1:])]
        down = {"qu": parts[0].bitcast(I16).rearrange("p (b n) -> p b n", b=NB),
                "res": parts[1].bitcast(F32).rearrange("p (b n) -> p b n", b=NB),
                "y": parts[2].bitcast(F32).rearrange("p (b n) -> p b n", b=NB),
                "qo": parts[3].bitcast(I16).rearrange("p (c n) -> p c n", c=NCH),
                "loaded": [ctx.enter_context(nc.semaphore(f"d_loaded{i}")) for i in range(NB)]}

        def load(sp, g, b):
            sp.dma_start(down["qu"][:, b, :], qu_d[:, bass.ts(g, NCH * CW)]).then_inc(down["loaded"][b], 16)
            sp.dma_start(down["res"][:, b, :], h2_d[:, bass.ts(g, GS * DM)]).then_inc(down["loaded"][b], 16)
        pass_max(nc, t, c, h2, a_tok, xq, amax, h2_d)
        pass_gate(nc, t, c, xq, amax, acc)
        pass_up(nc, t, c, xq, acc, acc2, qu_d, load)
        pass_down(nc, t, c, acc2, down, load, out)


def input_scale(nc, ctx, t, c, a_tok):
    tok = ctx.enter_context(nc.sbuf_tensor("x_tok", [P, NSEQ], F32))
    mx = ctx.enter_context(nc.sbuf_tensor("x_mx", [P, 1], F32))
    gx = ctx.enter_context(nc.sbuf_tensor("x_gx", [P, 1], F32))
    step = ctx.enter_context(nc.semaphore("x_step"))
    reduced = ctx.enter_context(nc.semaphore("x_reduced"))
    rstd = t["rstd"]

    def pool_part(pool):
        pool.wait_ge(step, 2)
        pool.partition_all_reduce(gx[:, :], mx[:, :], P, RMAX).then_inc(reduced, 1)

    def dve_part(dve):
        dve.tensor_tensor(tok[:, :], t["dev_max"][:, :], rstd[:, :], ALU.mult).then_inc(step, 1)
        dve.wait_ge(step, 1)
        dve.tensor_reduce(mx[:, :], tok[:, :], AX_X, ALU.max).then_inc(step, 1)
        dve.wait_ge(reduced, 1)
        dve.tensor_scalar(c["s_x"], gx[:, :], 1.0 / QMAX, TINY, ALU.mult, ALU.max).then_inc(step, 1)
        dve.wait_ge(step, 3)
        dve.reciprocal(c["k_x"], c["s_x"]).then_inc(step, 1)
        dve.wait_ge(step, 4)
        dve.tensor_scalar(a_tok[:, :], rstd[:, :], c["k_x"], None, ALU.mult).then_inc(step, 1)
        dve.wait_ge(step, 5)
    return pool_part, dve_part


def gate_up_scales(nc, ctx, c, amax):
    mx = ctx.enter_context(nc.sbuf_tensor("ug_mx", [P, 2], F32))
    gx = ctx.enter_context(nc.sbuf_tensor("ug_gx", [P, 2], F32))
    sx = ctx.enter_context(nc.sbuf_tensor("ug_sx", [P, 1], F32))
    inv = ctx.enter_context(nc.sbuf_tensor("ug_inv", [P, 2], F32))
    step = ctx.enter_context(nc.semaphore("ug_step"))
    reduced = ctx.enter_context(nc.semaphore("ug_reduced"))

    def pool_part(pool):
        pool.wait_ge(step, 2)
        pool.partition_all_reduce(gx[:, :], mx[:, :], P, RMAX).then_inc(reduced, 1)

    def dve_part(dve):
        dve.tensor_scalar(sx[:, :], c["s_x"], 1.0 / SC_W, None, ALU.mult).then_inc(step, 1)
        dve.tensor_reduce(mx[:, :], amax[:, :].rearrange("p (w c) -> p w c", w=2), AX_X, ALU.max).then_inc(step, 1)
        dve.wait_ge(reduced, 1)
        dve.wait_ge(step, 2)
        for i, s in enumerate(("s_up", "s_gate")):
            dve.tensor_scalar(c[s], gx[:, i:i + 1], sx[:, :], 1.0 / QMAX, ALU.mult, ALU.mult).then_inc(step, 1)
        dve.wait_ge(step, 4)
        for i, s in enumerate(("s_up", "s_gate")):
            dve.tensor_scalar(c[s], c[s], TINY, None, ALU.max).then_inc(step, 1)
        dve.wait_ge(step, 6)
        for i, s in enumerate(("s_up", "s_gate")):
            dve.reciprocal(inv[:, i:i + 1], c[s]).then_inc(step, 1)
        dve.wait_ge(step, 8)
        for i, k in enumerate(("k_up", "k_gate")):
            dve.tensor_scalar(c[k], inv[:, i:i + 1], sx[:, :], None, ALU.mult).then_inc(step, 1)
    return pool_part, dve_part, (step, 10)


def product_scale(nc, ctx, c, acc, sa, sb_, factor, s_out, k_out, divide=1.0):
    names = ("gx", "unit", "sc", "inv")
    gx, unit, sc, inv = (ctx.enter_context(nc.sbuf_tensor(f"{s_out}_{n}", [P, 1], F32))[:, :] for n in names)
    step = ctx.enter_context(nc.semaphore(f"{s_out}_step"))
    reduced = ctx.enter_context(nc.semaphore(f"{s_out}_reduced"))

    def pool_part(pool):
        pool.partition_all_reduce(gx, acc[:, 1:2], P, RMAX).then_inc(reduced, 1)

    def dve_part(dve):
        if sb_ is None:
            dve.tensor_scalar(unit, c[sa], factor, None, ALU.mult).then_inc(step, 1)
        else:
            dve.tensor_scalar(unit, c[sa], c[sb_], None, ALU.mult).then_inc(step, 1)
        dve.wait_ge(step, 1)
        dve.wait_ge(reduced, 1)
        dve.tensor_scalar(sc, gx, unit, 1.0 / QMAX, ALU.mult, ALU.mult).then_inc(step, 1)
        dve.wait_ge(step, 2)
        dve.tensor_scalar(sc, sc, TINY, None, ALU.max).then_inc(step, 1)
        dve.wait_ge(step, 3)
        dve.reciprocal(inv, sc).then_inc(step, 1)
        dve.tensor_scalar(c[s_out], sc, 1.0 / divide, None, ALU.mult).then_inc(step, 1)
        dve.wait_ge(step, 5)
        dve.tensor_scalar(c[k_out], inv, unit, None, ALU.mult).then_inc(step, 1)
        dve.wait_ge(step, 6)
    return pool_part, dve_part


def chunk_products(pe, ps, w, ch, xq, tok):
    for f in range(CT):
        cols = slice((ch * CT + f) * P, (ch * CT + f + 1) * P)
        terms = [(k, wh, xh) for k in range(DT) for wh, xh in ((0, 0), (0, 1), (1, 0))]
        for i, (k, wh, xh) in enumerate(terms):
            last = pe.matmul(ps[:, f, :], w[:, wh, k, cols], xq[:, xh, k, tok], start=i == 0, stop=i == len(terms) - 1)
    return last


def pass_max(nc, t, c, h2, a_tok, xq, amax, h2_d):
    with ExitStack() as ctx:
        def sb(name, shape, dt):
            return ctx.enter_context(nc.sbuf_tensor(name, shape, dt))

        def sem(name):
            return ctx.enter_context(nc.semaphore(name))
        y = sb("y_norm", [P, GS, DM], F32)
        xi = sb("x_int", [P, DT, GT], I16)
        amax_g = sb("amax_g", [P, 4], F32)
        ps_x = ctx.enter_context(nc.psum_tensor("ps_x", [P, DT, 512], F32))
        ps_c = [ctx.enter_context(nc.psum_tensor(f"ps_c{i}", [P, CT, 512], F32)) for i in range(2)]
        scaled = sem("scaled")
        x_turned = sem("x_turned")
        rounded = sem("rounded")
        x_split = sem("xq_split")
        products = sem("products")
        chunk_max = sem("chunk_max")
        running = sem("running")
        saved = sem("h2_saved")
        scale_on_pool, scale_on_dve = input_scale(nc, ctx, t, c, a_tok)
        block = ctx.enter_context(nc.Block())

        def groups(eng, group):
            group(0, True)
            with eng.Fori(1, NG - 1) as g:
                group(g, True)
            group(NG - 1, False)

        @block.sync
        def _(sp):
            flat = h2.rearrange("p n f -> p (n f)")
            for q in range(4):
                part = slice(q * NSEQ * DM // 4, (q + 1) * NSEQ * DM // 4)
                sp.dma_start(h2_d[:, part], flat[:, part]).then_inc(saved, 16)
            sp.wait_ge(saved, 64)

        @block.gpsimd
        def _(pool):
            scale_on_pool(pool)

        @block.tensor
        def _(pe):
            def turn(g):
                pe.wait_ge(scaled, g + 1)
                wait(pe, rounded, g)
                for s in range(GS):
                    for k in range(DT):
                        last = pe.transpose(ps_x[:, k, s * P:(s + 1) * P], y[:, s, k * P:(k + 1) * P], t["ident32"][:, :])
                last.then_inc(x_turned, 1)

            def group(g, more):
                pe.wait_ge(x_split, g * 2 + 2)
                for m in range(4):
                    if m == 2 and more:
                        turn(g + 1)
                    wait(pe, chunk_max, g * 4 + m - 1)
                    w = (t["wup"], t["wgate"])[m // 2]
                    chunk_products(pe, ps_c[m % 2], w, m % 2, xq, bass.ts(g, GT)).then_inc(products, 1)
            turn(0)
            groups(pe, group)

        @block.scalar
        def _(act):
            def round_(g):
                act.wait_ge(x_turned, g + 1)
                wait(act, x_split, g * 2)
                act.copy(xi[:, :, :], ps_x[:, :, :]).then_inc(rounded, 1)
            round_(0)
            groups(act, lambda g, more: more and round_(g + 1))

        @block.vector
        def _(dve):
            def scale(g):
                wait(dve, x_turned, g)
                for s in range(GS):
                    n = g * GS + s
                    last = dve.tensor_scalar(y[:, s, :], h2[:, n, :], t["mean_var"][:, n, 0:1], a_tok[:, bass.ts(n, 1)],
                                             ALU.subtract, ALU.mult)
                last.then_inc(scaled, 1)

            def split(g):
                tok = bass.ts(g, GT)
                dve.wait_ge(rounded, g + 1)
                dve.tensor_copy(xq[:, 0, :, tok], xi[:, :, :]).then_inc(x_split, 1)
                dve.wait_ge(x_split, g * 2 + 1)
                dve.tensor_tensor(xq[:, 1, :, tok], xi[:, :, :], xq[:, 0, :, tok], ALU.subtract).then_inc(x_split, 1)

            def group(g, more):
                if more:
                    scale(g + 1)
                for m in range(4):
                    if m == 0:
                        dve.wait_ge(running, g + 1)
                    dve.wait_ge(products, g * 4 + m + 1)
                    dve.tensor_reduce(amax_g[:, m:m + 1], ps_c[m % 2][:, :, :].rearrange("p f n -> p (f n)"), AX_X, ALU.max,
                                      apply_absolute_value=True).then_inc(chunk_max, 1)
                    if m == 1 and more:
                        split(g + 1)
                dve.wait_ge(chunk_max, g * 4 + 4)
                dve.tensor_tensor(amax[:, :], amax[:, :], amax_g[:, :], ALU.max).then_inc(running, 1)

            scale_on_dve(dve)
            dve.memset(amax[:, :], 0.0).then_inc(running, 1)
            dve.wait_ge(running, 1)
            scale(0)
            split(0)
            groups(dve, group)


def pass_gate(nc, t, c, xq, amax, acc):
    with ExitStack() as ctx:
        def sb(name, shape, dt):
            return ctx.enter_context(nc.sbuf_tensor(name, shape, dt))

        def sem(name):
            return ctx.enter_context(nc.semaphore(name))
        sig = sb("sig", [P, 2, CW], F32)
        qs = sb("qs", [P, 2, CW], U16)
        neg = sb("neg", [P, CW], I16)
        mag = sb("mag", [P, 2, CW], I16)
        ps_c = [ctx.enter_context(nc.psum_tensor(f"ps_g{i}", [P, CT, 512], F32)) for i in range(2)]
        products = sem("g_products")
        quantised = sem("g_quantised")
        sigged = sem("g_sigged")
        sig_q = sem("g_sig_q")
        negated = sem("g_negated")
        waited = sem("g_waited")
        magged = sem("g_magged")
        maxed = sem("g_maxed")
        scale_on_pool, scale_on_dve, (scale_step, scale_there) = gate_up_scales(nc, ctx, c, amax)
        block = ctx.enter_context(nc.Block())
        big = t["big"]

        def groups(eng, group):
            group(0)
            with eng.Fori(1, NG) as g:
                group(g)

        @block.tensor
        def _(pe):
            def group(g):
                for ch in range(NCH):
                    wait(pe, quantised, g * NCH + ch - 1)
                    chunk_products(pe, ps_c[ch], t["wgate"], ch, xq, bass.ts(g, GT)).then_inc(products, 1)
            groups(pe, group)

        @block.scalar
        def _(act):
            def quantise(m, ch):
                act.wait_ge(products, m + 1)
                act.mul(big[:, bass.ts(m, CW)], ps_c[ch][:, :, :].rearrange("p f n -> p (f n)"),
                        c["k_gate"]).then_inc(quantised, 1)

            def group(g, last=False):
                for ch in range(NCH):
                    m = g * NCH + ch
                    wait(act, sig_q, m - 1)
                    act.wait_ge(quantised, m + 1)
                    if not (last and ch == NCH - 1):
                        quantise(m + 1, 1 - ch)
                    act.activation(sig[:, ch, :], big[:, bass.ts(m, CW)], ACT.Sigmoid, scale=c["s_gate"]).then_inc(sigged, 1)
            act.wait_ge(scale_step, scale_there)
            quantise(0, 0)
            group(0)
            with act.Fori(1, NG - 1) as g:
                group(g)
            group(NG - 1, True)

        @block.gpsimd
        def _(pool):
            scale_on_pool(pool)

            def group(g):
                for ch in range(NCH):
                    m = g * NCH + ch
                    pool.wait_ge(sigged, m + 1)
                    wait(pool, maxed, m - 1)
                    sigmoid_levels(pool, qs[:, ch, :], sig[:, ch, :], waited).then_inc(sig_q, 1)
            groups(pool, group)

        @block.vector
        def _(dve):
            scale_on_dve(dve)

            def magnitude(m, ch):
                chunk = big[:, bass.ts(m, CW)]
                dve.wait_ge(quantised, m + 1)
                wait(dve, magged, m)
                dve.tensor_scalar(neg[:, :], chunk, -1.0, None, ALU.mult).then_inc(negated, 1)
                dve.wait_ge(negated, m + 1)
                if not (isinstance(m, int) and m == 0):
                    dve.wait_ge(sig_q, m)
                dve.tensor_tensor(mag[:, ch, :], chunk, neg[:, :], ALU.max).then_inc(magged, 1)

            def reduce(m, ch):
                dve.tensor_tensor_reduce(mag[:, ch, :], mag[:, ch, :], qs[:, ch, :], 1.0,
                                         0.0 if isinstance(m, int) and m == 0 else acc[:, 1 - ch:2 - ch],
                                         ALU.mult, ALU.max, acc[:, ch:ch + 1]).then_inc(maxed, 1)

            def group(g):
                for ch in range(NCH):
                    m = g * NCH + ch
                    magnitude(m, ch)
                    if not (isinstance(m, int) and m == 0):
                        reduce(m - 1, 1 - ch)
            groups(dve, group)
            dve.wait_ge(sig_q, NG * NCH)
            dve.wait_ge(magged, NG * NCH)
            dve.wait_ge(maxed, NG * NCH - 1)
            reduce(NG * NCH - 1, 1)


def sigmoid_levels(pool, out, sig, waited):
    pool.sem_inc(waited, 1)
    return pool.tensor_scalar(out, sig, 65536.0, 1.0, ALU.mult, ALU.mult)


def pass_up(nc, t, c, xq, acc_gate, acc, qu_d, load):
    with ExitStack() as ctx:
        def sb(name, shape, dt):
            return ctx.enter_context(nc.sbuf_tensor(name, shape, dt))

        def sem(name):
            return ctx.enter_context(nc.semaphore(name))
        sig = sb("u_sig", [P, CW], F32)
        qs = sb("u_qs", [P, 2, CW], U16)
        qu = sb("u_qu", [P, 2, CW], I16)
        mag_g = t["wgate"][:, :, :, :].rearrange("p l k f -> p (l k f)").bitcast(I16).rearrange("p (b n) -> p b n", b=2)
        mag_u = sb("u_mag_u", [P, 2, CW], I16)
        ps_c = [ctx.enter_context(nc.psum_tensor(f"ps_u{i}", [P, CT, 512], F32)) for i in range(2)]
        products = sem("u_products")
        quantised = sem("u_quantised")
        sigged = sem("u_sigged")
        sig_q = sem("u_sig_q")
        mag_up = sem("u_mag_up")
        negated = sem("u_negated")
        waited = sem("u_waited")
        gated = sem("u_gated")
        magged = sem("u_magged")
        maxed = sem("u_maxed")
        carried = sem("u_carried")
        saved = [sem(f"u_saved{i}") for i in range(2)]
        scale_on_pool, scale_on_dve = product_scale(nc, ctx, c, acc_gate, "s_gate", None, 1.0 / 65536.0, "s_p", "k_p")
        block = ctx.enter_context(nc.Block())
        big = t["big"]

        def groups(eng, group):
            group(0)
            with eng.Fori(1, NG) as g:
                group(g)

        @block.sync
        def _(sp):
            def group(g):
                for ch in range(NCH):
                    m = g * NCH + ch
                    sp.wait_ge(quantised, m + 1)
                    sp.dma_start(qu_d[:, bass.ts(m, CW)], qu[:, ch, :]).then_inc(saved[ch], 16)
            groups(sp, group)
            sp.wait_ge(products, NG * NCH)
            for s in saved:
                sp.wait_ge(s, 16 * NB)
            for b in range(NB):
                load(sp, b, b)
            for s in saved:
                sp.wait_ge(s, 16 * NG)

        @block.tensor
        def _(pe):
            def group(g):
                for ch in range(NCH):
                    wait(pe, mag_up, g * NCH + ch - 1)
                    chunk_products(pe, ps_c[ch], t["wup"], ch, xq, bass.ts(g, GT)).then_inc(products, 1)
            groups(pe, group)

        @block.scalar
        def _(act):
            def sigmoid(m):
                wait(act, sig_q, m)
                act.activation(sig[:, :], big[:, bass.ts(m, CW)], ACT.Sigmoid, scale=c["s_gate"]).then_inc(sigged, 1)

            def group(g, last=False):
                for ch in range(NCH):
                    m = g * NCH + ch
                    ps = ps_c[ch][:, :, :].rearrange("p f n -> p (f n)")
                    act.wait_ge(products, m + 1)
                    wait(act, saved[ch], g * 16)
                    act.mul(qu[:, ch, :], ps, c["k_up"]).then_inc(quantised, 1)
                    if not (last and ch == NCH - 1):
                        sigmoid(m + 1)
                    wait(act, maxed, m - 1)
                    act.activation(mag_u[:, ch, :], ps, ACT.Abs, scale=c["k_up"]).then_inc(mag_up, 1)
            sigmoid(0)
            group(0)
            with act.Fori(1, NG - 1) as g:
                group(g)
            group(NG - 1, True)

        @block.gpsimd
        def _(pool):
            scale_on_pool(pool)

            def group(g):
                for ch in range(NCH):
                    m = g * NCH + ch
                    pool.wait_ge(sigged, m + 1)
                    wait(pool, gated, m - 1)
                    sigmoid_levels(pool, qs[:, ch, :], sig[:, :], waited).then_inc(sig_q, 1)
            groups(pool, group)

        @block.vector
        def _(dve):
            scale_on_dve(dve)

            def magnitude(m, ch):
                dve.wait_ge(negated, m + 1)
                dve.tensor_tensor(mag_g[:, ch, :], big[:, bass.ts(m, CW)], mag_g[:, ch, :], ALU.max).then_inc(magged, 1)

            def reduce(m, ch):
                dve.tensor_tensor_reduce(mag_u[:, ch, :], mag_g[:, ch, :], mag_u[:, ch, :], 1.0,
                                         0.0 if isinstance(m, int) and m == 0 else acc[:, 1 - ch:2 - ch],
                                         ALU.mult, ALU.max, acc[:, ch:ch + 1]).then_inc(maxed, 1)

            def group(g):
                for ch in range(NCH):
                    m = g * NCH + ch
                    chunk = big[:, bass.ts(m, CW)]
                    dve.wait_ge(sig_q, m + 1)
                    dve.scalar_tensor_tensor(chunk, chunk, c["k_p"], qs[:, ch, :], ALU.mult, ALU.mult).then_inc(gated, 1)
                    if not (isinstance(m, int) and m == 0):
                        magnitude(m - 1, 1 - ch)
                    dve.wait_ge(gated, m + 1)
                    wait(dve, maxed, m - 1)
                    dve.tensor_scalar(mag_g[:, ch, :], chunk, -1.0, None, ALU.mult).then_inc(negated, 1)
                    if not (isinstance(m, int) and m == 0):
                        dve.wait_ge(magged, m)
                        dve.wait_ge(mag_up, m)
                        dve.sem_inc(carried, 1)
                        reduce(m - 1, 1 - ch)
            groups(dve, group)
            magnitude(NG * NCH - 1, 1)
            dve.wait_ge(magged, NG * NCH)
            dve.wait_ge(mag_up, NG * NCH)
            dve.wait_ge(maxed, NG * NCH - 1)
            reduce(NG * NCH - 1, 1)


def pass_down(nc, t, c, acc_product, down, load, out):
    with ExitStack() as ctx:
        def sb(name, shape, dt):
            return ctx.enter_context(nc.sbuf_tensor(name, shape, dt))

        def sem(name):
            return ctx.enter_context(nc.semaphore(name))
        qu, res, y, qo, loaded = (down[k] for k in ("qu", "res", "y", "qo", "loaded"))
        o_hl = sb("d_o_hl", [P, 2, 2, CW * NCH], F16)
        ps_d = [ctx.enter_context(nc.psum_tensor(f"ps_d{i}", [P, 2, 512], F32)) for i in range(2)]
        levels = sem("d_levels")
        o_high = sem("d_high")
        o_low = sem("d_low")
        products = sem("d_products")
        added = sem("d_added")
        stored = [sem(f"d_stored{i}") for i in range(NB)]
        scale_on_pool, scale_on_dve = product_scale(nc, ctx, c, acc_product, "s_p", "s_up", 1.0, "s_y", "k_o", SC_W)
        block = ctx.enter_context(nc.Block())
        big = t["big"]
        out_v = out.rearrange("n p f -> p n f")

        def rounds(eng, group):
            for g in range(NB):
                group(g, g, 0)
            with eng.Fori(1, NG // NB) as r:
                for b in range(NB):
                    group(r * NB + b, b, r)

        @block.sync
        def _(sp):
            def store(g, b):
                sp.wait_ge(added, g + 1)
                sp.dma_start(out_v[:, bass.ts(g, GS), :], y[:, b, :].rearrange("p (s f) -> p s f", f=DM)).then_inc(stored[b], 16)
            with sp.Fori(0, NG // NB - 1) as r:
                for b in range(NB):
                    store(r * NB + b, b)
                    load(sp, r * NB + NB + b, b)
            for b in range(NB):
                store(NG - NB + b, b)
            for s in stored:
                sp.wait_ge(s, 16 * NG // NB)

        @block.gpsimd
        def _(pool):
            scale_on_pool(pool)

        @block.vector
        def _(dve):
            scale_on_dve(dve)

            def finish(g, b, r):
                dve.wait_ge(products, g + 1)
                wait(dve, stored[b], r * 16)
                dve.scalar_tensor_tensor(y[:, b, :], ps_d[b % 2][:, :, :].rearrange("p b n -> p (b n)"), c["s_y"],
                                         res[:, b, :], ALU.mult, ALU.add).then_inc(added, 1)

            def quantise(g, b, r):
                dve.wait_ge(loaded[b], r * 32 + 32)
                wait(dve, o_low, g * NCH)
                for ch in range(NCH):
                    dve.scalar_tensor_tensor(qo[:, ch, :], big[:, bass.ts(g * NCH + ch, CW)], c["k_o"],
                                             qu[:, b, ch * CW:(ch + 1) * CW], ALU.mult, ALU.mult).then_inc(levels, 1)

            def split(g, b):
                for ch in range(NCH):
                    cols = slice(ch * CW, (ch + 1) * CW)
                    dve.wait_ge(o_high, g * NCH + ch + 1)
                    dve.tensor_tensor(o_hl[:, b % 2, 1, cols], qo[:, ch, :], o_hl[:, b % 2, 0, cols], ALU.subtract).then_inc(o_low, 1)

            def group(g, b, r):
                quantise(g, b, r)
                split(g, b)
                if not (isinstance(g, int) and g == 0):
                    finish(g - 1, (b - 1) % NB, r if b else r - 1)

            for g in range(NB + 1):
                group(g, g % NB, g // NB)
            with dve.Fori(1, NG // NB - 1) as r:
                for b in range(1, NB + 1):
                    group(r * NB + b, b % NB, r if b < NB else r + 1)
            for g in range(NG - NB + 1, NG):
                group(g, g % NB, g // NB)
            finish(NG - 1, NB - 1, NG // NB - 1)

        @block.scalar
        def _(act):
            def group(g, b, r):
                wait(act, products, g - 1)
                for ch in range(NCH):
                    act.wait_ge(levels, g * NCH + ch + 1)
                    act.copy(o_hl[:, b % 2, 0, ch * CW:(ch + 1) * CW], qo[:, ch, :]).then_inc(o_high, 1)
            rounds(act, group)

        @block.tensor
        def _(pe):
            def group(g, b, r):
                pe.wait_ge(o_low, g * NCH + NCH)
                wait(pe, added, g - 1)
                terms = [(k, xh, wh) for k in range(FT) for xh, wh in ((0, 0), (1, 0), (0, 1))]
                for s in range(GS):
                    for i, (k, xh, wh) in enumerate(terms):
                        last = pe.matmul(ps_d[b % 2][:, s // 2, s % 2 * DM:(s % 2 + 1) * DM],
                                         o_hl[:, b % 2, xh, k * GT + s * P:k * GT + (s + 1) * P], t["wdown"][:, wh, k, :],
                                         start=i == 0, stop=i == len(terms) - 1)
                last.then_inc(products, 1)
            rounds(pe, group)


_INS = ["x", "L0_tok_emb_weight", "L0_tok_proj_weight", "L0_tok_scale", "L0_attn_W_qk", "L0_attn_W_v",
        "L0_attn_W_out", "L0_attn_b_out", "L0_attn_conv", "L0_ffn_w_gate", "L0_ffn_w_up", "L0_ffn_w_down"]


def kernel(**inputs):
    import numpy as _np
    import concourse.bacc as _bacc
    from concourse import mybir as _mybir
    from concourse.bass_utils import run_bass_kernel_spmd as _run

    nc = _bacc.Bacc("TRN2", target_bir_lowering=False, num_devices=1)
    arrays, args = {}, []
    for name in _INS:
        v = _np.ascontiguousarray(inputs[name])
        if v.ndim == 0:
            v = v.reshape(1)
        arrays[f"in_{name}"] = v
        args.append(nc.dram_tensor(f"in_{name}", v.shape, _mybir.dt.from_np(v.dtype), kind="ExternalInput").ap())
    out = nc.dram_tensor("out_h", (NSEQ, P, DM), F32, kind="ExternalOutput").ap()
    build(nc, *args, out)
    r = _run(nc, [arrays], core_ids=[0])
    return r.results[0]["out_h"]
```
